# Optimizing a Trainium2 kernel written in Bass

```python
import numpy as np
import jax
import jax.numpy as jnp

def _softmax(x, axis=-1):
    return jax.nn.softmax(x, axis=axis)

def _gelu(x):
    return jax.nn.gelu(x, approximate=True)

def _silu(x):
    return jax.nn.silu(x)

def _sigmoid(x):
    return jax.nn.sigmoid(x)

def _layernorm(x, axis=-1, eps=1e-05):
    m = jnp.mean(x, axis=axis, keepdims=True)
    v = jnp.var(x, axis=axis, keepdims=True)
    return (x - m) / jnp.sqrt(v + eps)

def _scatter_add(tgt, idx, src, axis=0):
    return tgt.at[idx].add(src)

def _segment_sum(src, seg, n):
    return jax.ops.segment_sum(src, seg, n)
kernel_name = 'mk_decoder_preln_d1_seqx_r4_a8ff14'

def setup_inputs(seed: int=0):
    np.random.seed(seed)
    _w = jnp.asarray

    def _rec_inputs():
        import jax
        import jax.numpy as jnp
        _rk = jax.random.key(seed)
        x = -0.0002928 + 1 * jax.random.normal(jax.random.fold_in(_rk, 1), (8, 512, 256), jnp.float32)
        _lenS = 512 - jax.random.randint(jax.random.fold_in(_rk, 7), (8,), 0, max(1, 512 // 4) + 1, jnp.int32)
        _lenS2 = 512 - jax.random.randint(jax.random.fold_in(_rk, 8), (8,), 0, max(1, 512 // 4) + 1, jnp.int32)
        _ctx_1024P = jax.random.normal(jax.random.fold_in(_rk, 11), (8, 16, 256), jnp.float32)
        _ctx_1024c = jax.random.dirichlet(jax.random.fold_in(_rk, 511), 0.3 * jnp.ones((16,), jnp.float32), (8, 512))
        _ctx_1024t = jnp.einsum('bsk,bkd->bsd', _ctx_1024c, _ctx_1024P)
        _ctx_1024t = _ctx_1024t * jax.lax.rsqrt(jnp.mean(jnp.square(_ctx_1024t)) + 1e-12) * 0.953939
        ctx_1024 = -1.39393e-06 + 0.999914 * (_ctx_1024t + 0.3 * jax.random.normal(jax.random.fold_in(_rk, 611), (8, 512, 256), jnp.float32))
        return (x, ctx_1024)
    x, ctx_1024 = _rec_inputs()

    def _L0_attn_setup():
        import math
        import jax, jax.numpy as jnp
        import numpy as np
        EPS_SUM = 1e-07
        EPS_NORM = 1e-12

        def _l2norm(x, axis):
            n = jnp.sqrt(jnp.sum(x * x, axis=axis, keepdims=True))
            return x / jnp.maximum(n, EPS_NORM)
        key = jax.random.key(seed)
        ks = jax.random.split(key, 5)
        b, N, C = (4, 1024, 256)
        x = jax.random.normal(ks[0], (b, N, C), dtype=jnp.float32)
        Wqkv = jax.random.normal(ks[1], (C, 3 * C), dtype=jnp.float32) / math.sqrt(C)
        bqkv = jax.random.normal(ks[2], (3 * C,), dtype=jnp.float32) * 0.01
        Wln = jax.random.normal(ks[3], (C, C), dtype=jnp.float32) / math.sqrt(C)
        bln = jax.random.normal(ks[4], (C,), dtype=jnp.float32) * 0.01
        return {'x': x, 'Wqkv': Wqkv, 'bqkv': bqkv, 'Wln': Wln, 'bln': bln}
    _L0_attn_all = _L0_attn_setup()
    _L0_attn_in = {k: v for k, v in _L0_attn_all.items() if k in ('Wqkv', 'bqkv', 'Wln', 'bln')}
    del _L0_attn_all

    def _L0_xattn_setup():
        import jax, jax.numpy as jnp
        import numpy as np
        B, S, D = (2, 512, 256)
        H, HD = (16, 64)
        key = jax.random.key(seed)
        ks = jax.random.split(key, 8)
        scale = 1.0 / np.sqrt(D)
        return {'q': jax.random.normal(ks[0], (B, S, D), jnp.float32), 'k': jax.random.normal(ks[1], (B, S, D), jnp.float32), 'v': jax.random.normal(ks[2], (B, S, D), jnp.float32), 'Wq': jax.random.normal(ks[3], (H * HD, D), jnp.float32) * scale, 'bq': jnp.zeros((H * HD,), jnp.float32), 'Wk': jax.random.normal(ks[4], (H * HD, D), jnp.float32) * scale, 'bk': jnp.zeros((H * HD,), jnp.float32), 'Wv': jax.random.normal(ks[5], (H * HD, D), jnp.float32) * scale, 'bv': jnp.zeros((H * HD,), jnp.float32), 'Wo': jax.random.normal(ks[6], (D, H * HD), jnp.float32) * scale, 'bo': jnp.zeros((D,), jnp.float32)}
    _L0_xattn_all = _L0_xattn_setup()
    _L0_xattn_in = {k: v for k, v in _L0_xattn_all.items() if k in ('Wq', 'bq', 'Wk', 'bk', 'Wv', 'bv', 'Wo', 'bo')}
    del _L0_xattn_all

    def _L0_ffn_setup():
        import jax, jax.numpy as jnp
        import numpy as np
        E = 16
        K = 4
        B, S, H, I = (4, 256, 256, 512)
        key = jax.random.key(seed)
        k0, k1, k2, k3 = jax.random.split(key, 4)
        scale = 0.02
        return {'hidden_states': jax.random.normal(k0, (B, S, H), jnp.float32), 'router_w': jax.random.normal(k1, (H, E), jnp.float32) * scale, 'router_b': jnp.zeros((E,), jnp.float32), 'w1': jax.random.normal(k2, (E, H, I), jnp.float32) * scale, 'b1': jnp.zeros((E, I), jnp.float32), 'w2': jax.random.normal(k3, (E, I, H), jnp.float32) * scale, 'b2': jnp.zeros((E, H), jnp.float32)}
    _L0_ffn_all = _L0_ffn_setup()
    _L0_ffn_in = {k: v for k, v in _L0_ffn_all.items() if k in ('router_w', 'router_b', 'w1', 'b1', 'w2', 'b2')}
    del _L0_ffn_all
    return {'x': x, 'ctx_1024': ctx_1024, 'L0_attn_Wqkv': _L0_attn_in['Wqkv'], 'L0_attn_bqkv': _L0_attn_in['bqkv'], 'L0_attn_Wln': _L0_attn_in['Wln'], 'L0_attn_bln': _L0_attn_in['bln'], 'L0_xattn_Wq': _L0_xattn_in['Wq'], 'L0_xattn_bq': _L0_xattn_in['bq'], 'L0_xattn_Wk': _L0_xattn_in['Wk'], 'L0_xattn_bk': _L0_xattn_in['bk'], 'L0_xattn_Wv': _L0_xattn_in['Wv'], 'L0_xattn_bv': _L0_xattn_in['bv'], 'L0_xattn_Wo': _L0_xattn_in['Wo'], 'L0_xattn_bo': _L0_xattn_in['bo'], 'L0_ffn_router_w': _L0_ffn_in['router_w'], 'L0_ffn_router_b': _L0_ffn_in['router_b'], 'L0_ffn_w1': _L0_ffn_in['w1'], 'L0_ffn_b1': _L0_ffn_in['b1'], 'L0_ffn_w2': _L0_ffn_in['w2'], 'L0_ffn_b2': _L0_ffn_in['b2']}

def reference(x, ctx_1024, L0_attn_Wqkv, L0_attn_bqkv, L0_attn_Wln, L0_attn_bln, L0_xattn_Wq, L0_xattn_bq, L0_xattn_Wk, L0_xattn_bk, L0_xattn_Wv, L0_xattn_bv, L0_xattn_Wo, L0_xattn_bo, L0_ffn_router_w, L0_ffn_router_b, L0_ffn_w1, L0_ffn_b1, L0_ffn_w2, L0_ffn_b2):
    import jax
    import jax.numpy as jnp

    def _L0_attn_ref(x, Wqkv, bqkv, Wln, bln):
        import math
        import jax, jax.numpy as jnp
        import numpy as np
        EPS_SUM = 1e-07
        EPS_NORM = 1e-12

        def _l2norm(x, axis):
            n = jnp.sqrt(jnp.sum(x * x, axis=axis, keepdims=True))
            return x / jnp.maximum(n, EPS_NORM)
        b, N, C = x.shape
        qkv = x @ Wqkv + bqkv
        q, k, v = jnp.split(qkv, 3, axis=2)
        q = q - q.mean(axis=2, keepdims=True)
        k = k - k.mean(axis=2, keepdims=True)
        q2 = q * q
        k2 = k * k
        q2 = q2 / (q2.sum(axis=2, keepdims=True) + EPS_SUM)
        q2 = _l2norm(q2, axis=-1)
        k2 = k2 / (k2.sum(axis=2, keepdims=True) + EPS_SUM)
        k2 = _l2norm(k2, axis=-2)
        kv = jnp.einsum('bnc,bnd->bcd', k2, v)
        t2 = jnp.einsum('bnc,bcd->bnd', q2, kv) / math.sqrt(N)
        return (v + t2) @ Wln + bln

    def _L0_xattn_ref(q, k, v, Wq, bq, Wk, bk, Wv, bv, Wo, bo):
        import jax, jax.numpy as jnp
        import numpy as np
        B, S, D = (2, 512, 256)
        H, HD = (16, 64)
        b, s, _ = q.shape
        qh = (q @ Wq.T + bq).reshape(b, s, H, HD).transpose(0, 2, 1, 3)
        kh = (k @ Wk.T + bk).reshape(b, s, H, HD).transpose(0, 2, 1, 3)
        vh = (v @ Wv.T + bv).reshape(b, s, H, HD).transpose(0, 2, 1, 3)
        scores = jnp.einsum('bhqd,bhkd->bhqk', qh, kh) / np.sqrt(HD).astype(np.float32)
        causal = jnp.tril(jnp.ones((s, s), bool))
        scores = jnp.where(causal, scores, -jnp.inf)
        attn = jax.nn.softmax(scores, axis=-1)
        out = jnp.einsum('bhqk,bhkd->bhqd', attn, vh)
        out = out.transpose(0, 2, 1, 3).reshape(b, s, H * HD)
        return out @ Wo.T + bo

    def _L0_ffn_ref(hidden_states, router_w, router_b, w1, b1, w2, b2):
        import jax, jax.numpy as jnp
        import numpy as np
        E = 16
        K = 4
        B, S, H, I = (4, 256, 256, 512)
        b, s, h = hidden_states.shape
        logits = hidden_states @ router_w + router_b
        probs = jax.nn.softmax(logits, axis=-1)
        topw, topi = jax.lax.top_k(probs, K)
        topw = topw / jnp.sum(topw, axis=-1, keepdims=True)
        combine = jnp.sum(jax.nn.one_hot(topi, E, dtype=hidden_states.dtype) * topw[..., None], axis=2)
        x = hidden_states.reshape(b * s, h)
        c = combine.reshape(b * s, E)

        def body(acc, expert):
            w1e, b1e, w2e, b2e, ce = expert
            hmid = jax.nn.gelu(x @ w1e + b1e, approximate=False)
            return (acc + (hmid @ w2e + b2e) * ce[:, None], None)
        out, _ = jax.lax.scan(body, jnp.zeros_like(x), (w1, b1, w2, b2, c.T))
        return out.reshape(b, s, h)
    x = x + _L0_attn_ref(_layernorm(x, axis=-1), L0_attn_Wqkv, L0_attn_bqkv, L0_attn_Wln, L0_attn_bln)
    x = x + _L0_xattn_ref(_layernorm(x, axis=-1), ctx_1024, ctx_1024, L0_xattn_Wq, L0_xattn_bq, L0_xattn_Wk, L0_xattn_bk, L0_xattn_Wv, L0_xattn_bv, L0_xattn_Wo, L0_xattn_bo)
    x = x + _L0_ffn_ref(_layernorm(x, axis=-1), L0_ffn_router_w, L0_ffn_router_b, L0_ffn_w1, L0_ffn_b1, L0_ffn_w2, L0_ffn_b2)
    return x

_drawn_inputs = setup_inputs


def setup_inputs(seed=0):
    import zlib

    import numpy as np

    out = dict(_drawn_inputs(seed))
    spreads = {'L0_xattn_bq': (0.0, 0.282),
     'L0_xattn_bk': (0.0, 0.8),
     'L0_xattn_bv': (0.0, 0.1),
     'L0_xattn_bo': (0.0, 0.1),
     'L0_ffn_router_b': (0.0, 0.463),
     'L0_ffn_b1': (0.0, 0.8),
     'L0_ffn_b2': (0.0, 0.286)}
    factors = {'L0_attn_bln': 8.0, 'L0_ffn_w1': 2.675}
    for name, (base, spread) in spreads.items():
        noise = np.random.default_rng([zlib.crc32(name.encode()), seed]).standard_normal(out[name].shape)
        drawn = base * np.exp(spread * noise) if base else spread * noise
        out[name] = jnp.asarray(drawn.astype(out[name].dtype))
    for name, factor in factors.items():
        out[name] = (out[name] * factor).astype(out[name].dtype)
    return out
```

```python
from contextlib import ExitStack

import numpy as np

import concourse.bass as bass
from concourse import mybir

F32 = mybir.dt.float32
F32R = mybir.dt.float32r
BF16 = mybir.dt.bfloat16
I32 = mybir.dt.int32
ACT = mybir.ActivationFunctionType
ALU = mybir.AluOpType
AX = mybir.AxisListType

P = 128
B, S, D = 8, 512, 256
N_TILES = S // P
KC = D // P
H, HD = 16, 64
INNER = H * HD
PAIRS = H // 2
E, TOPK, FF = 16, 4, 512
FC = FF // P
TOKENS = B * S
ALL_TILES = TOKENS // P
ROWS = 256
RT = ROWS // P
REGION = TOKENS + ROWS
MOE_TILES = (TOKENS * TOPK + E * (ROWS - 1)) // ROWS
LN_EPS, EPS_SUM, EPS_NORM = 1e-5, 1e-7, 1e-12
NEG = -1e30


class Counter:

    def __init__(self, sem, step=1):
        self.sem, self.step, self.value = sem, step, 0

    def next(self):
        self.value += self.step
        return (self, self.value)


class Queue:

    def __init__(self):
        self.steps = []

    def do(self, make, after=(), counts=None):
        self.steps.append((make, [a for a in after if a is not None], counts))
        return counts.next() if counts is not None else None

    def play(self, engine):
        waited = {}
        for make, after, counts in self.steps:
            for sig, value in after:
                if waited.get(sig, 0) < value:
                    engine.wait_ge(sig.sem, value)
                    waited[sig] = value
            instruction = make(engine)
            if counts is not None:
                instruction.then_inc(counts.sem, counts.step)


class Part:

    def __init__(self, nc, stack, name):
        self.nc, self.stack, self.name = nc, stack, name
        self.pe, self.act, self.dve, self.pool, self.sp = (Queue() for _ in range(5))

    def sb(self, name, shape, dtype=F32):
        return self.stack.enter_context(self.nc.sbuf_tensor(f"{self.name}_{name}", shape, dtype))

    def bank(self, name):
        return self.stack.enter_context(self.nc.psum_tensor(f"{self.name}_{name}", [P, 512], F32))

    def counter(self, name, step=1):
        return Counter(self.stack.enter_context(self.nc.semaphore(f"{self.name}_{name}")), step)

    def dma_counter(self, name):
        return self.counter(name, 16)

    def run(self):
        with self.nc.Block() as block:
            for register, queue in ((block.tensor, self.pe), (block.scalar, self.act), (block.vector, self.dve),
                                    (block.gpsimd, self.pool), (block.sync, self.sp)):
                register(queue.play)


def split3(a, b):
    (ah, al), (bh, bl) = a, b
    return ((al, bh), (ah, bl), (ah, bh))


def f32(ap):
    return ap.bitcast(F32)


def constants(part):
    done = part.counter("const")
    ident = part.sb("ident", [P, P])
    e0 = part.pool.do(lambda e: e.memset(ident[:], 0.0), counts=done)
    e1 = part.pool.do(lambda e: e.affine_select(out=ident[:], in_=ident[:], compare_op=ALU.not_equal, fill=1.0,
                                                base=0, pattern=[[-1, P]], channel_multiplier=1),
                      after=[e0], counts=done)
    return ident, e1, done


def load_split(part, name, dram, shape, stage, scale=None):
    hi, lo = part.sb(name + "_hi", shape, F32R), part.sb(name + "_lo", shape, F32R)
    dims = "p a b -> p (a b)"
    size = shape[1] * shape[2]
    view = stage["tile"][:, 0:size]
    got = part.sp.do(lambda e: e.dma_start(view.rearrange("p (a b) -> p a b", a=shape[1]), dram),
                     after=stage["free"], counts=stage["dma"])
    h2, l2 = hi[:].rearrange(dims), lo[:].rearrange(dims)
    if scale is not None:
        got = part.dve.do(lambda e: e.tensor_scalar(view, view, scale, None, ALU.mult), after=[got],
                          counts=stage["split"])
    a = part.act.do(lambda e: e.activation(h2, view, ACT.Copy), after=[got], counts=stage["hi"])
    d = part.dve.do(lambda e: e.tensor_tensor(l2, view, f32(h2), op=ALU.subtract), after=[got, a],
                    counts=stage["split"])
    stage["free"] = [d]
    return (hi, lo), d


class Norm:

    def __init__(self, part, name):
        self.part = part
        self.stats = part.sb(name + "_stats", [P, N_TILES, 6])
        self.mv = part.sb(name + "_mv", [P, N_TILES, 2])
        self.rstd = part.sb(name + "_rstd", [P, N_TILES])
        self.power = part.sb(name + "_power", [P, N_TILES])
        self.dve, self.pool = part.counter(name + "_dve"), part.counter(name + "_pool")
        self.power_set = part.pool.do(lambda e: e.memset(self.power[:], -0.5), counts=self.pool)
        self.last = []

    def run(self, x, out, ready, out_free):
        p, mv, stats, rstd = self.part, self.mv, self.stats, self.rstd
        for t in range(N_TILES):
            s = p.dve.do(lambda e, t=t: e.bn_stats(stats[:, t, :], x[:, t, :]), after=ready + self.last,
                         counts=self.dve)
        for t in range(N_TILES):
            a = p.dve.do(lambda e, t=t: e.bn_aggr(mv[:, t, :], stats[:, t, :]), after=[s], counts=self.dve)
        v = p.dve.do(lambda e: e.tensor_scalar(rstd[:], mv[:, :, 1], LN_EPS, None, ALU.add), after=[a],
                     counts=self.dve)
        r = p.pool.do(lambda e: e.tensor_tensor(rstd[:], rstd[:], self.power[:], op=ALU.pow),
                      after=[v, self.power_set], counts=self.pool)
        for t in range(N_TILES):
            d = p.dve.do(lambda e, t=t: e.tensor_scalar(out[:, t, :], x[:, t, :], mv[:, t, 0:1], rstd[:, t:t + 1],
                                                        ALU.subtract, ALU.mult),
                         after=[r] + out_free, counts=self.dve)
        self.last = [d]
        return d


def first_attention(nc, d, x1_dram):
    with ExitStack() as stack:
        p = Part(nc, stack, "a1")
        pe, act, dve, pool, sp = p.pe, p.act, p.dve, p.pool, p.sp
        ident, const_ready, _ = constants(p)
        stage = {"tile": p.sb("stage", [P, KC * 768]), "dma": p.dma_counter("w_in"), "hi": p.counter("w_hi"),
                 "split": p.counter("w_split"), "free": []}
        x_loaded = [p.dma_counter(f"x_loaded{i}") for i in range(2)]
        x_in = [p.sb(f"x{i}", [P, N_TILES, D]) for i in range(2)]

        def load_x(b, free):
            return sp.do(lambda e: e.dma_start(x_in[b % 2][:], d['x'][b].rearrange("(t p) c -> p t c", p=P)),
                         after=free, counts=x_loaded[b % 2])

        loaded = {0: load_x(0, [])}
        Wqkv, wqkv_ready = load_split(p, "wqkv", d['Wqkv'].rearrange("(k p) n -> p k n", p=P), [P, KC, 768], stage)
        Wln, wln_ready = load_split(p, "wln", d['Wln'].rearrange("(k p) n -> p k n", p=P), [P, KC, D], stage)
        bias_in = p.dma_counter("bias_in")
        bqkv = p.sb("bqkv", [P, 768])
        bvT = p.sb("bvT", [P, KC])
        bln = p.sb("bln", [P, D])
        sp.do(lambda e: e.dma_start(bqkv[:], d['bqkv'].rearrange("(a n) -> a n", a=1).broadcast_to([P, 768])),
              counts=bias_in)
        sp.do(lambda e: e.dma_start(bvT[:], d['bqkv'][512:768].rearrange("(k p) -> p k", p=P),
                                    allow_slow_non_contiguous=True), counts=bias_in)
        bias_ready = sp.do(lambda e: e.dma_start(bln[:], d['bln'].rearrange("(a n) -> a n", a=1)
                                                 .broadcast_to([P, D])), counts=bias_in)
        norm = Norm(p, "ln")
        xn = p.sb("xn", [P, N_TILES, D])
        xT = tuple(p.sb(f"xT{i}", [P, KC, S], F32R) for i in range(2))
        qk = p.sb("qk", [P, N_TILES, 512])
        v32 = p.sb("v32", [P, N_TILES, D])
        v = tuple(p.sb(f"v{i}", [P, N_TILES, D], F32R) for i in range(2))
        qk_stats = p.sb("qk_stats", [P, N_TILES * 2, 6])
        qk_mv = p.sb("qk_mv", [P, N_TILES * 2, 2])
        neg_mean = p.sb("neg_mean", [P, N_TILES * 2])
        sq = p.sb("sq", [P, N_TILES, 512])
        sq4 = p.sb("sq4", [P, D])
        s2 = p.sb("s2", [P, N_TILES * 2])
        s4 = p.sb("s4", [P, N_TILES])
        qf = p.sb("qf", [P, N_TILES])
        half = p.sb("half", [P, N_TILES])
        q2n = p.sb("q2n", [P, N_TILES, D])
        q2T = tuple(p.sb(f"q2T{i}", [P, KC, S], F32R) for i in range(2))
        k2 = p.sb("k2", [P, N_TILES, D])
        k2s = tuple(p.sb(f"k2s{i}", [P, N_TILES, D], F32R) for i in range(2))
        k4 = p.sb("k4", [P, N_TILES, D])
        ones = p.sb("ones", [P, 2])
        knorm = p.sb("knorm", [P, KC])
        kv32 = p.sb("kv32", [P, KC, D])
        kv = tuple(p.sb(f"kv{i}", [P, KC, D], F32R) for i in range(2))
        yT = tuple(p.sb(f"yT{i}", [P, KC, S], F32R) for i in range(2))
        xb = p.sb("xb", [P, N_TILES, D])
        x1 = [p.sb(f"x1_{i}", [P, N_TILES, D]) for i in range(2)]
        T = [p.bank(f"T{i}") for i in range(2)]
        QK = [p.bank(f"QK{i}") for i in range(2)]
        V, KV, NB, Y = p.bank("V"), p.bank("KV"), p.bank("NB"), p.bank("Y")
        free = {k: [] for k in ("T0", "T1", "QK0", "QK1", "V", "KV", "NB", "Y")}

        g = {n: p.counter(n) for n in ("xT_pe", "xT_hi", "xT_lo", "qkv_pe", "qk_ev", "v_ev", "v_hi", "v_lo", "st",
                                      "sqr", "small", "small_pool", "q2n", "q2T_pe", "q2T_hi", "q2T_lo", "k2",
                                      "k2_hi", "k2_lo", "k4", "kv_pe", "kn_pool", "kn", "kv_ev", "kv_hi", "kv_lo",
                                      "yT_pe", "yT_hi", "yT_lo", "y_pe", "xb", "x1")}
        stored = [p.dma_counter(f"x1_stored{i}") for i in range(2)]
        c0 = pool.do(lambda e: e.memset(ones[:], 1.0), counts=g["small_pool"])
        c1 = pool.do(lambda e: e.memset(half[:], 0.5), counts=g["small_pool"])
        last_store = {}
        prev = {}

        for b in range(B):
            xi = x_in[b % 2]
            if b + 1 < B:
                loaded[b + 1] = load_x(b + 1, prev.get("xb_all", []))
            n = norm.run(xi, xn, [loaded[b]], prev.get("xn_read", []))
            e_xb = pool.do(lambda e, xi=xi: e.tensor_tensor(
                xb[:], xi[:], bln[:].rearrange("p (a c) -> p a c", a=1).broadcast_to([P, N_TILES, D]), op=ALU.add),
                after=[loaded[b], bias_ready] + prev.get("x1", []), counts=g["xb"])

            def transposed(src, dst, names, src_ready, dst_free):
                out = []
                for c in range(KC):
                    for t in range(N_TILES):
                        tp = pe.do(lambda e, c=c, t=t: e.transpose(T[c][:, t * P:(t + 1) * P],
                                                                   src[:, t, c * P:(c + 1) * P], ident[:]),
                                   after=[src_ready, const_ready] + free[f"T{c}"], counts=g[names + "_pe"])
                    hi = act.do(lambda e, c=c: e.activation(dst[0][:, c, :], T[c][:], ACT.Copy),
                                after=[tp] + dst_free, counts=g[names + "_hi"])
                    lo = dve.do(lambda e, c=c: e.tensor_tensor(dst[1][:, c, :], T[c][:], f32(dst[0][:, c, :]),
                                                               op=ALU.subtract),
                                after=[tp, hi] + dst_free, counts=g[names + "_lo"])
                    free[f"T{c}"] = [lo]
                    out = [hi, lo]
                return tp, out

            tp, xT_ready = transposed(xn, xT, "xT", n, prev.get("xT_read", []))
            prev["xn_read"] = [tp]

            st_last = []
            for t in range(N_TILES):
                bank = QK[t % 2]
                for c in range(KC):
                    for i, (a, w) in enumerate(split3(xT, Wqkv)):
                        m = pe.do(lambda e, t=t, c=c, i=i, a=a, w=w, bank=bank: e.matmul(
                            bank[:], a[:, c, t * P:(t + 1) * P], w[:, c, 0:512],
                            start=(c == 0 and i == 0), stop=(c == KC - 1 and i == 2)),
                            after=xT_ready + [wqkv_ready] + free[f"QK{t % 2}"], counts=g["qkv_pe"])
                ev = dve.do(lambda e, t=t, bank=bank: e.tensor_tensor(qk[:, t, :], bank[:], bqkv[:, 0:512], op=ALU.add),
                            after=[m, bias_ready] + prev.get("qk_read", []), counts=g["qk_ev"])
                free[f"QK{t % 2}"] = [ev]
                for c in range(KC):
                    for i, (a, w) in enumerate(split3(xT, Wqkv)):
                        mv_ = pe.do(lambda e, t=t, c=c, i=i, a=a, w=w: e.matmul(
                            V[:, (t % 2) * D:(t % 2 + 1) * D], a[:, c, t * P:(t + 1) * P], w[:, c, 512:768],
                            start=(c == 0 and i == 0), stop=(c == KC - 1 and i == 2)),
                            after=(free["V"] if t % 2 == 0 else []), counts=g["qkv_pe"])
                if t % 2 == 1:
                    ve = dve.do(lambda e, t=t: e.tensor_tensor(
                        v32[:, t - 1:t + 1, :], V[:].rearrange("p (a c) -> p a c", a=2),
                        bqkv[:, 512:768].rearrange("p (a c) -> p a c", a=1).broadcast_to([P, 2, D]), op=ALU.add),
                        after=[mv_] + prev.get("v32_read", []), counts=g["v_ev"])
                    free["V"] = [ve]
                for j in range(2):
                    st = dve.do(lambda e, t=t, j=j: e.bn_stats(qk_stats[:, 2 * t + j, :], qk[:, t, j * D:(j + 1) * D]),
                                after=[ev] + prev.get("stats_read", []), counts=g["st"])
            vh = act.do(lambda e: e.activation(v[0][:], v32[:], ACT.Copy), after=[ve] + prev.get("v_read", []),
                        counts=g["v_hi"])
            vl = pool.do(lambda e: e.tensor_tensor(v[1][:], v32[:], f32(v[0][:]), op=ALU.subtract),
                         after=[vh, ve] + prev.get("v_read", []), counts=g["v_lo"])
            prev["v32_read"] = [vl]
            for j in range(2 * N_TILES):
                ag = dve.do(lambda e, j=j: e.bn_aggr(qk_mv[:, j, :], qk_stats[:, j, :]),
                            after=[st] + prev.get("mv_read", []), counts=g["st"])
            nm = dve.do(lambda e: e.tensor_scalar(neg_mean[:], qk_mv[:, :, 0], -1.0, None, ALU.mult),
                        after=[ag] + prev.get("sq_done", []), counts=g["st"])
            prev["stats_read"] = [ag]
            s2a = dve.do(lambda e: e.tensor_scalar(s2[:], qk_mv[:, :, 1], float(D), EPS_SUM, ALU.mult, ALU.add),
                         after=[ag] + prev.get("s2_read", []), counts=g["small"])
            s2b = dve.do(lambda e: e.reciprocal(s2[:], s2[:]), after=[s2a], counts=g["small"])
            prev["mv_read"] = [s2a, nm]
            sq_last = []
            for t in range(N_TILES):
                for j in range(2):
                    a1 = act.do(lambda e, t=t, j=j: e.activation(
                        sq[:, t, j * D:(j + 1) * D], qk[:, t, j * D:(j + 1) * D], ACT.Square,
                        bias=neg_mean[:, 2 * t + j:2 * t + j + 1]),
                        after=[nm, ev] + prev.get("sq_read", []), counts=g["sqr"])
                    if j == 0:
                        a2 = act.do(lambda e, t=t: e.activation(sq4[:], sq[:, t, 0:D], ACT.Square,
                                                                accum_out=s4[:, t:t + 1]),
                                    after=[a1] + prev.get("s4_read", []) + ([a2] if t else prev.get("sq4", [])),
                                    counts=g["sqr"])
            prev["qk_read"] = prev["sq_done"] = [a1]
            prev["sq4"] = [a2]
            aq = s2[:].rearrange("p (t j) -> p t j", j=2)[:, :, 0]
            r = pool.do(lambda e: e.tensor_tensor(s4[:], s4[:], half[:], op=ALU.pow), after=[a1, a2, c1],
                        counts=g["small_pool"])
            f1 = dve.do(lambda e: e.tensor_tensor(s4[:], s4[:], aq, op=ALU.mult), after=[r, s2b], counts=g["small"])
            f2 = dve.do(lambda e: e.tensor_scalar(s4[:], s4[:], EPS_NORM, float(S) ** 0.5, ALU.max, ALU.mult),
                        after=[f1], counts=g["small"])
            f3 = dve.do(lambda e: e.reciprocal(s4[:], s4[:]), after=[f2], counts=g["small"])
            f4 = dve.do(lambda e: e.tensor_tensor(qf[:], s4[:], aq, op=ALU.mult), after=[f3] + prev.get("qf_read", []),
                        counts=g["small"])
            prev["s4_read"] = [f4]
            for t in range(N_TILES):
                qn = dve.do(lambda e, t=t: e.tensor_scalar(q2n[:, t, :], sq[:, t, 0:D], qf[:, t:t + 1], None, ALU.mult),
                            after=[f4, a1] + prev.get("q2n_read", []), counts=g["q2n"])
                kn_ = dve.do(lambda e, t=t: e.tensor_scalar(k2[:, t, :], sq[:, t, D:512], s2[:, 2 * t + 1:2 * t + 2],
                                                            None, ALU.mult),
                             after=[s2b, a1] + prev.get("k2_read", []), counts=g["k2"])
            prev["sq_read"] = [qn, kn_]
            prev["s2_read"] = [kn_, f4]
            prev["qf_read"] = [qn]
            k4e = pool.do(lambda e: e.tensor_tensor(k4[:], k2[:], k2[:], op=ALU.mult),
                          after=[kn_] + prev.get("k4_read", []), counts=g["k4"])
            kh = act.do(lambda e: e.activation(k2s[0][:], k2[:], ACT.Copy), after=[kn_] + prev.get("k2s_read", []),
                        counts=g["k2_hi"])
            kl = dve.do(lambda e: e.tensor_tensor(k2s[1][:], k2[:], f32(k2s[0][:]), op=ALU.subtract),
                        after=[kh, kn_] + prev.get("k2s_read", []), counts=g["k2_lo"])
            prev["k2_read"] = [kl, k4e]

            tp, q2T_ready = transposed(q2n, q2T, "q2T", qn, prev.get("q2T_read", []))
            prev["q2n_read"] = [tp]

            for c in range(KC):
                for t in range(N_TILES):
                    for i, (a, w) in enumerate(split3(k2s, v)):
                        m = pe.do(lambda e, t=t, c=c, i=i, a=a, w=w: e.matmul(
                            KV[:, c * D:(c + 1) * D], a[:, t, c * P:(c + 1) * P], w[:, t, :],
                            start=(t == 0 and i == 0), stop=(t == N_TILES - 1 and i == 2)),
                            after=[kl, kh, vh, vl] + free["KV"], counts=g["kv_pe"])
            prev["k2s_read"] = prev["v_read"] = [m]
            for c in range(KC):
                for t in range(N_TILES):
                    mn = pe.do(lambda e, t=t, c=c: e.matmul(NB[:, 2 * c:2 * c + 2], k4[:, t, c * P:(c + 1) * P],
                                                            ones[:], start=(t == 0), stop=(t == N_TILES - 1)),
                               after=[k4e, c0] + free["NB"], counts=g["kv_pe"])
            prev["k4_read"] = [mn]
            nb = NB[:, 0:4].rearrange("p (c j) -> p c j", j=2)[:, :, 0]
            n1 = dve.do(lambda e: e.tensor_copy(knorm[:], nb), after=[mn] + prev.get("knorm_read", []), counts=g["kn"])
            free["NB"] = [n1]
            n2 = pool.do(lambda e: e.tensor_tensor(knorm[:], knorm[:], half[:, 0:KC], op=ALU.pow), after=[n1],
                         counts=g["kn_pool"])
            n3 = dve.do(lambda e: e.tensor_scalar(knorm[:], knorm[:], EPS_NORM, None, ALU.max), after=[n2],
                        counts=g["kn"])
            n4 = dve.do(lambda e: e.reciprocal(knorm[:], knorm[:]), after=[n3], counts=g["kn"])
            for c in range(KC):
                k5 = dve.do(lambda e, c=c: e.tensor_scalar(kv32[:, c, :], KV[:, c * D:(c + 1) * D], knorm[:, c:c + 1],
                                                           None, ALU.mult),
                            after=[n4, m] + prev.get("kv32_read", []), counts=g["kv_ev"])
            prev["knorm_read"] = [k5]
            free["KV"] = [k5]
            k6 = act.do(lambda e: e.activation(kv[0][:], kv32[:], ACT.Copy), after=[k5] + prev.get("kv_read", []),
                        counts=g["kv_hi"])
            k7 = dve.do(lambda e: e.tensor_tensor(kv[1][:], kv32[:], f32(kv[0][:]), op=ALU.subtract),
                        after=[k6, k5] + prev.get("kv_read", []), counts=g["kv_lo"])
            prev["kv32_read"] = [k7]

            for m_ in range(KC):
                terms = [(w, a, c, 512) for c in range(KC) for w, a in split3(Wqkv, xT)]
                terms += [(w, a, c, 0) for c in range(KC) for w, a in split3(kv, q2T)]
                for i, (w, a, c, off) in enumerate(terms):
                    yp = pe.do(lambda e, m_=m_, i=i, w=w, a=a, c=c, off=off, n=len(terms): e.matmul(
                        T[m_][:], w[:, c, off + m_ * P:off + (m_ + 1) * P], a[:, c, :],
                        start=(i == 0), stop=(i == n - 1)),
                        after=(free[f"T{m_}"] if off else q2T_ready + [k6, k7]), counts=g["yT_pe"])
                hi = act.do(lambda e, m_=m_: e.activation(yT[0][:, m_, :], T[m_][:], ACT.Identity,
                                                          bias=bvT[:, m_:m_ + 1]),
                            after=[yp, bias_ready] + prev.get("yT_read", []), counts=g["yT_hi"])
                lo = dve.do(lambda e, m_=m_: e.scalar_tensor_tensor(
                    yT[1][:, m_, :], T[m_][:], bvT[:, m_:m_ + 1], f32(yT[0][:, m_, :]), op0=ALU.add,
                    op1=ALU.subtract), after=[yp, hi] + prev.get("yT_read", []), counts=g["yT_lo"])
                free[f"T{m_}"] = [lo]
            prev["xT_read"] = prev["q2T_read"] = prev["kv_read"] = [yp]

            o = x1[b % 2]
            for u in range(N_TILES // 2):
                for t in (2 * u, 2 * u + 1):
                    for c in range(KC):
                        for i, (a, w) in enumerate(split3(yT, Wln)):
                            m = pe.do(lambda e, t=t, c=c, i=i, a=a, w=w: e.matmul(
                                Y[:, (t % 2) * D:(t % 2 + 1) * D], a[:, c, t * P:(t + 1) * P], w[:, c, :],
                                start=(c == 0 and i == 0), stop=(c == KC - 1 and i == 2)),
                                after=[hi, lo, wln_ready] + (free["Y"] if t % 2 == 0 else []), counts=g["y_pe"])
                ye = dve.do(lambda e, u=u, o=o: e.tensor_tensor(
                    o[:, 2 * u:2 * u + 2, :], Y[:].rearrange("p (a c) -> p a c", a=2), xb[:, 2 * u:2 * u + 2, :],
                    op=ALU.add), after=[m, e_xb, last_store.get(b - 2)], counts=g["x1"])
                free["Y"] = [ye]
            prev["yT_read"] = [m]
            prev["x1"] = [ye]
            prev["xb_all"] = [e_xb, n]
            last_store[b] = sp.do(lambda e, b=b, o=o: e.dma_start(x1_dram[b], o[:]), after=[ye], counts=stored[b % 2])
        sp.do(lambda e: e.nop(), after=[last_store[B - 1], last_store[B - 2]])
        p.run()


SCORE_AT = {3: 0, 2: 512, 0: 896, 1: 1024}
PROB_T_AT = {0: 0, 1: 512, 3: 896, 2: 1024}
TRIANGLE = 1280
V_TILE_AT = (2, 4, 6, 7)
BANK_TILES = ((3,), (2, 0), (1,))
BANK_COLS = ((0, 512), (512, 1024), (1024, TRIANGLE))


def cross_attention(nc, d, x1_dram, x2_dram, rows_dram, routing):
    with ExitStack() as stack:
        p = Part(nc, stack, "xa")
        pe, act, dve, pool, sp = p.pe, p.act, p.dve, p.pool, p.sp
        ident, const_ready, _ = constants(p)
        cols = lambda n: p.sb(n, [P, N_TILES, D])
        xn = cols("xn")
        stage = {"tile": None, "dma": p.dma_counter("w_in"), "hi": p.counter("w_hi"),
                 "split": p.counter("w_split"), "free": []}
        ctx32 = p.sb("ctx32", [P, KC, S])
        stage_a = dict(stage, tile=ctx32[:].rearrange("p a b -> p (a b)"))
        W = {}
        w_ready = {}
        for name in ("WqT", "WkT", "WvT"):
            hi = p.sb(name + "_hi", [P, KC, INNER], F32R)
            lo = p.sb(name + "_lo", [P, KC, INNER], F32R)
            W[name] = (hi, lo)
            for c in range(KC):
                view = stage_a["tile"]
                got = sp.do(lambda e, name=name, c=c: e.dma_start(view[:, 0:INNER], d[name][c * P:(c + 1) * P, :]),
                            after=stage["free"], counts=stage["dma"])
                if name == "WqT":
                    got = dve.do(lambda e: e.tensor_scalar(view[:, 0:INNER], view[:, 0:INNER], HD ** -0.5, None,
                                                           ALU.mult), after=[got], counts=stage["split"])
                a = act.do(lambda e, hi=hi, c=c: e.activation(hi[:, c, :], view[:, 0:INNER], ACT.Copy), after=[got],
                           counts=stage["hi"])
                s = dve.do(lambda e, hi=hi, lo=lo, c=c: e.tensor_tensor(lo[:, c, :], view[:, 0:INNER],
                                                                        f32(hi[:, c, :]), op=ALU.subtract),
                           after=[got, a], counts=stage["split"])
                stage["free"] = [s]
            w_ready[name] = s
        stage_last = s
        WoT = p.sb("WoT", [P, PAIRS, D])
        bqT, bkT = p.sb("bqT", [P, PAIRS]), p.sb("bkT", [P, PAIRS])
        bv, bo = p.sb("bv", [P, INNER]), p.sb("bo", [P, D])
        rw, rb = p.sb("rw", [P, KC, E]), p.sb("rb", [P, E])
        bias_in = p.dma_counter("bias_in")
        row = lambda v, n: v.rearrange("(a n) -> a n", a=1).broadcast_to([P, n])
        sp.do(lambda e: e.dma_start(WoT[:], d['WoT'].rearrange("(k p) n -> p k n", p=P)), counts=bias_in)
        sp.do(lambda e: e.dma_start(bqT[:], d['bq'].rearrange("(k p) -> p k", p=P), allow_slow_non_contiguous=True),
              counts=bias_in)
        sp.do(lambda e: e.dma_start(bkT[:], d['bk'].rearrange("(k p) -> p k", p=P), allow_slow_non_contiguous=True),
              counts=bias_in)
        sp.do(lambda e: e.dma_start(bv[:], row(d['bv'], INNER)), counts=bias_in)
        sp.do(lambda e: e.dma_start(bo[:], row(d['bo'], D)), counts=bias_in)
        sp.do(lambda e: e.dma_start(rw[:], d['router_w'].rearrange("(k p) n -> p k n", p=P)), counts=bias_in)
        bias_in_all = sp.do(lambda e: e.dma_start(rb[:], row(d['router_b'], E)), counts=bias_in)
        bias_ready = dve.do(lambda e: e.tensor_scalar(bqT[:], bqT[:], HD ** -0.5, None, ALU.mult),
                            after=[bias_in_all], counts=p.counter("bias"))
        const_p = p.counter("const_pool")

        identb, maskb = p.sb("identb", [P, P], BF16), p.sb("maskb", [P, P], BF16)
        tri, onesb = p.sb("tri", [P, P], BF16), p.sb("onesb", [P, P], BF16)
        for tile, fill in ((identb, 0.0), (maskb, 0.0), (tri, 1.0), (onesb, 1.0)):
            m0 = pool.do(lambda e, tile=tile, fill=fill: e.memset(tile[:], fill), counts=const_p)
        pool.do(lambda e: e.affine_select(out=identb[:], in_=identb[:], compare_op=ALU.not_equal, fill=1.0, base=0,
                                          pattern=[[-1, P]], channel_multiplier=1), after=[m0], counts=const_p)
        pool.do(lambda e: e.affine_select(out=maskb[:], in_=maskb[:], compare_op=ALU.is_ge, fill=NEG, base=0,
                                          pattern=[[-1, P]], channel_multiplier=1), after=[m0], counts=const_p)
        tri_ready = pool.do(lambda e: e.affine_select(out=tri[:], in_=tri[:], compare_op=ALU.is_ge, fill=0.0, base=-1,
                                                      pattern=[[1, P]], channel_multiplier=-1), after=[m0],
                            counts=const_p)
        ebase = p.sb("ebase", [P, E])
        for e_ in range(E):
            m1 = pool.do(lambda e, e_=e_: e.memset(ebase[:, e_:e_ + 1], float(e_ * REGION + 1)), counts=const_p)
        probs = p.sb("probs", [P, N_TILES, E + 4])
        sentinel = p.sb("sentinel", [P, N_TILES, 4])
        for i in range(4):
            pool.do(lambda e, i=i: e.memset(probs[:, :, E + i:E + i + 1], float(-1 - i)), counts=const_p)
            m2 = pool.do(lambda e, i=i: e.memset(sentinel[:, :, i:i + 1], float(-1 - i)), counts=const_p)
        count = routing["count"]
        consts = pool.do(lambda e: e.memset(count[:], 0.0), counts=const_p)

        ln2, ln3 = Norm(p, "ln2"), Norm(p, "ln3")
        x1 = [cols(f"x1_{i}") for i in range(2)]
        xT = [tuple(p.sb(f"xT{i}{j}", [P, KC, S], F32R) for j in range(2)) for i in range(2)]
        cT = [tuple(p.sb(f"cT{i}{j}", [P, KC, S], F32R) for j in range(2)) for i in range(2)]
        qT = [p.sb(f"qT{i}", [P, S]) for i in range(2)]
        kT = [[p.sb(f"kT{i}{j}", [P, S]) for j in range(2)] for i in range(2)]
        v = [p.sb(f"v{i}", [P, N_TILES, INNER // 2]) for i in range(2)]
        prob = [p.sb(f"prob{i}", [P, TRIANGLE]) for i in range(2)]
        probT = [p.sb(f"probT{i}", [P, TRIANGLE]) for i in range(2)]
        nmax = [p.sb(f"nmax{i}", [P, N_TILES]) for i in range(2)]
        sums = [p.sb(f"sums{i}", [P, N_TILES]) for i in range(2)]
        oT = p.sb("oT", [P, PAIRS, S])
        x2 = cols("x2")
        xn3 = cols("xn3")
        xn3T = p.sb("xn3T", [P, KC, S])
        small = lambda n, k=E: p.sb(n, [P, N_TILES, k])
        lg, repl, mask, key = small("lg"), small("repl", E + 4), small("mask"), small("key")
        maskb16 = p.sb("maskb16", [P, N_TILES, E], BF16)
        top8, key8 = small("top8", 8), small("key8", 8)
        red = p.sb("red", [P, N_TILES])
        rows_i = [p.sb(f"rows{i}", [P, N_TILES, TOPK], I32) for i in range(2)]

        SB = [p.bank(f"S{i}") for i in range(3)]
        TB = [p.bank(f"T{i}") for i in range(3)]
        OB, PJ = p.bank("O"), p.bank("PJ")
        free = {"S0": [], "S1": [], "S2": [], "T0": [], "T1": [], "T2": [], "O": [], "PJ": []}

        names = ("zero", "x_hi", "x_lo", "c_hi", "c_lo", "pj_pe", "q_ev", "k_ev_a", "k_ev_b", "v_ev", "s_pe", "max",
                 "exp", "rcp", "norm", "t_pe", "t_act", "t_dve", "pv_pe", "o_ev", "xb", "x2", "xn3T",
                 "r_dve", "r_act", "r_rows")
        g = {n: p.counter(n) for n in names}
        x1_in = [p.dma_counter(f"x1_in{i}") for i in range(2)]
        ctx_in, x2_out = p.dma_counter("ctx_in"), p.dma_counter("x2_out")
        scattered = p.dma_counter("scattered")

        for i in range(2):
            for j in range(2):
                z = dve.do(lambda e, i=i, j=j: e.memset(kT[i][j][64 * (1 - j):64 * (1 - j) + 64, :], 0.0),
                           counts=g["zero"])
        kzero = z
        last = {}
        G = lambda k: last.get(k, [])

        def load(b):
            last[f"x1_loaded{b}"] = [sp.do(lambda e: e.dma_start(x1[b % 2][:], x1_dram[b]),
                                           after=G(f"x1_free{b % 2}"), counts=x1_in[b % 2])]
            last["ctx_loaded"] = [sp.do(lambda e: e.dma_start(ctx32[:], d['ctxT'][b].rearrange("(k p) s -> p k s", p=P)),
                                        after=G("ctx32_free") + [stage_last], counts=ctx_in)]

        def split_ctx(b):
            hi, lo = cT[b % 2]
            a = act.do(lambda e: e.activation(hi[:], ctx32[:], ACT.Copy),
                       after=G("ctx_loaded") + G(f"cT_free{b % 2}"), counts=g["c_hi"])
            l = pool.do(lambda e: e.tensor_tensor(lo[:], ctx32[:], f32(hi[:]), op=ALU.subtract),
                        after=[a] + G("ctx_loaded") + G(f"cT_free{b % 2}"), counts=g["c_lo"])
            last["ctx32_free"] = [l]
            last[f"cT_ready{b}"] = [a, l]

        def norm2(b):
            last["xn_ready"] = [ln2.run(x1[b % 2], xn, G(f"x1_loaded{b}"), G("xn_free"))]
            last[f"xb{b}"] = [pool.do(lambda e: e.tensor_tensor(
                x1[b % 2][:], x1[b % 2][:], bo[:].rearrange("p (a c) -> p a c", a=1).broadcast_to([P, N_TILES, D]),
                op=ALU.add), after=G("xn_ready") + [bias_ready], counts=g["xb"])]

        def transpose_x(b, c):
            for t in range(N_TILES):
                m = pe.do(lambda e, t=t: e.transpose(PJ[:, t * P:(t + 1) * P], xn[:, t, c * P:(c + 1) * P], ident[:]),
                          after=G("xn_ready") + free["PJ"] + [const_ready], counts=g["pj_pe"])
            hi, lo = xT[b % 2]
            a = act.do(lambda e: e.activation(hi[:, c, :], PJ[:], ACT.Copy), after=[m] + G(f"xT_free{b % 2}"),
                       counts=g["x_hi"])
            l = dve.do(lambda e: e.tensor_tensor(lo[:, c, :], PJ[:], f32(hi[:, c, :]), op=ALU.subtract),
                       after=[m, a] + G(f"xT_free{b % 2}"), counts=g["x_lo"])
            free["PJ"] = [l]
            last["xn_free"] = [m]
            last[f"xT_ready{b}"] = G(f"xT_ready{b}") + [a, l]

        def project(src, w, col, ready):
            for c in range(KC):
                for i, (ww, xx) in enumerate(split3(W[w], src)):
                    m = pe.do(lambda e, c=c, i=i, ww=ww, xx=xx: e.matmul(
                        PJ[:], ww[:, c, col:col + P], xx[:, c, :], start=(c == 0 and i == 0),
                        stop=(c == KC - 1 and i == 2)), after=ready + [w_ready[w]] + free["PJ"], counts=g["pj_pe"])
            return m

        def project_q(n):
            b, pr = divmod(n, PAIRS)
            m = project(xT[b % 2], "WqT", pr * P, G(f"xT_ready{b}"))
            q = act.do(lambda e: e.activation(qT[n % 2][:], PJ[:], ACT.Identity, bias=bqT[:, pr:pr + 1]),
                       after=[m, bias_ready] + G(f"qT_free{n % 2}"), counts=g["q_ev"])
            free["PJ"] = [q]
            last[f"xT_free{b % 2}"] = [m]
            last[f"q_ready{n}"] = [q]

        def project_k(n):
            b, pr = divmod(n, PAIRS)
            m = project(cT[b % 2], "WkT", pr * P, G(f"cT_ready{b}"))
            a = act.do(lambda e: e.activation(kT[n % 2][0][0:64, :], PJ[0:64, :], ACT.Identity,
                                              bias=bkT[0:64, pr:pr + 1]),
                       after=[m, bias_ready] + G(f"kT_free{n % 2}"), counts=g["k_ev_a"])
            v_ = dve.do(lambda e: e.tensor_scalar(kT[n % 2][1][64:128, :], PJ[64:128, :], bkT[64:128, pr:pr + 1],
                                                  None, ALU.add),
                        after=[m] + G(f"kT_free{n % 2}"), counts=g["k_ev_b"])
            free["PJ"] = [a, v_]
            last[f"cT_free{b % 2}"] = [m]
            last[f"k_ready{n}"] = [a, v_, kzero]

        def project_v(n, t):
            b, half = divmod(n, 2)
            for c in range(KC):
                for i, (xx, ww) in enumerate(split3(cT[b % 2], W["WvT"])):
                    m = pe.do(lambda e, c=c, i=i, ww=ww, xx=xx: e.matmul(
                        PJ[:], xx[:, c, t * P:(t + 1) * P], ww[:, c, half * 512:half * 512 + 512],
                        start=(c == 0 and i == 0), stop=(c == KC - 1 and i == 2)),
                        after=G(f"cT_ready{b}") + [w_ready["WvT"]] + free["PJ"], counts=g["pj_pe"])
            v_ = dve.do(lambda e: e.tensor_tensor(v[n % 2][:, t, :], PJ[:], bv[:, half * 512:half * 512 + 512],
                                                  op=ALU.add),
                        after=[m, bias_ready] + G(f"v_free{n % 2}"), counts=g["v_ev"])
            free["PJ"] = [v_]
            last[f"cT_free{b % 2}"] = [m]
            last[f"v_ready{n}"] = [v_]

        def scores(hh):
            n, odd = divmod(hh, 2)
            for k, tiles in enumerate(BANK_TILES):
                for i in tiles:
                    at, width = SCORE_AT[i] - BANK_COLS[k][0], (i + 1) * P
                    pe.do(lambda e, k=k, i=i, at=at, width=width: e.matmul(
                        SB[k][:, at:at + width], qT[n % 2][:, i * P:(i + 1) * P], kT[n % 2][odd][:, 0:width],
                        start=True, stop=False), after=G(f"q_ready{n}") + G(f"k_ready{n}") + free[f"S{k}"])
                    m = pe.do(lambda e, k=k, at=at, width=width: e.matmul(
                        SB[k][:, at + width - P:at + width], identb[:], maskb[:], start=False, stop=True),
                        after=[tri_ready], counts=g["s_pe"])
                last[f"S{k}"] = [m]
            last[f"qT_free{n % 2}"] = last[f"kT_free{n % 2}"] = [m]

        def row_max(hh):
            for k, tiles in enumerate(BANK_TILES):
                for i in tiles:
                    at, width = SCORE_AT[i] - BANK_COLS[k][0], (i + 1) * P
                    r = dve.do(lambda e, k=k, i=i, at=at, width=width: e.tensor_reduce(
                        nmax[hh % 2][:, i:i + 1], SB[k][:, at:at + width], AX.X, ALU.max, negate=True),
                        after=G(f"S{k}") + G(f"nmax_free{hh % 2}"), counts=g["max"])
                last[f"max{k}"] = [r]

        def exponent(hh):
            for k, tiles in enumerate(BANK_TILES):
                for i in tiles:
                    at, width = SCORE_AT[i] - BANK_COLS[k][0], (i + 1) * P
                    a = act.do(lambda e, k=k, i=i, at=at, width=width: e.activation(
                        prob[hh % 2][:, SCORE_AT[i]:SCORE_AT[i] + width], SB[k][:, at:at + width], ACT.Exp,
                        bias=nmax[hh % 2][:, i:i + 1], accum_out=sums[hh % 2][:, i:i + 1]),
                        after=G(f"S{k}") + G(f"max{k}") + G(f"prob_free{hh % 2}") + G(f"sums_free{hh % 2}"),
                        counts=g["exp"])
                free[f"S{k}"] = [a]
            last[f"exp{hh}"] = [a]
            last[f"nmax_free{hh % 2}"] = [a]

        def normalise(hh):
            r = dve.do(lambda e: e.reciprocal(sums[hh % 2][:], sums[hh % 2][:]), after=G(f"exp{hh}"), counts=g["rcp"])
            for i in range(N_TILES):
                at, width = SCORE_AT[i], (i + 1) * P
                s = dve.do(lambda e, i=i, at=at, width=width: e.tensor_scalar(
                    prob[hh % 2][:, at:at + width], prob[hh % 2][:, at:at + width], sums[hh % 2][:, i:i + 1], None,
                    ALU.mult), after=[r], counts=g["norm"])
            last[f"norm{hh}"] = [s]
            last[f"sums_free{hh % 2}"] = [s]

        def transpose_probs(hh):
            for k, tiles in enumerate(((0,), (1, 3), (2,))):
                for j in tiles:
                    for i in range(j, N_TILES):
                        at = PROB_T_AT[j] - BANK_COLS[k][0] + (i - j) * P
                        m = pe.do(lambda e, k=k, i=i, j=j, at=at: e.transpose(
                            TB[k][:, at:at + P], prob[hh % 2][:, SCORE_AT[i] + j * P:SCORE_AT[i] + (j + 1) * P],
                            ident[:]), after=G(f"norm{hh}") + free[f"T{k}"], counts=g["t_pe"])
                lo_, hi_ = BANK_COLS[k]
                if k == 1:
                    ev = dve.do(lambda e, k=k, lo_=lo_, hi_=hi_: e.tensor_copy(probT[hh % 2][:, lo_:hi_],
                                                                              TB[k][:, 0:hi_ - lo_]),
                                after=[m] + G(f"probT_free{hh % 2}"), counts=g["t_dve"])
                else:
                    ev = act.do(lambda e, k=k, lo_=lo_, hi_=hi_: e.activation(probT[hh % 2][:, lo_:hi_],
                                                                             TB[k][:, 0:hi_ - lo_], ACT.Copy),
                                after=[m] + G(f"probT_free{hh % 2}"), counts=g["t_act"])
                free[f"T{k}"] = [ev]
                last[f"probT{hh}"] = G(f"probT{hh}") + [ev]
            last[f"prob_free{hh % 2}"] = [m]

        def weigh_values(hh):
            b, h = divmod(hh, H)
            n, col, lo_ = hh // 8, (h % 8) // 2 * P, 64 * (h % 2)
            for j in range(N_TILES):
                m = pe.do(lambda e, j=j: e.matmul(
                    OB[:, j * P:512], v[n % 2][:, j, col:col + P],
                    probT[hh % 2][:, PROB_T_AT[j]:PROB_T_AT[j] + (N_TILES - j) * P],
                    start=(j == 0), stop=(j == N_TILES - 1)),
                    after=G(f"probT{hh}") + G(f"v_ready{n}") + free["O"], counts=g["pv_pe"])
            a = act.do(lambda e: e.activation(oT[lo_:lo_ + 64, h // 2, :], OB[lo_:lo_ + 64, :], ACT.Copy),
                       after=[m] + G("oT_free"), counts=g["o_ev"])
            free["O"] = [a]
            last[f"probT_free{hh % 2}"] = last[f"v_free{n % 2}"] = [m]
            last[f"oT_ready{b}"] = [a]

        def output(b, u):
            for t in (2 * u, 2 * u + 1):
                for pr in range(PAIRS):
                    m = pe.do(lambda e, t=t, pr=pr: e.matmul(
                        PJ[:, (t % 2) * D:(t % 2 + 1) * D], oT[:, pr, t * P:(t + 1) * P], WoT[:, pr, :],
                        start=(pr == 0), stop=(pr == PAIRS - 1)),
                        after=G(f"oT_ready{b}") + [bias_ready] + free["PJ"], counts=g["pj_pe"])
            o = dve.do(lambda e: e.tensor_tensor(x2[:, 2 * u:2 * u + 2, :], PJ[:].rearrange("p (a c) -> p a c", a=2),
                                                 x1[b % 2][:, 2 * u:2 * u + 2, :], op=ALU.add),
                       after=[m] + G(f"xb{b}") + G("x2_free"), counts=g["x2"])
            free["PJ"] = [o]
            last["oT_free"] = [m]
            last[f"x1_free{b % 2}"] = [o]
            last["x2_ready"] = [o]

        def norm3(b):
            s = sp.do(lambda e: e.dma_start(x2_dram[b], x2[:]), after=G("x2_ready"), counts=x2_out)
            last["xn3_ready"] = [ln3.run(x2, xn3, G("x2_ready"), G("xn3_free"))]
            last["x2_free"] = [s] + G("xn3_ready")

        def transpose_x3(b, c):
            for t in range(N_TILES):
                m = pe.do(lambda e, t=t: e.transpose(PJ[:, t * P:(t + 1) * P], xn3[:, t, c * P:(c + 1) * P], ident[:]),
                          after=G("xn3_ready") + free["PJ"], counts=g["pj_pe"])
            a = act.do(lambda e: e.activation(xn3T[:, c, :], PJ[:], ACT.Copy), after=[m] + G("xn3T_free"),
                       counts=g["xn3T"])
            free["PJ"] = [a]
            last["xn3T_ready"] = [a]

        bc = lambda ap: ap.rearrange("p (t a) -> p t a", a=1).broadcast_to([P, N_TILES, E])
        be = lambda ap: ap.rearrange("p (a e) -> p a e", a=1).broadcast_to([P, N_TILES, E])

        def route(b):
            for t in range(N_TILES):
                for c in range(KC):
                    m = pe.do(lambda e, t=t, c=c: e.matmul(PJ[:, t * E:(t + 1) * E], xn3T[:, c, t * P:(t + 1) * P],
                                                           rw[:, c, :], start=(c == 0), stop=(c == KC - 1)),
                              after=G("xn3T_ready") + free["PJ"], counts=g["pj_pe"])
            last["xn3T_free"] = [m]
            R = lambda make, after: dve.do(make, after=after, counts=g["r_dve"])
            bt = slice(b * N_TILES, (b + 1) * N_TILES)
            weight, pos, chosen = routing["weight"], routing["pos"], routing["chosen"]
            pr = probs[:, :, 0:E]
            r = R(lambda e: e.tensor_tensor(lg[:], PJ[:, 0:N_TILES * E].rearrange("p (t e) -> p t e", t=N_TILES),
                                            be(rb[:]), op=ALU.add), [m, bias_ready])
            free["PJ"] = [r]
            r = R(lambda e: e.tensor_reduce(red[:], lg[:], AX.X, ALU.max), [r])
            r = R(lambda e: e.tensor_tensor(lg[:], lg[:], bc(red[:]), op=ALU.subtract), [r])
            x = act.do(lambda e: e.activation(pr, lg[:], ACT.Exp), after=[r, consts] + G("probs_free"),
                       counts=g["r_act"])
            r = R(lambda e: e.tensor_reduce(red[:], pr, AX.X, ALU.add), [x, r])
            r = R(lambda e: e.reciprocal(red[:], red[:]), [r])
            r = R(lambda e: e.tensor_tensor(pr, pr, bc(red[:]), op=ALU.mult), [r])
            for t in range(N_TILES):
                r2 = R(lambda e, t=t: e.max(top8[:, t, :], probs[:, t, 0:E]), [r])
            r = R(lambda e: e.tensor_copy(top8[:, :, TOPK:8], sentinel[:]), [r2])
            for t in range(N_TILES):
                r2 = R(lambda e, t=t: e.match_replace(repl[:, t, :], top8[:, t, :], probs[:, t, :], -8.0), [r])
            r = R(lambda e: e.tensor_scalar(mask[:], repl[:, :, 0:E], -8.0, None, ALU.is_equal), [r2])
            mb = R(lambda e: e.tensor_copy(maskb16[:], mask[:]), [r])
            r = R(lambda e: e.tensor_tensor(pr, pr, mask[:], op=ALU.mult), [mb])
            r = R(lambda e: e.tensor_reduce(red[:], pr, AX.X, ALU.add), [r])
            r = R(lambda e: e.reciprocal(red[:], red[:]), [r])
            r = R(lambda e: e.tensor_tensor(weight[:, bt, :], pr, bc(red[:]), op=ALU.mult), [r])
            r = R(lambda e: e.tensor_copy(chosen[:, bt, :], mask[:]), [r])
            last["probs_free"] = [r]
            last["mask_ready"] = [r]

        def place(b):
            bt = slice(b * N_TILES, (b + 1) * N_TILES)
            pos = routing["pos"]
            for t in range(N_TILES + 1):
                terms = [(tri, t)] if t < N_TILES else []
                terms += [(onesb, s_) for s_ in range(min(t, N_TILES))]
                for i, (w, s_) in enumerate(terms):
                    m = pe.do(lambda e, t=t, i=i, w=w, s_=s_, n=len(terms): e.matmul(
                        PJ[:, t * E:(t + 1) * E], w[:], maskb16[:, s_, :], start=(i == 0), stop=(i == n - 1)),
                        after=G("mask_ready") + [consts] + free["PJ"], counts=g["pj_pe"])
            R = lambda make, after: dve.do(make, after=after, counts=g["r_dve"])
            r = R(lambda e: e.tensor_tensor(pos[:, bt, :], PJ[:, 0:N_TILES * E].rearrange("p (t e) -> p t e", t=N_TILES),
                                            be(count[:]), op=ALU.add), [m, consts] + G("count_ready"))
            c = R(lambda e: e.tensor_tensor(count[:], PJ[:, N_TILES * E:(N_TILES + 1) * E], count[:], op=ALU.add), [r])
            last["count_ready"] = [c]
            free["PJ"] = [c]
            r = R(lambda e: e.tensor_tensor(key[:], pos[:, bt, :], be(ebase[:]), op=ALU.add), [r])
            r = R(lambda e: e.tensor_tensor(key[:], key[:], mask[:], op=ALU.mult), [r])
            for t in range(N_TILES):
                r2 = R(lambda e, t=t: e.max(key8[:, t, :], key[:, t, :]), [r])
            w = dve.do(lambda e: e.tensor_scalar(rows_i[b % 2][:], key8[:, :, 0:TOPK], -1.0, None, ALU.add),
                       after=[r2] + G(f"rows_free{b % 2}"), counts=g["r_rows"])
            for t in range(N_TILES):
                for k in range(TOPK):
                    s = pool.do(lambda e, t=t, k=k: e.indirect_dma_start(
                        rows_dram, bass.IndirectOffsetOnAxis(rows_i[b % 2][:, t, k:k + 1], 0), xn3[:, t, :], None),
                        after=[w] + G("xn3_ready"), counts=scattered)
            last["xn3_free"] = last[f"rows_free{b % 2}"] = [s]

        def tasks(b, h):
            nxt, out = b * PAIRS + h // 2 + 1, b - 1
            first, second, third = [], [], []
            if nxt < B * PAIRS:
                first.append(lambda: (project_k if h % 2 else project_q)(nxt))
            half = 2 * b + 1 + h // 8
            if h % 8 in V_TILE_AT and half < 2 * B:
                second.append(lambda: project_v(half, V_TILE_AT.index(h % 8)))
            if b + 1 < B:
                if h == 4:
                    second.append(lambda: load(b + 1))
                if h == 6:
                    second.append(lambda: split_ctx(b + 1))
                if h == 9:
                    second.append(lambda: norm2(b + 1))
                if h in (11, 13):
                    third.append(lambda: transpose_x(b + 1, (h - 11) // 2))
            if out >= 0:
                if h == 2:
                    third.append(lambda: output(out, 0))
                    third.append(lambda: output(out, 1))
                    third.append(lambda: norm3(out))
                if h in (5, 6):
                    third.append(lambda: transpose_x3(out, h - 5))
                if h == 7:
                    third.append(lambda: route(out))
                if h == 9:
                    third.append(lambda: place(out))
            return first, second, third

        load(0)
        split_ctx(0)
        norm2(0)
        transpose_x(0, 0)
        transpose_x(0, 1)
        project_q(0)
        project_k(0)
        for t in range(N_TILES):
            project_v(0, t)
        for hh in range(B * H + 2):
            first, second, third = tasks(*divmod(hh, H)) if hh < B * H else ([], [], [])
            for f in first:
                f()
            if hh < B * H:
                scores(hh)
            if 0 <= hh - 1 < B * H:
                normalise(hh - 1)
            if hh < B * H:
                row_max(hh)
                exponent(hh)
            for f in second:
                f()
            if 0 <= hh - 1 < B * H:
                transpose_probs(hh - 1)
            for f in third:
                f()
            if hh - 2 >= 0:
                weigh_values(hh - 2)
        output(B - 1, 0)
        output(B - 1, 1)
        norm3(B - 1)
        transpose_x3(B - 1, 0)
        transpose_x3(B - 1, 1)
        route(B - 1)
        place(B - 1)
        sp.do(lambda e: e.nop(), after=G("x2_free"))
        pool.do(lambda e: e.nop(), after=G("xn3_free"))
        p.run()


def experts(nc, d, rows_dram, y_dram, routing):
    with ExitStack() as stack:
        p = Part(nc, stack, "ex")
        pe, act, dve, pool, sp = p.pe, p.act, p.dve, p.pool, p.sp
        ident, const_ready, _ = constants(p)
        NX = 3
        W1 = p.sb("w1", [P, E * KC * FF])
        W2 = p.sb("w2", [P, E * FC * D])
        WE = KC * FF
        b1T = p.sb("b1T", [P, E * FC])
        x_in = [p.sb(f"x{i}", [P, RT, D]) for i in range(NX)]
        xT = [tuple(p.sb(f"xT{i}{j}", [P, KC, ROWS], F32R) for j in range(2)) for i in range(2)]
        w1 = [tuple(p.sb(f"w1_{i}{j}", [P, KC, FF], F32R) for j in range(2)) for i in range(2)]
        w2 = [tuple(p.sb(f"w2_{i}{j}", [P, FC, D], F32R) for j in range(2)) for i in range(2)]
        b1 = [p.sb(f"b1_{i}", [P, FC]) for i in range(2)]
        h32 = p.sb("h32", [P, FC, ROWS])
        hT = [tuple(p.sb(f"hT{i}{j}", [P, FC, ROWS], F32R) for j in range(2)) for i in range(2)]
        y = [p.sb(f"y{i}", [P, RT, D]) for i in range(2)]
        XB = [p.bank(f"X{i}") for i in range(2)]
        HB = [p.bank(f"H{i}") for i in range(4)]
        YB = [p.bank(f"Y{i}") for i in range(2)]

        w_in = [p.dma_counter(f"w_in{e_}") for e_ in range(E)]
        b1_in = p.dma_counter("b1_in")
        b1_ready = sp.do(lambda e: e.dma_start(b1T[:], d['b1T']), counts=b1_in)
        w_ready = []
        for e_ in range(E):
            sp.do(lambda e, e_=e_: e.dma_start(W1[:, e_ * WE:(e_ + 1) * WE].rearrange("p (k n) -> p k n", k=KC),
                                               d['w1'][e_].rearrange("(k p) n -> p k n", p=P)), counts=w_in[e_])
            w_ready.append(sp.do(lambda e, e_=e_: e.dma_start(
                W2[:, e_ * WE:(e_ + 1) * WE].rearrange("p (k n) -> p k n", k=FC),
                d['w2'][e_].rearrange("(k p) n -> p k n", p=P)), counts=w_in[e_]))

        tab = p.counter("tables")
        R = lambda make, after: dve.do(make, after=after, counts=tab)
        count = routing["count"]
        scr = p.sb("scr", [P, 4, E])
        scr_i = p.sb("scr_i", [P, E], I32)
        tiles, cum, base, one = (scr[:, i, :] for i in range(4))
        tile_no = p.sb("tile_no", [1, MOE_TILES])
        spare = y[1][:].rearrange("p a c -> p (a c)")
        top = spare[:, 0:ALL_TILES * 8].rearrange("p (t k) -> p t k", k=8)
        before, row, hit = (spare[0:1, ALL_TILES * 8 + i * MOE_TILES:ALL_TILES * 8 + (i + 1) * MOE_TILES]
                            for i in range(3))
        owner = p.sb("owner", [1, MOE_TILES])
        owner_i, row_i = p.sb("owner_i", [1, MOE_TILES], I32), p.sb("row_i", [1, MOE_TILES], I32)
        pad_i = p.sb("pad_i", [1, E], I32)
        region = p.sb("region", [1, E])
        pool_tab = p.counter("pool_tab")
        pool.do(lambda e: e.iota(tile_no[:], [[1, MOE_TILES]], base=0, channel_multiplier=0,
                                 allow_small_or_imprecise_dtypes=True), counts=pool_tab)
        it = pool.do(lambda e: e.iota(region[:], [[REGION, E]], base=0, channel_multiplier=0,
                                      allow_small_or_imprecise_dtypes=True), counts=pool_tab)
        r = R(lambda e: e.memset(one, 1.0), [])
        r = R(lambda e: e.tensor_scalar(scr_i[:], count[:], float(ROWS - 1), None, ALU.add), [r])
        r = R(lambda e: e.tensor_scalar(scr_i[:], scr_i[:], ROWS.bit_length() - 1, None, ALU.arith_shift_right), [r])
        r = R(lambda e: e.tensor_copy(tiles, scr_i[:]), [r])
        r = R(lambda e: e.tensor_tensor_scan(cum, one, tiles, 0.0, ALU.mult, ALU.add), [r])
        r = R(lambda e: e.tensor_tensor(base, cum, tiles, op=ALU.subtract), [r])
        r = R(lambda e: e.tensor_scalar(base, base, float(ROWS), 1.0, ALU.mult, ALU.add), [r])
        r = R(lambda e: e.tensor_tensor(pad_i[:], count[0:1, :], region[:], op=ALU.add), [r, it])
        pad_ready = r
        r = R(lambda e: e.memset(owner[:], 0.0), [r])
        r = R(lambda e: e.memset(before, 0.0), [r])
        for e_ in range(E):
            h = R(lambda e, e_=e_: e.tensor_scalar(hit, tile_no[:], cum[0:1, e_:e_ + 1], None, ALU.is_ge), [r, it])
            r = R(lambda e: e.tensor_tensor(owner[:], owner[:], hit, op=ALU.add), [h])
            r = R(lambda e, e_=e_: e.scalar_tensor_tensor(before, hit, tiles[0:1, e_:e_ + 1], before,
                                                          op0=ALU.mult, op1=ALU.add), [r])
        r = R(lambda e: e.tensor_scalar(hit, owner[:], float(E), None, ALU.is_lt), [r])
        r = R(lambda e: e.tensor_tensor(owner[:], owner[:], hit, op=ALU.mult), [r])
        r = R(lambda e: e.tensor_copy(owner_i[:], owner[:]), [r])
        r = R(lambda e: e.tensor_tensor(row, tile_no[:], before, op=ALU.subtract), [r])
        r = R(lambda e: e.tensor_scalar(row, row, float(ROWS), None, ALU.mult), [r])
        r = R(lambda e: e.scalar_tensor_tensor(row, owner[:], float(REGION), row, op0=ALU.mult, op1=ALU.add), [r])
        table_ready = R(lambda e: e.tensor_tensor(row_i[:], row, hit, op=ALU.mult), [r])

        z = dve.do(lambda e: e.memset(y[0][:], 0.0), counts=p.counter("zero"))
        padded = p.dma_counter("padded")
        for e_ in range(E):
            def pad(e, e_=e_):
                at = e.value_load(pad_i[0:1, e_:e_ + 1], min_val=0, max_val=E * REGION - ROWS)
                return e.dma_start(rows_dram[bass.ds(at, ROWS), :].rearrange("(p a) c -> p a c", p=P), y[0][:])
            pads = sp.do(pad, after=[z, pad_ready], counts=padded)

        pos, chosen, weight = routing["pos"], routing["chosen"], routing["weight"]
        slots, slot_weight = routing["slots"], routing["slot_weight"]
        key = h32[:].rearrange("p a b -> p (a b)")[:, 0:ALL_TILES * E].rearrange("p (t e) -> p t e", e=E)
        eq = h32[:].rearrange("p a b -> p (a b)")[:, ALL_TILES * E:2 * ALL_TILES * E].rearrange("p (t e) -> p t e", e=E)
        r = R(lambda e: e.tensor_tensor(key, pos[:], base.rearrange("p (a e) -> p a e", a=1)
                                        .broadcast_to([P, ALL_TILES, E]), op=ALU.add), [table_ready])
        r = R(lambda e: e.tensor_tensor(key, key, chosen[:], op=ALU.mult), [r])
        for t in range(ALL_TILES):
            r2 = R(lambda e, t=t: e.max(top[:, t, :], key[:, t, :]), [r])
        for k in range(TOPK):
            r = R(lambda e, k=k: e.tensor_tensor(eq, key, top[:, :, k:k + 1].broadcast_to([P, ALL_TILES, E]),
                                                 op=ALU.is_equal), [r2, r])
            r = R(lambda e: e.tensor_tensor(eq, eq, weight[:], op=ALU.mult), [r])
            r = R(lambda e, k=k: e.tensor_reduce(slot_weight[:, :, k], eq, AX.X, ALU.add), [r])
        slots_done = R(lambda e: e.tensor_scalar(slots[:], top[:, :, 0:TOPK], -1.0, None, ALU.add), [r])

        g = {n: p.counter(n) for n in ("t_pe", "x_hi", "x_lo", "w1_hi", "w1_lo", "w2_hi", "w2_lo", "b1c", "h_pe",
                                      "gelu", "h_hi", "h_lo", "y_pe", "y_ev")}
        x_loaded = [p.dma_counter(f"x_loaded{i}") for i in range(NX)]
        y_stored = [p.dma_counter(f"y_stored{i}") for i in range(2)]
        last = {}
        G = lambda k: last.get(k, [])

        def load_rows(j):
            def load(e):
                at = e.value_load(row_i[0:1, j:j + 1], min_val=0, max_val=E * REGION - ROWS)
                return e.dma_start(x_in[j % NX][:], rows_dram[bass.ds(at, ROWS), :].rearrange("(a p) c -> p a c", p=P))
            last[f"x{j}"] = [sp.do(load, after=[table_ready, pads] + G(f"x_free{j % NX}"), counts=x_loaded[j % NX])]

        def owner_of(e, j):
            return e.value_load(owner_i[0:1, j:j + 1], min_val=0, max_val=E - 1)

        flat = lambda t: t[:].rearrange("p a b -> p (a b)")

        def split_w1(j):
            h1, l1 = w1[j % 2]
            regs = {}

            def w1_hi(e):
                regs["dve"] = owner_of(e, j)
                return e.tensor_copy(flat(h1), W1[:, bass.ds(regs["dve"] * WE, WE)])

            def w1_lo(e):
                at = owner_of(e, j)
                return e.tensor_tensor(flat(l1), W1[:, bass.ds(at * WE, WE)], f32(flat(h1)), op=ALU.subtract)
            wait = ([w_ready[e_] for e_ in range(E)] + [b1_ready, table_ready])
            a = dve.do(w1_hi, after=wait + G(f"w1_free{j % 2}"), counts=g["w1_hi"])
            b = pool.do(w1_lo, after=wait + [a] + G(f"w1_free{j % 2}"), counts=g["w1_lo"])
            c = dve.do(lambda e: e.tensor_copy(b1[j % 2][:], b1T[:, bass.ds(regs["dve"] * FC, FC)]),
                       after=G(f"b1_free{j % 2}"), counts=g["b1c"])
            last[f"w1_{j}"] = [a, b]
            last[f"b1_{j}"] = [c]

        def split_w2(j):
            h2, l2 = w2[j % 2]
            regs = {}

            def w2_hi(e):
                regs["dve"] = owner_of(e, j)
                return e.tensor_copy(flat(h2), W2[:, bass.ds(regs["dve"] * WE, WE)])
            d_ = dve.do(w2_hi, after=G(f"w2_free{j % 2}"), counts=g["w2_hi"])
            e_ = dve.do(lambda e: e.tensor_tensor(flat(l2), W2[:, bass.ds(regs["dve"] * WE, WE)], f32(flat(h2)),
                                                  op=ALU.subtract), after=[d_] + G(f"w2_free{j % 2}"),
                        counts=g["w2_lo"])
            last[f"w2_{j}"] = [d_, e_]

        def transpose_rows(j):
            bank = XB[j % 2]
            for c in range(KC):
                for a in range(RT):
                    m = pe.do(lambda e, c=c, a=a: e.transpose(bank[:, c * ROWS + a * P:c * ROWS + (a + 1) * P],
                                                              x_in[j % NX][:, a, c * P:(c + 1) * P], ident[:]),
                              after=G(f"x{j}") + G(f"X_free{j % 2}") + [const_ready], counts=g["t_pe"])
            last[f"x_free{j % NX}"] = [m]
            hi, lo = xT[j % 2]
            view = bank[:].rearrange("p (c s) -> p c s", c=KC)
            a = act.do(lambda e: e.activation(hi[:], view, ACT.Copy), after=[m] + G(f"xT_free{j % 2}"),
                       counts=g["x_hi"])
            l = dve.do(lambda e: e.tensor_tensor(lo[:], view, f32(hi[:]), op=ALU.subtract),
                       after=[m, a] + G(f"xT_free{j % 2}"), counts=g["x_lo"])
            last[f"X_free{j % 2}"] = [l]
            last[f"xT{j}"] = [a, l]

        def hidden(j):
            hh, hl = hT[j % 2]
            for u in range(FC // 2):
                bank = HB[2 * (j % 2) + u]
                for f in (2 * u, 2 * u + 1):
                    terms = [(w, x, c) for c in range(KC) for w, x in split3(w1[j % 2], xT[j % 2])]
                    for i, (w, x, c) in enumerate(terms):
                        m = pe.do(lambda e, f=f, i=i, w=w, x=x, c=c, bank=bank, n=len(terms): e.matmul(
                            bank[:, (f % 2) * ROWS:(f % 2 + 1) * ROWS], w[:, c, f * P:(f + 1) * P], x[:, c, :],
                            start=(i == 0), stop=(i == n - 1)),
                            after=G(f"w1_{j}") + G(f"xT{j}") + G(f"H_free{2 * (j % 2) + u}"), counts=g["h_pe"])
                for f in (2 * u, 2 * u + 1):
                    a = act.do(lambda e, f=f, bank=bank: e.activation(
                        h32[:, f, :], bank[:, (f % 2) * ROWS:(f % 2 + 1) * ROWS], ACT.Gelu, bias=b1[j % 2][:, f:f + 1]),
                        after=[m, slots_done] + G(f"b1_{j}") + G(f"h32_free{u}"), counts=g["gelu"])
                last[f"H_free{2 * (j % 2) + u}"] = [a]
                fs = slice(2 * u, 2 * u + 2)
                hi = act.do(lambda e, fs=fs: e.activation(hh[:, fs, :], h32[:, fs, :], ACT.Copy),
                            after=[a] + G(f"hT_free{j % 2}"), counts=g["h_hi"])
                lo = dve.do(lambda e, fs=fs: e.tensor_tensor(hl[:, fs, :], h32[:, fs, :], f32(hh[:, fs, :]),
                                                             op=ALU.subtract),
                            after=[a, hi] + G(f"hT_free{j % 2}"), counts=g["h_lo"])
                last[f"h32_free{u}"] = [lo]
                last[f"h{j}_{u}"] = [hi, lo]
            last[f"w1_free{j % 2}"] = last[f"xT_free{j % 2}"] = [m]
            last[f"b1_free{j % 2}"] = [a]

        def results(j):
            bank = YB[j % 2]
            for a in range(RT):
                terms = [(h, w, f) for f in range(FC) for h, w in split3(hT[j % 2], w2[j % 2])]
                for i, (h, w, f) in enumerate(terms):
                    m = pe.do(lambda e, a=a, i=i, h=h, w=w, f=f, n=len(terms): e.matmul(
                        bank[:, a * D:(a + 1) * D], h[:, f, a * P:(a + 1) * P], w[:, f, :],
                        start=(i == 0), stop=(i == n - 1)),
                        after=G(f"w2_{j}") + G(f"h{j}_{f // 2}") + G(f"Y_free{j % 2}"), counts=g["y_pe"])
            last[f"w2_free{j % 2}"] = last[f"hT_free{j % 2}"] = [m]
            o = act.do(lambda e: e.activation(y[j % 2][:], bank[:].rearrange("p (a c) -> p a c", a=RT), ACT.Copy),
                       after=[m] + G(f"y_free{j % 2}") + [pads], counts=g["y_ev"])
            last[f"Y_free{j % 2}"] = [o]
            last[f"y_free{j % 2}"] = [sp.do(lambda e: e.dma_start(
                y_dram[j * ROWS:(j + 1) * ROWS, :].rearrange("(a p) c -> p a c", p=P), y[j % 2][:]),
                after=[o], counts=y_stored[j % 2])]

        for j in range(NX):
            load_rows(j)
        split_w1(0)
        split_w1(1)
        split_w2(0)
        transpose_rows(0)
        for j in range(MOE_TILES + 1):
            if j + NX < MOE_TILES:
                load_rows(j + NX)
            if j + 1 < MOE_TILES:
                transpose_rows(j + 1)
            if j < MOE_TILES:
                hidden(j)
            if j + 2 < MOE_TILES:
                split_w1(j + 2)
            if j >= 1:
                results(j - 1)
            if j + 1 < MOE_TILES:
                split_w2(j + 1)
        sp.do(lambda e: e.nop(), after=G("y_free0") + G("y_free1") + [pads])
        p.run()


def combine(nc, d, x2_dram, y_dram, out, routing):
    with ExitStack() as stack:
        p = Part(nc, stack, "co")
        pe, act, dve, pool, sp = p.pe, p.act, p.dve, p.pool, p.sp
        ident, const_ready, _ = constants(p)
        slots, slot_weight, weight = routing["slots"], routing["slot_weight"], routing["weight"]
        NB = 6
        b2 = p.sb("b2", [E, D])
        wT = p.sb("wT", [E, TOKENS])
        got = [p.sb(f"got{i}", [P, TOPK, D]) for i in range(NB)]
        x2 = [p.sb(f"x2_{i}", [P, N_TILES, D]) for i in range(2)]
        o = [p.sb(f"o{i}", [P, N_TILES, D]) for i in range(2)]
        TB = [p.bank(f"T{i}") for i in range(2)]
        BB = [p.bank(f"B{i}") for i in range(2)]
        b2_in = p.dma_counter("b2_in")
        b2_ready = sp.do(lambda e: e.dma_start(b2[:], d['b2']), counts=b2_in)
        gathered = [p.dma_counter(f"gathered{i}") for i in range(NB)]
        x2_in = [p.dma_counter(f"x2_in{i}") for i in range(2)]
        stored = [p.dma_counter(f"stored{i}") for i in range(2)]
        g = {n: p.counter(n) for n in ("wT_pe", "wT_ev", "b_pe", "sum")}
        last = {}
        G = lambda k: last.get(k, [])

        def gather(tt):
            for k in range(TOPK):
                last[f"g{tt}"] = [pool.do(lambda e, k=k: e.indirect_dma_start(
                    got[tt % NB][:, k, :], None, y_dram, bass.IndirectOffsetOnAxis(slots[:, tt, k:k + 1], 0)),
                    after=G(f"got_free{tt % NB}"), counts=gathered[tt % NB])]

        for b in range(B):
            x2_ready = sp.do(lambda e, b=b: e.dma_start(x2[b % 2][:], x2_dram[b]), after=G(f"x2_free{b % 2}"),
                             counts=x2_in[b % 2])
            for t in range(N_TILES):
                m = pe.do(lambda e, b=b, t=t: e.transpose(TB[b % 2][0:E, t * P:(t + 1) * P],
                                                          weight[:, b * N_TILES + t, :], ident[:]),
                          after=[const_ready] + G(f"T_free{b % 2}"), counts=g["wT_pe"])
            w = act.do(lambda e, b=b: e.activation(wT[:, b * S:(b + 1) * S], TB[b % 2][0:E, :], ACT.Copy), after=[m],
                       counts=g["wT_ev"])
            last[f"T_free{b % 2}"] = [w]
            for t in range(N_TILES):
                tt = b * N_TILES + t
                gather(tt)
                m = pe.do(lambda e, tt=tt: e.matmul(BB[tt % 2][:, 0:D], wT[:, tt * P:(tt + 1) * P], b2[:],
                                                    start=True, stop=True),
                          after=[w, b2_ready] + G(f"B_free{tt % 2}"), counts=g["b_pe"])
                acc = o[b % 2][:, t, :]
                s = dve.do(lambda e, b=b, t=t, tt=tt, acc=acc: e.tensor_tensor(acc, BB[tt % 2][:, 0:D],
                                                                              x2[b % 2][:, t, :], op=ALU.add),
                           after=[m, x2_ready] + G(f"o_free{b % 2}"), counts=g["sum"])
                last[f"B_free{tt % 2}"] = [s]
                for k in range(TOPK):
                    s = dve.do(lambda e, tt=tt, k=k, acc=acc: e.scalar_tensor_tensor(
                        acc, got[tt % NB][:, k, :], slot_weight[:, tt, k:k + 1], acc, op0=ALU.mult, op1=ALU.add),
                        after=[s] + G(f"g{tt}"), counts=g["sum"])
                last[f"got_free{tt % NB}"] = [s]
            last[f"x2_free{b % 2}"] = [s]
            last[f"o_free{b % 2}"] = [sp.do(lambda e, b=b: e.dma_start(
                out[b].rearrange("(t p) c -> p t c", p=P), o[b % 2][:]), after=[s], counts=stored[b % 2])]
        sp.do(lambda e: e.nop(), after=G("o_free0") + G("o_free1"))
        p.run()


def decoder_layer(nc, d, out):
    with ExitStack() as stack:
        scratch = lambda n, shape: nc.dram_tensor(n, shape, F32, kind="Internal").ap()
        x1_dram = scratch("x1_rows", [B, P, N_TILES, D])
        x2_dram = scratch("x2_rows", [B, P, N_TILES, D])
        rows_dram = scratch("expert_rows", [E * REGION, D])
        y_dram = scratch("expert_results", [MOE_TILES * ROWS, D])
        first_attention(nc, d, x1_dram)
        sb = lambda n, shape, dt=F32: stack.enter_context(nc.sbuf_tensor("routing_" + n, shape, dt))
        routing = {n: sb(n, [P, ALL_TILES, E]) for n in ("weight", "pos", "chosen")}
        routing["count"] = sb("count", [P, E])
        routing["slots"] = sb("slots", [P, ALL_TILES, TOPK], I32)
        routing["slot_weight"] = sb("slot_weight", [P, ALL_TILES, TOPK])
        cross_attention(nc, d, x1_dram, x2_dram, rows_dram, routing)
        experts(nc, d, rows_dram, y_dram, routing)
        combine(nc, d, x2_dram, y_dram, out, routing)


def kernel(**inputs):
    import concourse.bacc as bacc
    from concourse.bass_utils import run_bass_kernel_spmd

    take = lambda name: np.asarray(inputs[name])
    own = {n: take(f"L0_attn_{n}") for n in ("Wqkv", "bqkv", "Wln", "bln")}
    own |= {n: take(f"L0_xattn_{n}") for n in ("bq", "bk", "bv", "bo")}
    own |= {n + "T": take(f"L0_xattn_{n}").T for n in ("Wq", "Wk", "Wv", "Wo")}
    own |= {n: take(f"L0_ffn_{n}") for n in ("router_w", "router_b", "w1", "w2", "b2")}
    own["b1T"] = take("L0_ffn_b1").reshape(E, FC, P).transpose(2, 0, 1).reshape(P, E * FC)
    own["x"] = take("x")
    own["ctxT"] = take("ctx_1024").transpose(0, 2, 1)

    nc = bacc.Bacc("TRN2", target_bir_lowering=False, num_devices=1)
    arrays, d = {}, {}
    for name, a in own.items():
        arrays["in_" + name] = np.ascontiguousarray(a)
        d[name] = nc.dram_tensor("in_" + name, a.shape, F32, kind="ExternalInput").ap()
    out = nc.dram_tensor("out", (B, S, D), F32, kind="ExternalOutput").ap()
    decoder_layer(nc, d, out)
    result = run_bass_kernel_spmd(nc, [arrays], core_ids=[0])
    return result.results[0]["out"]
```

```python
from contextlib import ExitStack

import numpy as np

import concourse.bass as bass
from concourse import mybir

F32 = mybir.dt.float32
F32R = mybir.dt.float32r
BF16 = mybir.dt.bfloat16
I32 = mybir.dt.int32
ACT = mybir.ActivationFunctionType
ALU = mybir.AluOpType
AX = mybir.AxisListType

P = 128
B, S, D = 8, 512, 256
N_TILES = S // P
KC = D // P
H, HD = 16, 64
INNER = H * HD
PAIRS = H // 2
E, TOPK, FF = 16, 4, 512
FC = FF // P
TOKENS = B * S
ALL_TILES = TOKENS // P
ROWS = 256
RT = ROWS // P
REGION = TOKENS + ROWS
MOE_TILES = (TOKENS * TOPK + E * (ROWS - 1)) // ROWS
LN_EPS, EPS_SUM, EPS_NORM = 1e-5, 1e-7, 1e-12
NEG = -1e30


class Counter:

    def __init__(self, sem, step=1):
        self.sem, self.step, self.value = sem, step, 0

    def next(self):
        self.value += self.step
        return (self, self.value)


class Queue:

    def __init__(self):
        self.steps = []

    def do(self, make, after=(), counts=None):
        self.steps.append((make, [a for a in after if a is not None], counts))
        return counts.next() if counts is not None else None

    def play(self, engine):
        waited = {}
        for make, after, counts in self.steps:
            for sig, value in after:
                if waited.get(sig, 0) < value:
                    engine.wait_ge(sig.sem, value)
                    waited[sig] = value
            instruction = make(engine)
            if counts is not None:
                instruction.then_inc(counts.sem, counts.step)


class Part:

    def __init__(self, nc, stack, name):
        self.nc, self.stack, self.name = nc, stack, name
        self.pe, self.act, self.dve, self.pool, self.sp = (Queue() for _ in range(5))

    def sb(self, name, shape, dtype=F32):
        return self.stack.enter_context(self.nc.sbuf_tensor(f"{self.name}_{name}", shape, dtype))

    def bank(self, name):
        return self.stack.enter_context(self.nc.psum_tensor(f"{self.name}_{name}", [P, 512], F32))

    def counter(self, name, step=1):
        return Counter(self.stack.enter_context(self.nc.semaphore(f"{self.name}_{name}")), step)

    def dma_counter(self, name):
        return self.counter(name, 16)

    def run(self):
        with self.nc.Block() as block:
            for register, queue in ((block.tensor, self.pe), (block.scalar, self.act), (block.vector, self.dve),
                                    (block.gpsimd, self.pool), (block.sync, self.sp)):
                register(queue.play)


def split3(a, b):
    (ah, al), (bh, bl) = a, b
    return ((al, bh), (ah, bl), (ah, bh))


def f32(ap):
    return ap.bitcast(F32)


def constants(part):
    done = part.counter("const")
    ident = part.sb("ident", [P, P])
    e0 = part.pool.do(lambda e: e.memset(ident[:], 0.0), counts=done)
    e1 = part.pool.do(lambda e: e.affine_select(out=ident[:], in_=ident[:], compare_op=ALU.not_equal, fill=1.0,
                                                base=0, pattern=[[-1, P]], channel_multiplier=1),
                      after=[e0], counts=done)
    return ident, e1, done


def load_split(part, name, dram, shape, stage, scale=None):
    hi, lo = part.sb(name + "_hi", shape, F32R), part.sb(name + "_lo", shape, F32R)
    dims = "p a b -> p (a b)"
    size = shape[1] * shape[2]
    view = stage["tile"][:, 0:size]
    got = part.sp.do(lambda e: e.dma_start(view.rearrange("p (a b) -> p a b", a=shape[1]), dram),
                     after=stage["free"], counts=stage["dma"])
    h2, l2 = hi[:].rearrange(dims), lo[:].rearrange(dims)
    if scale is not None:
        got = part.dve.do(lambda e: e.tensor_scalar(view, view, scale, None, ALU.mult), after=[got],
                          counts=stage["split"])
    a = part.act.do(lambda e: e.activation(h2, view, ACT.Copy), after=[got], counts=stage["hi"])
    d = part.dve.do(lambda e: e.tensor_tensor(l2, view, f32(h2), op=ALU.subtract), after=[got, a],
                    counts=stage["split"])
    stage["free"] = [d]
    return (hi, lo), d


class Norm:

    def __init__(self, part, name):
        self.part = part
        self.stats = part.sb(name + "_stats", [P, N_TILES, 6])
        self.mv = part.sb(name + "_mv", [P, N_TILES, 2])
        self.rstd = part.sb(name + "_rstd", [P, N_TILES])
        self.power = part.sb(name + "_power", [P, N_TILES])
        self.dve, self.pool = part.counter(name + "_dve"), part.counter(name + "_pool")
        self.power_set = part.pool.do(lambda e: e.memset(self.power[:], -0.5), counts=self.pool)
        self.last = []

    def run(self, x, out, ready, out_free):
        p, mv, stats, rstd = self.part, self.mv, self.stats, self.rstd
        for t in range(N_TILES):
            s = p.dve.do(lambda e, t=t: e.bn_stats(stats[:, t, :], x[:, t, :]), after=ready + self.last,
                         counts=self.dve)
        for t in range(N_TILES):
            a = p.dve.do(lambda e, t=t: e.bn_aggr(mv[:, t, :], stats[:, t, :]), after=[s], counts=self.dve)
        v = p.dve.do(lambda e: e.tensor_scalar(rstd[:], mv[:, :, 1], LN_EPS, None, ALU.add), after=[a],
                     counts=self.dve)
        r = p.pool.do(lambda e: e.tensor_tensor(rstd[:], rstd[:], self.power[:], op=ALU.pow),
                      after=[v, self.power_set], counts=self.pool)
        for t in range(N_TILES):
            d = p.dve.do(lambda e, t=t: e.tensor_scalar(out[:, t, :], x[:, t, :], mv[:, t, 0:1], rstd[:, t:t + 1],
                                                        ALU.subtract, ALU.mult),
                         after=[r] + out_free, counts=self.dve)
        self.last = [d]
        return d


def first_attention(nc, d, x1_dram):
    with ExitStack() as stack:
        p = Part(nc, stack, "a1")
        pe, act, dve, pool, sp = p.pe, p.act, p.dve, p.pool, p.sp
        ident, const_ready, _ = constants(p)
        stage = {"tile": p.sb("stage", [P, KC * 768]), "dma": p.dma_counter("w_in"), "hi": p.counter("w_hi"),
                 "split": p.counter("w_split"), "free": []}
        x_loaded = [p.dma_counter(f"x_loaded{i}") for i in range(2)]
        x_in = [p.sb(f"x{i}", [P, N_TILES, D]) for i in range(2)]

        def load_x(b, free):
            return sp.do(lambda e: e.dma_start(x_in[b % 2][:], d['x'][b].rearrange("(t p) c -> p t c", p=P)),
                         after=free, counts=x_loaded[b % 2])

        Wqkv, wqkv_ready = load_split(p, "wqkv", d['Wqkv'].rearrange("(k p) n -> p k n", p=P), [P, KC, 768], stage)
        Wln, wln_ready = load_split(p, "wln", d['Wln'].rearrange("(k p) n -> p k n", p=P), [P, KC, D], stage)
        bias_in = p.dma_counter("bias_in")
        bqkv = p.sb("bqkv", [P, 768])
        bvT = p.sb("bvT", [P, KC])
        bln = p.sb("bln", [P, D])
        sp.do(lambda e: e.dma_start(bqkv[:], d['bqkv'].rearrange("(a n) -> a n", a=1).broadcast_to([P, 768])),
              counts=bias_in)
        sp.do(lambda e: e.dma_start(bvT[:], d['bqkv'][512:768].rearrange("(k p) -> p k", p=P),
                                    allow_slow_non_contiguous=True), counts=bias_in)
        bias_ready = sp.do(lambda e: e.dma_start(bln[:], d['bln'].rearrange("(a n) -> a n", a=1)
                                                 .broadcast_to([P, D])), counts=bias_in)
        norm = Norm(p, "ln")
        xn = p.sb("xn", [P, N_TILES, D])
        xT = [tuple(p.sb(f"xT{i}{j}", [P, KC, S], F32R) for j in range(2)) for i in range(2)]
        qk = p.sb("qk", [P, N_TILES, 512])
        v32 = p.sb("v32", [P, N_TILES, D])
        v = [tuple(p.sb(f"v{i}{j}", [P, N_TILES, D], F32R) for j in range(2)) for i in range(2)]
        qk_stats = p.sb("qk_stats", [P, N_TILES * 2, 6])
        qk_mv = p.sb("qk_mv", [P, N_TILES * 2, 2])
        neg_mean = p.sb("neg_mean", [P, N_TILES * 2])
        sq = p.sb("sq", [P, N_TILES, 512])
        sq4 = p.sb("sq4", [P, D])
        s2 = p.sb("s2", [P, N_TILES * 2])
        s4 = p.sb("s4", [P, N_TILES])
        qf = p.sb("qf", [P, N_TILES])
        half = p.sb("half", [P, N_TILES])
        q2n = p.sb("q2n", [P, N_TILES, D])
        q2T = tuple(p.sb(f"q2T{i}", [P, KC, S], F32R) for i in range(2))
        k2 = p.sb("k2", [P, N_TILES, D])
        k2s = tuple(p.sb(f"k2s{i}", [P, N_TILES, D], F32R) for i in range(2))
        k4 = p.sb("k4", [P, N_TILES, D])
        ones = p.sb("ones", [P, 2])
        knorm = p.sb("knorm", [P, KC])
        kv32 = p.sb("kv32", [P, KC, D])
        kv = tuple(p.sb(f"kv{i}", [P, KC, D], F32R) for i in range(2))
        yT = tuple(p.sb(f"yT{i}", [P, KC, S], F32R) for i in range(2))
        xb = [p.sb(f"xb{i}", [P, N_TILES, D]) for i in range(3)]
        x1 = [p.sb(f"x1_{i}", [P, N_TILES, D]) for i in range(2)]
        T = [p.bank(f"T{i}") for i in range(2)]
        QK = [p.bank(f"QK{i}") for i in range(2)]
        V, KV, NB, Y = p.bank("V"), p.bank("KV"), p.bank("NB"), p.bank("Y")
        free = {k: [] for k in ("T0", "T1", "QK0", "QK1", "V", "KV", "NB", "Y")}

        g = {n: p.counter(n) for n in ("xT_pe", "xT_hi", "xT_lo", "qkv_pe", "qk_ev", "v_ev", "v_hi", "v_lo", "st",
                                      "sqr", "small", "small_pool", "q2n", "q2T_pe", "q2T_hi", "q2T_lo", "k2",
                                      "k2_hi", "k2_lo", "k4", "kv_pe", "kn_pool", "kn", "kv_ev", "kv_hi", "kv_lo",
                                      "yT_pe", "yT_hi", "yT_lo", "y_pe", "xb", "x1")}
        stored = [p.dma_counter(f"x1_stored{i}") for i in range(2)]
        c0 = pool.do(lambda e: e.memset(ones[:], 1.0), counts=g["small_pool"])
        c1 = pool.do(lambda e: e.memset(half[:], 0.5), counts=g["small_pool"])
        prev = {}
        done = {}
        G = lambda k: prev.get(k, [])

        def transposed(src, dst, names, src_ready, dst_free):
            for c in range(KC):
                for t in range(N_TILES):
                    tp = pe.do(lambda e, c=c, t=t: e.transpose(T[c][:, t * P:(t + 1) * P],
                                                               src[:, t, c * P:(c + 1) * P], ident[:]),
                               after=[src_ready, const_ready] + free[f"T{c}"], counts=g[names + "_pe"])
                hi = act.do(lambda e, c=c: e.activation(dst[0][:, c, :], T[c][:], ACT.Copy),
                            after=[tp] + dst_free, counts=g[names + "_hi"])
                lo = dve.do(lambda e, c=c: e.tensor_tensor(dst[1][:, c, :], T[c][:], f32(dst[0][:, c, :]),
                                                           op=ALU.subtract),
                            after=[tp, hi] + dst_free, counts=g[names + "_lo"])
                free[f"T{c}"] = [lo]
            return tp, [hi, lo]

        def normalise(b):
            par, xi = b % 2, x_in[b % 2]
            loaded = load_x(b, G(f"x_in{par}"))
            n = norm.run(xi, xn, [loaded], G("xn"))
            e_xb = pool.do(lambda e: e.tensor_tensor(
                xb[b % 3][:], xi[:], bln[:].rearrange("p (a c) -> p a c", a=1).broadcast_to([P, N_TILES, D]),
                op=ALU.add), after=[loaded, bias_ready] + G(f"xb{b % 3}"), counts=g["xb"])
            prev[f"x_in{par}"] = [n, e_xb]
            done[b] = {"xn": n, "xb": e_xb}

        def transpose_x(b):
            tp, done[b]["xT"] = transposed(xn, xT[b % 2], "xT", done[b]["xn"], G(f"xT{b % 2}"))
            prev["xn"] = [tp]

        def project(b, u):
            par, dn = b % 2, done[b]
            xT_ready = dn["xT"]
            for t in (2 * u, 2 * u + 1):
                bank = QK[t % 2]
                for c in range(KC):
                    for i, (a, w) in enumerate(split3(xT[par], Wqkv)):
                        m = pe.do(lambda e, t=t, c=c, i=i, a=a, w=w, bank=bank: e.matmul(
                            bank[:], a[:, c, t * P:(t + 1) * P], w[:, c, 0:512],
                            start=(c == 0 and i == 0), stop=(c == KC - 1 and i == 2)),
                            after=xT_ready + [wqkv_ready] + free[f"QK{t % 2}"], counts=g["qkv_pe"])
                ev = dve.do(lambda e, t=t, bank=bank: e.tensor_tensor(qk[:, t, :], bank[:], bqkv[:, 0:512], op=ALU.add),
                            after=[m, bias_ready] + G("qk"), counts=g["qk_ev"])
                free[f"QK{t % 2}"] = [ev]
                for c in range(KC):
                    for i, (a, w) in enumerate(split3(xT[par], Wqkv)):
                        mv_ = pe.do(lambda e, t=t, c=c, i=i, a=a, w=w: e.matmul(
                            V[:, (t % 2) * D:(t % 2 + 1) * D], a[:, c, t * P:(t + 1) * P], w[:, c, 512:768],
                            start=(c == 0 and i == 0), stop=(c == KC - 1 and i == 2)),
                            after=(free["V"] if t % 2 == 0 else []), counts=g["qkv_pe"])
                if t % 2 == 1:
                    ve = dve.do(lambda e, t=t: e.tensor_tensor(
                        v32[:, t - 1:t + 1, :], V[:].rearrange("p (a c) -> p a c", a=2),
                        bqkv[:, 512:768].rearrange("p (a c) -> p a c", a=1).broadcast_to([P, 2, D]), op=ALU.add),
                        after=[mv_] + G("v32"), counts=g["v_ev"])
                    free["V"] = [ve]
                for j in range(2):
                    st = dve.do(lambda e, t=t, j=j: e.bn_stats(qk_stats[:, 2 * t + j, :], qk[:, t, j * D:(j + 1) * D]),
                                after=[ev] + G("stats"), counts=g["st"])
            ts = slice(2 * u, 2 * u + 2)
            vh = act.do(lambda e: e.activation(v[par][0][:, ts, :], v32[:, ts, :], ACT.Copy), after=[ve] + G(f"v{par}"),
                        counts=g["v_hi"])
            vl = pool.do(lambda e: e.tensor_tensor(v[par][1][:, ts, :], v32[:, ts, :], f32(v[par][0][:, ts, :]),
                                                   op=ALU.subtract),
                         after=[vh, ve] + G(f"v{par}"), counts=g["v_lo"])
            if u == 1:
                prev["v32"] = [vl]
            dn.update(qk=ev, st=st, v=[vh, vl])

        def square(b, u):
            dn = done[b]
            tiles, ts, js = (2 * u, 2 * u + 1), slice(2 * u, 2 * u + 2), slice(4 * u, 4 * u + 4)
            for j in range(4 * u, 4 * u + 4):
                ag = dve.do(lambda e, j=j: e.bn_aggr(qk_mv[:, j, :], qk_stats[:, j, :]),
                            after=[dn["st"]] + G("mv"), counts=g["st"])
            nm = dve.do(lambda e: e.tensor_scalar(neg_mean[:, js], qk_mv[:, js, 0], -1.0, None, ALU.mult),
                        after=[ag] + G("neg_mean"), counts=g["st"])
            if u == 1:
                prev["stats"] = [ag]
            s2a = dve.do(lambda e: e.tensor_scalar(s2[:, js], qk_mv[:, js, 1], float(D), EPS_SUM, ALU.mult, ALU.add),
                         after=[ag] + G("s2"), counts=g["small"])
            s2b = dve.do(lambda e: e.reciprocal(s2[:, js], s2[:, js]), after=[s2a], counts=g["small"])
            if u == 1:
                prev["mv"] = [s2a, nm]
            for t in tiles:
                for j in range(2):
                    a1 = act.do(lambda e, t=t, j=j: e.activation(
                        sq[:, t, j * D:(j + 1) * D], qk[:, t, j * D:(j + 1) * D], ACT.Square,
                        bias=neg_mean[:, 2 * t + j:2 * t + j + 1]), after=[nm, dn["qk"]] + G("sq"), counts=g["sqr"])
                    if j == 0:
                        a2 = act.do(lambda e, t=t: e.activation(sq4[:], sq[:, t, 0:D], ACT.Square,
                                                                accum_out=s4[:, t:t + 1]),
                                    after=[a1] + G("s4") + G("sq4"), counts=g["sqr"])
                        prev["sq4"] = [a2]
            if u == 1:
                prev["qk"] = prev["neg_mean"] = [a1]
            aq = s2[:, js].rearrange("p (t j) -> p t j", j=2)[:, :, 0]
            r = pool.do(lambda e: e.tensor_tensor(s4[:, ts], s4[:, ts], half[:, ts], op=ALU.pow), after=[a1, a2, c1],
                        counts=g["small_pool"])
            for t in tiles:
                kn_ = dve.do(lambda e, t=t: e.tensor_scalar(k2[:, t, :], sq[:, t, D:512], s2[:, 2 * t + 1:2 * t + 2],
                                                            None, ALU.mult),
                             after=[s2b, a1] + G("k2"), counts=g["k2"])
            f1 = dve.do(lambda e: e.tensor_tensor(s4[:, ts], s4[:, ts], aq, op=ALU.mult), after=[r, s2b], counts=g["small"])
            f2 = dve.do(lambda e: e.tensor_scalar(s4[:, ts], s4[:, ts], EPS_NORM, float(S) ** 0.5, ALU.max, ALU.mult),
                        after=[f1], counts=g["small"])
            f3 = dve.do(lambda e: e.reciprocal(s4[:, ts], s4[:, ts]), after=[f2], counts=g["small"])
            f4 = dve.do(lambda e: e.tensor_tensor(qf[:, ts], s4[:, ts], aq, op=ALU.mult), after=[f3] + G("qf"),
                        counts=g["small"])
            if u == 1:
                prev["s4"] = [f4]
            for t in tiles:
                qn = dve.do(lambda e, t=t: e.tensor_scalar(q2n[:, t, :], sq[:, t, 0:D], qf[:, t:t + 1], None, ALU.mult),
                            after=[f4, a1] + G("q2n"), counts=g["q2n"])
            if u == 1:
                prev["sq"] = [qn, kn_]
            if u == 1:
                prev["s2"] = [kn_, f4]
            if u == 1:
                prev["qf"] = [qn]
            k4e = pool.do(lambda e: e.tensor_tensor(k4[:, ts, :], k2[:, ts, :], k2[:, ts, :], op=ALU.mult),
                          after=[kn_] + G("k4"), counts=g["k4"])
            kh = act.do(lambda e: e.activation(k2s[0][:, ts, :], k2[:, ts, :], ACT.Copy), after=[kn_] + G("k2s"),
                        counts=g["k2_hi"])
            kl = dve.do(lambda e: e.tensor_tensor(k2s[1][:, ts, :], k2[:, ts, :], f32(k2s[0][:, ts, :]), op=ALU.subtract),
                        after=[kh, kn_] + G("k2s"), counts=g["k2_lo"])
            if u == 1:
                prev["k2"] = [kl, k4e]
            dn.update(q2n=qn, k2s=[kh, kl], k4=k4e)

        def state(b):
            par, dn = b % 2, done[b]
            tp, dn["q2T"] = transposed(q2n, q2T, "q2T", dn["q2n"], G("q2T"))
            prev["q2n"] = [tp]
            for c in range(KC):
                for t in range(N_TILES):
                    mn = pe.do(lambda e, t=t, c=c: e.matmul(NB[:, 2 * c:2 * c + 2], k4[:, t, c * P:(c + 1) * P],
                                                            ones[:], start=(t == 0), stop=(t == N_TILES - 1)),
                               after=[dn["k4"], c0] + free["NB"], counts=g["kv_pe"])
            prev["k4"] = [mn]
            for c in range(KC):
                for t in range(N_TILES):
                    for i, (a, w) in enumerate(split3(k2s, v[par])):
                        m = pe.do(lambda e, t=t, c=c, i=i, a=a, w=w: e.matmul(
                            KV[:, c * D:(c + 1) * D], a[:, t, c * P:(c + 1) * P], w[:, t, :],
                            start=(t == 0 and i == 0), stop=(t == N_TILES - 1 and i == 2)),
                            after=dn["k2s"] + dn["v"] + free["KV"], counts=g["kv_pe"])
            prev["k2s"] = prev[f"v{par}"] = [m]
            nb = NB[:, 0:4].rearrange("p (c j) -> p c j", j=2)[:, :, 0]
            n1 = dve.do(lambda e: e.tensor_copy(knorm[:], nb), after=[mn] + G("knorm"), counts=g["kn"])
            free["NB"] = [n1]
            n2 = pool.do(lambda e: e.tensor_tensor(knorm[:], knorm[:], half[:, 0:KC], op=ALU.pow), after=[n1],
                         counts=g["kn_pool"])
            n3 = dve.do(lambda e: e.tensor_scalar(knorm[:], knorm[:], EPS_NORM, None, ALU.max), after=[n2],
                        counts=g["kn"])
            n4 = dve.do(lambda e: e.reciprocal(knorm[:], knorm[:]), after=[n3], counts=g["kn"])
            for c in range(KC):
                k5 = dve.do(lambda e, c=c: e.tensor_scalar(kv32[:, c, :], KV[:, c * D:(c + 1) * D], knorm[:, c:c + 1],
                                                           None, ALU.mult),
                            after=[n4, m] + G("kv32"), counts=g["kv_ev"])
            prev["knorm"] = [k5]
            free["KV"] = [k5]
            k6 = act.do(lambda e: e.activation(kv[0][:], kv32[:], ACT.Copy), after=[k5] + G("kv"),
                        counts=g["kv_hi"])
            k7 = dve.do(lambda e: e.tensor_tensor(kv[1][:], kv32[:], f32(kv[0][:]), op=ALU.subtract),
                        after=[k6, k5] + G("kv"), counts=g["kv_lo"])
            prev["kv32"] = [k7]
            dn["kv"] = [k6, k7]

        def attend(b):
            par, dn = b % 2, done[b]
            for m_ in range(KC):
                terms = [(w, a, c, 512) for c in range(KC) for w, a in split3(Wqkv, xT[par])]
                terms += [(w, a, c, 0) for c in range(KC) for w, a in split3(kv, q2T)]
                for i, (w, a, c, off) in enumerate(terms):
                    yp = pe.do(lambda e, m_=m_, i=i, w=w, a=a, c=c, off=off, n=len(terms): e.matmul(
                        QK[m_][:], w[:, c, off + m_ * P:off + (m_ + 1) * P], a[:, c, :],
                        start=(i == 0), stop=(i == n - 1)),
                        after=(free[f"QK{m_}"] if off else dn["q2T"] + dn["kv"]), counts=g["yT_pe"])
                hi = act.do(lambda e, m_=m_: e.activation(yT[0][:, m_, :], QK[m_][:], ACT.Identity,
                                                          bias=bvT[:, m_:m_ + 1]),
                            after=[yp, bias_ready] + G("yT"), counts=g["yT_hi"])
                lo = dve.do(lambda e, m_=m_: e.scalar_tensor_tensor(
                    yT[1][:, m_, :], QK[m_][:], bvT[:, m_:m_ + 1], f32(yT[0][:, m_, :]), op0=ALU.add,
                    op1=ALU.subtract), after=[yp, hi] + G("yT"), counts=g["yT_lo"])
                free[f"QK{m_}"] = [lo]
            prev[f"xT{par}"] = prev["q2T"] = prev["kv"] = [yp]
            dn["yT"] = [hi, lo]

        def output(b):
            par, dn, o = b % 2, done[b], x1[b % 2]
            for u, (name, bank) in enumerate((("Y", Y), ("V", V))):
                for t in (2 * u, 2 * u + 1):
                    for c in range(KC):
                        for i, (a, w) in enumerate(split3(yT, Wln)):
                            m = pe.do(lambda e, t=t, c=c, i=i, a=a, w=w, bank=bank: e.matmul(
                                bank[:, (t % 2) * D:(t % 2 + 1) * D], a[:, c, t * P:(t + 1) * P], w[:, c, :],
                                start=(c == 0 and i == 0), stop=(c == KC - 1 and i == 2)),
                                after=dn["yT"] + [wln_ready] + (free[name] if t % 2 == 0 else []), counts=g["y_pe"])
                ye = dve.do(lambda e, u=u, bank=bank: e.tensor_tensor(
                    o[:, 2 * u:2 * u + 2, :], bank[:].rearrange("p (a c) -> p a c", a=2), xb[b % 3][:, 2 * u:2 * u + 2, :],
                    op=ALU.add), after=[m, dn["xb"]] + G(f"x1{par}"), counts=g["x1"])
                free[name] = [ye]
            prev["yT"] = [m]
            prev[f"xb{b % 3}"] = [ye]
            prev[f"x1{par}"] = [sp.do(lambda e: e.dma_start(x1_dram[b], o[:]), after=[ye], counts=stored[par])]

        normalise(0)
        transpose_x(0)
        for b in range(B + 1):
            if b < B:
                project(b, 0)
            if b >= 1:
                state(b - 1)
            if b < B:
                project(b, 1)
            if b + 1 < B:
                normalise(b + 1)
            if b < B:
                square(b, 0)
            if b >= 1:
                attend(b - 1)
            if b + 1 < B:
                transpose_x(b + 1)
            if b < B:
                square(b, 1)
            if b >= 1:
                output(b - 1)
        sp.do(lambda e: e.nop(), after=G("x10") + G("x11"))
        p.run()


SCORE_AT = {3: 0, 2: 512, 0: 896, 1: 1024}
PROB_T_AT = {0: 0, 1: 512, 3: 896, 2: 1024}
TRIANGLE = 1280
V_TILE_AT = (2, 4, 6, 7)
BANK_TILES = ((3,), (2, 0), (1,))
BANK_COLS = ((0, 512), (512, 1024), (1024, TRIANGLE))


def cross_attention(nc, d, x1_dram, x2_dram, rows_dram, routing):
    with ExitStack() as stack:
        p = Part(nc, stack, "xa")
        pe, act, dve, pool, sp = p.pe, p.act, p.dve, p.pool, p.sp
        ident, const_ready, _ = constants(p)
        cols = lambda n: p.sb(n, [P, N_TILES, D])
        xn = cols("xn")
        stage = {"tile": None, "dma": p.dma_counter("w_in"), "hi": p.counter("w_hi"),
                 "split": p.counter("w_split"), "free": []}
        ctx32 = p.sb("ctx32", [P, KC, S])
        stage_a = dict(stage, tile=ctx32[:].rearrange("p a b -> p (a b)"))
        W = {}
        w_ready = {}
        for name in ("WqT", "WkT", "WvT"):
            hi = p.sb(name + "_hi", [P, KC, INNER], F32R)
            lo = p.sb(name + "_lo", [P, KC, INNER], F32R)
            W[name] = (hi, lo)
            for c in range(KC):
                view = stage_a["tile"]
                got = sp.do(lambda e, name=name, c=c: e.dma_start(view[:, 0:INNER], d[name][c * P:(c + 1) * P, :]),
                            after=stage["free"], counts=stage["dma"])
                if name == "WqT":
                    got = dve.do(lambda e: e.tensor_scalar(view[:, 0:INNER], view[:, 0:INNER], HD ** -0.5, None,
                                                           ALU.mult), after=[got], counts=stage["split"])
                a = act.do(lambda e, hi=hi, c=c: e.activation(hi[:, c, :], view[:, 0:INNER], ACT.Copy), after=[got],
                           counts=stage["hi"])
                s = dve.do(lambda e, hi=hi, lo=lo, c=c: e.tensor_tensor(lo[:, c, :], view[:, 0:INNER],
                                                                        f32(hi[:, c, :]), op=ALU.subtract),
                           after=[got, a], counts=stage["split"])
                stage["free"] = [s]
            w_ready[name] = s
        stage_last = s
        WoT = p.sb("WoT", [P, PAIRS, D])
        bqT, bkT = p.sb("bqT", [P, PAIRS]), p.sb("bkT", [P, PAIRS])
        bv, bo = p.sb("bv", [P, INNER]), p.sb("bo", [P, D])
        rw, rb = p.sb("rw", [P, KC, E]), p.sb("rb", [P, E])
        bias_in = p.dma_counter("bias_in")
        row = lambda v, n: v.rearrange("(a n) -> a n", a=1).broadcast_to([P, n])
        sp.do(lambda e: e.dma_start(WoT[:], d['WoT'].rearrange("(k p) n -> p k n", p=P)), counts=bias_in)
        sp.do(lambda e: e.dma_start(bqT[:], d['bq'].rearrange("(k p) -> p k", p=P), allow_slow_non_contiguous=True),
              counts=bias_in)
        sp.do(lambda e: e.dma_start(bkT[:], d['bk'].rearrange("(k p) -> p k", p=P), allow_slow_non_contiguous=True),
              counts=bias_in)
        sp.do(lambda e: e.dma_start(bv[:], row(d['bv'], INNER)), counts=bias_in)
        sp.do(lambda e: e.dma_start(bo[:], row(d['bo'], D)), counts=bias_in)
        sp.do(lambda e: e.dma_start(rw[:], d['router_w'].rearrange("(k p) n -> p k n", p=P)), counts=bias_in)
        bias_in_all = sp.do(lambda e: e.dma_start(rb[:], row(d['router_b'], E)), counts=bias_in)
        bias_ready = dve.do(lambda e: e.tensor_scalar(bqT[:], bqT[:], HD ** -0.5, None, ALU.mult),
                            after=[bias_in_all], counts=p.counter("bias"))
        const_p = p.counter("const_pool")

        identb, maskb = p.sb("identb", [P, P], BF16), p.sb("maskb", [P, P], BF16)
        tri, onesb = p.sb("tri", [P, P], BF16), p.sb("onesb", [P, P], BF16)
        for tile, fill in ((identb, 0.0), (maskb, 0.0), (tri, 1.0), (onesb, 1.0)):
            m0 = pool.do(lambda e, tile=tile, fill=fill: e.memset(tile[:], fill), counts=const_p)
        pool.do(lambda e: e.affine_select(out=identb[:], in_=identb[:], compare_op=ALU.not_equal, fill=1.0, base=0,
                                          pattern=[[-1, P]], channel_multiplier=1), after=[m0], counts=const_p)
        pool.do(lambda e: e.affine_select(out=maskb[:], in_=maskb[:], compare_op=ALU.is_ge, fill=NEG, base=0,
                                          pattern=[[-1, P]], channel_multiplier=1), after=[m0], counts=const_p)
        tri_ready = pool.do(lambda e: e.affine_select(out=tri[:], in_=tri[:], compare_op=ALU.is_ge, fill=0.0, base=-1,
                                                      pattern=[[1, P]], channel_multiplier=-1), after=[m0],
                            counts=const_p)
        ebase = p.sb("ebase", [P, E])
        for e_ in range(E):
            m1 = pool.do(lambda e, e_=e_: e.memset(ebase[:, e_:e_ + 1], float(e_ * REGION + 1)), counts=const_p)
        probs = p.sb("probs", [P, N_TILES, E + 4])
        sentinel = p.sb("sentinel", [P, N_TILES, 4])
        for i in range(4):
            pool.do(lambda e, i=i: e.memset(probs[:, :, E + i:E + i + 1], float(-1 - i)), counts=const_p)
            m2 = pool.do(lambda e, i=i: e.memset(sentinel[:, :, i:i + 1], float(-1 - i)), counts=const_p)
        count = routing["count"]
        consts = pool.do(lambda e: e.memset(count[:], 0.0), counts=const_p)

        ln2, ln3 = Norm(p, "ln2"), Norm(p, "ln3")
        x1 = [cols(f"x1_{i}") for i in range(2)]
        xT = [tuple(p.sb(f"xT{i}{j}", [P, KC, S], F32R) for j in range(2)) for i in range(2)]
        cT = [tuple(p.sb(f"cT{i}{j}", [P, KC, S], F32R) for j in range(2)) for i in range(2)]
        qT = [p.sb(f"qT{i}", [P, S]) for i in range(2)]
        kT = [[p.sb(f"kT{i}{j}", [P, S]) for j in range(2)] for i in range(2)]
        v = [p.sb(f"v{i}", [P, N_TILES, INNER // 2]) for i in range(2)]
        prob = [p.sb(f"prob{i}", [P, TRIANGLE]) for i in range(2)]
        probT = [p.sb(f"probT{i}", [P, TRIANGLE]) for i in range(2)]
        nmax = [p.sb(f"nmax{i}", [P, N_TILES]) for i in range(2)]
        sums = [p.sb(f"sums{i}", [P, N_TILES]) for i in range(2)]
        oT = p.sb("oT", [P, PAIRS, S])
        x2 = cols("x2")
        xn3 = cols("xn3")
        xn3T = p.sb("xn3T", [P, KC, S])
        small = lambda n, k=E: p.sb(n, [P, N_TILES, k])
        lg, repl, mask, key = small("lg"), small("repl", E + 4), small("mask"), small("key")
        maskb16 = p.sb("maskb16", [P, N_TILES, E], BF16)
        top8, key8 = small("top8", 8), small("key8", 8)
        red = p.sb("red", [P, N_TILES])
        rows_i = [p.sb(f"rows{i}", [P, N_TILES, TOPK], I32) for i in range(2)]

        SB = [p.bank(f"S{i}") for i in range(3)]
        TB = [p.bank(f"T{i}") for i in range(3)]
        OB, PJ = p.bank("O"), p.bank("PJ")
        free = {"S0": [], "S1": [], "S2": [], "T0": [], "T1": [], "T2": [], "O": [], "PJ": []}

        names = ("zero", "x_hi", "x_lo", "c_hi", "c_lo", "pj_pe", "q_ev", "k_ev_a", "k_ev_b", "v_ev", "s_pe", "max",
                 "exp", "rcp", "norm", "t_pe", "t_act", "t_dve", "pv_pe", "o_ev", "xb", "x2", "xn3T",
                 "r_dve", "r_act", "r_rows")
        g = {n: p.counter(n) for n in names}
        x1_in = [p.dma_counter(f"x1_in{i}") for i in range(2)]
        ctx_in, x2_out = p.dma_counter("ctx_in"), p.dma_counter("x2_out")
        scattered = p.dma_counter("scattered")

        for i in range(2):
            for j in range(2):
                z = dve.do(lambda e, i=i, j=j: e.memset(kT[i][j][64 * (1 - j):64 * (1 - j) + 64, :], 0.0),
                           counts=g["zero"])
        kzero = z
        last = {}
        G = lambda k: last.get(k, [])

        def load(b):
            last[f"x1_loaded{b}"] = [sp.do(lambda e: e.dma_start(x1[b % 2][:], x1_dram[b]),
                                           after=G(f"x1_free{b % 2}"), counts=x1_in[b % 2])]
            last["ctx_loaded"] = [sp.do(lambda e: e.dma_start(ctx32[:], d['ctxT'][b].rearrange("(k p) s -> p k s", p=P)),
                                        after=G("ctx32_free") + [stage_last], counts=ctx_in)]

        def split_ctx(b):
            hi, lo = cT[b % 2]
            a = act.do(lambda e: e.activation(hi[:], ctx32[:], ACT.Copy),
                       after=G("ctx_loaded") + G(f"cT_free{b % 2}"), counts=g["c_hi"])
            l = pool.do(lambda e: e.tensor_tensor(lo[:], ctx32[:], f32(hi[:]), op=ALU.subtract),
                        after=[a] + G("ctx_loaded") + G(f"cT_free{b % 2}"), counts=g["c_lo"])
            last["ctx32_free"] = [l]
            last[f"cT_ready{b}"] = [a, l]

        def norm2(b):
            last["xn_ready"] = [ln2.run(x1[b % 2], xn, G(f"x1_loaded{b}"), G("xn_free"))]
            last[f"xb{b}"] = [pool.do(lambda e: e.tensor_tensor(
                x1[b % 2][:], x1[b % 2][:], bo[:].rearrange("p (a c) -> p a c", a=1).broadcast_to([P, N_TILES, D]),
                op=ALU.add), after=G("xn_ready") + [bias_ready], counts=g["xb"])]

        def transpose_x(b, c):
            for t in range(N_TILES):
                m = pe.do(lambda e, t=t: e.transpose(PJ[:, t * P:(t + 1) * P], xn[:, t, c * P:(c + 1) * P], ident[:]),
                          after=G("xn_ready") + free["PJ"] + [const_ready], counts=g["pj_pe"])
            hi, lo = xT[b % 2]
            a = act.do(lambda e: e.activation(hi[:, c, :], PJ[:], ACT.Copy), after=[m] + G(f"xT_free{b % 2}"),
                       counts=g["x_hi"])
            l = dve.do(lambda e: e.tensor_tensor(lo[:, c, :], PJ[:], f32(hi[:, c, :]), op=ALU.subtract),
                       after=[m, a] + G(f"xT_free{b % 2}"), counts=g["x_lo"])
            free["PJ"] = [l]
            last["xn_free"] = [m]
            last[f"xT_ready{b}"] = G(f"xT_ready{b}") + [a, l]

        def project(src, w, col, ready):
            for c in range(KC):
                for i, (ww, xx) in enumerate(split3(W[w], src)):
                    m = pe.do(lambda e, c=c, i=i, ww=ww, xx=xx: e.matmul(
                        PJ[:], ww[:, c, col:col + P], xx[:, c, :], start=(c == 0 and i == 0),
                        stop=(c == KC - 1 and i == 2)), after=ready + [w_ready[w]] + free["PJ"], counts=g["pj_pe"])
            return m

        def project_q(n):
            b, pr = divmod(n, PAIRS)
            m = project(xT[b % 2], "WqT", pr * P, G(f"xT_ready{b}"))
            q = act.do(lambda e: e.activation(qT[n % 2][:], PJ[:], ACT.Identity, bias=bqT[:, pr:pr + 1]),
                       after=[m, bias_ready] + G(f"qT_free{n % 2}"), counts=g["q_ev"])
            free["PJ"] = [q]
            last[f"xT_free{b % 2}"] = [m]
            last[f"q_ready{n}"] = [q]

        def project_k(n):
            b, pr = divmod(n, PAIRS)
            m = project(cT[b % 2], "WkT", pr * P, G(f"cT_ready{b}"))
            a = act.do(lambda e: e.activation(kT[n % 2][0][0:64, :], PJ[0:64, :], ACT.Identity,
                                              bias=bkT[0:64, pr:pr + 1]),
                       after=[m, bias_ready] + G(f"kT_free{n % 2}"), counts=g["k_ev_a"])
            v_ = dve.do(lambda e: e.tensor_scalar(kT[n % 2][1][64:128, :], PJ[64:128, :], bkT[64:128, pr:pr + 1],
                                                  None, ALU.add),
                        after=[m] + G(f"kT_free{n % 2}"), counts=g["k_ev_b"])
            free["PJ"] = [a, v_]
            last[f"cT_free{b % 2}"] = [m]
            last[f"k_ready{n}"] = [a, v_, kzero]

        def project_v(n, t):
            b, half = divmod(n, 2)
            for c in range(KC):
                for i, (xx, ww) in enumerate(split3(cT[b % 2], W["WvT"])):
                    m = pe.do(lambda e, c=c, i=i, ww=ww, xx=xx: e.matmul(
                        PJ[:], xx[:, c, t * P:(t + 1) * P], ww[:, c, half * 512:half * 512 + 512],
                        start=(c == 0 and i == 0), stop=(c == KC - 1 and i == 2)),
                        after=G(f"cT_ready{b}") + [w_ready["WvT"]] + free["PJ"], counts=g["pj_pe"])
            v_ = dve.do(lambda e: e.tensor_tensor(v[n % 2][:, t, :], PJ[:], bv[:, half * 512:half * 512 + 512],
                                                  op=ALU.add),
                        after=[m, bias_ready] + G(f"v_free{n % 2}"), counts=g["v_ev"])
            free["PJ"] = [v_]
            last[f"cT_free{b % 2}"] = [m]
            last[f"v_ready{n}"] = [v_]

        def scores(hh):
            n, odd = divmod(hh, 2)
            for k, tiles in enumerate(BANK_TILES):
                for i in tiles:
                    at, width = SCORE_AT[i] - BANK_COLS[k][0], (i + 1) * P
                    pe.do(lambda e, k=k, i=i, at=at, width=width: e.matmul(
                        SB[k][:, at:at + width], qT[n % 2][:, i * P:(i + 1) * P], kT[n % 2][odd][:, 0:width],
                        start=True, stop=False), after=G(f"q_ready{n}") + G(f"k_ready{n}") + free[f"S{k}"])
                    m = pe.do(lambda e, k=k, at=at, width=width: e.matmul(
                        SB[k][:, at + width - P:at + width], identb[:], maskb[:], start=False, stop=True),
                        after=[tri_ready], counts=g["s_pe"])
                last[f"S{k}"] = [m]
            last[f"qT_free{n % 2}"] = last[f"kT_free{n % 2}"] = [m]

        def row_max(hh):
            for k, tiles in enumerate(BANK_TILES):
                for i in tiles:
                    at, width = SCORE_AT[i] - BANK_COLS[k][0], (i + 1) * P
                    r = dve.do(lambda e, k=k, i=i, at=at, width=width: e.tensor_reduce(
                        nmax[hh % 2][:, i:i + 1], SB[k][:, at:at + width], AX.X, ALU.max, negate=True),
                        after=G(f"S{k}") + G(f"nmax_free{hh % 2}"), counts=g["max"])
                last[f"max{k}"] = [r]

        def exponent(hh):
            for k, tiles in enumerate(BANK_TILES):
                for i in tiles:
                    at, width = SCORE_AT[i] - BANK_COLS[k][0], (i + 1) * P
                    a = act.do(lambda e, k=k, i=i, at=at, width=width: e.activation(
                        prob[hh % 2][:, SCORE_AT[i]:SCORE_AT[i] + width], SB[k][:, at:at + width], ACT.Exp,
                        bias=nmax[hh % 2][:, i:i + 1], accum_out=sums[hh % 2][:, i:i + 1]),
                        after=G(f"S{k}") + G(f"max{k}") + G(f"prob_free{hh % 2}") + G(f"sums_free{hh % 2}"),
                        counts=g["exp"])
                free[f"S{k}"] = [a]
            last[f"exp{hh}"] = [a]
            last[f"nmax_free{hh % 2}"] = [a]

        def normalise(hh):
            r = dve.do(lambda e: e.reciprocal(sums[hh % 2][:], sums[hh % 2][:]), after=G(f"exp{hh}"), counts=g["rcp"])
            for i in range(N_TILES):
                at, width = SCORE_AT[i], (i + 1) * P
                s = dve.do(lambda e, i=i, at=at, width=width: e.tensor_scalar(
                    prob[hh % 2][:, at:at + width], prob[hh % 2][:, at:at + width], sums[hh % 2][:, i:i + 1], None,
                    ALU.mult), after=[r], counts=g["norm"])
            last[f"norm{hh}"] = [s]
            last[f"sums_free{hh % 2}"] = [s]

        def transpose_probs(hh):
            for k, tiles in enumerate(((0,), (1, 3), (2,))):
                for j in tiles:
                    for i in range(j, N_TILES):
                        at = PROB_T_AT[j] - BANK_COLS[k][0] + (i - j) * P
                        m = pe.do(lambda e, k=k, i=i, j=j, at=at: e.transpose(
                            TB[k][:, at:at + P], prob[hh % 2][:, SCORE_AT[i] + j * P:SCORE_AT[i] + (j + 1) * P],
                            ident[:]), after=G(f"norm{hh}") + free[f"T{k}"], counts=g["t_pe"])
                lo_, hi_ = BANK_COLS[k]
                if k == 1:
                    ev = dve.do(lambda e, k=k, lo_=lo_, hi_=hi_: e.tensor_copy(probT[hh % 2][:, lo_:hi_],
                                                                              TB[k][:, 0:hi_ - lo_]),
                                after=[m] + G(f"probT_free{hh % 2}"), counts=g["t_dve"])
                else:
                    ev = act.do(lambda e, k=k, lo_=lo_, hi_=hi_: e.activation(probT[hh % 2][:, lo_:hi_],
                                                                             TB[k][:, 0:hi_ - lo_], ACT.Copy),
                                after=[m] + G(f"probT_free{hh % 2}"), counts=g["t_act"])
                free[f"T{k}"] = [ev]
                last[f"probT{hh}"] = G(f"probT{hh}") + [ev]
            last[f"prob_free{hh % 2}"] = [m]

        def weigh_values(hh):
            b, h = divmod(hh, H)
            n, col, lo_ = hh // 8, (h % 8) // 2 * P, 64 * (h % 2)
            for j in range(N_TILES):
                m = pe.do(lambda e, j=j: e.matmul(
                    OB[:, j * P:512], v[n % 2][:, j, col:col + P],
                    probT[hh % 2][:, PROB_T_AT[j]:PROB_T_AT[j] + (N_TILES - j) * P],
                    start=(j == 0), stop=(j == N_TILES - 1)),
                    after=G(f"probT{hh}") + G(f"v_ready{n}") + free["O"], counts=g["pv_pe"])
            a = act.do(lambda e: e.activation(oT[lo_:lo_ + 64, h // 2, :], OB[lo_:lo_ + 64, :], ACT.Copy),
                       after=[m] + G("oT_free"), counts=g["o_ev"])
            free["O"] = [a]
            last[f"probT_free{hh % 2}"] = last[f"v_free{n % 2}"] = [m]
            last[f"oT_ready{b}"] = [a]

        def output(b, u):
            for t in (2 * u, 2 * u + 1):
                for pr in range(PAIRS):
                    m = pe.do(lambda e, t=t, pr=pr: e.matmul(
                        PJ[:, (t % 2) * D:(t % 2 + 1) * D], oT[:, pr, t * P:(t + 1) * P], WoT[:, pr, :],
                        start=(pr == 0), stop=(pr == PAIRS - 1)),
                        after=G(f"oT_ready{b}") + [bias_ready] + free["PJ"], counts=g["pj_pe"])
            o = dve.do(lambda e: e.tensor_tensor(x2[:, 2 * u:2 * u + 2, :], PJ[:].rearrange("p (a c) -> p a c", a=2),
                                                 x1[b % 2][:, 2 * u:2 * u + 2, :], op=ALU.add),
                       after=[m] + G(f"xb{b}") + G("x2_free"), counts=g["x2"])
            free["PJ"] = [o]
            last["oT_free"] = [m]
            last[f"x1_free{b % 2}"] = [o]
            last["x2_ready"] = [o]

        def norm3(b):
            s = sp.do(lambda e: e.dma_start(x2_dram[b], x2[:]), after=G("x2_ready"), counts=x2_out)
            last["xn3_ready"] = [ln3.run(x2, xn3, G("x2_ready"), G("xn3_free"))]
            last["x2_free"] = [s] + G("xn3_ready")

        def transpose_x3(b, c):
            for t in range(N_TILES):
                m = pe.do(lambda e, t=t: e.transpose(PJ[:, t * P:(t + 1) * P], xn3[:, t, c * P:(c + 1) * P], ident[:]),
                          after=G("xn3_ready") + free["PJ"], counts=g["pj_pe"])
            a = act.do(lambda e: e.activation(xn3T[:, c, :], PJ[:], ACT.Copy), after=[m] + G("xn3T_free"),
                       counts=g["xn3T"])
            free["PJ"] = [a]
            last["xn3T_ready"] = [a]

        bc = lambda ap: ap.rearrange("p (t a) -> p t a", a=1).broadcast_to([P, N_TILES, E])
        be = lambda ap: ap.rearrange("p (a e) -> p a e", a=1).broadcast_to([P, N_TILES, E])

        def route(b):
            for t in range(N_TILES):
                for c in range(KC):
                    m = pe.do(lambda e, t=t, c=c: e.matmul(PJ[:, t * E:(t + 1) * E], xn3T[:, c, t * P:(t + 1) * P],
                                                           rw[:, c, :], start=(c == 0), stop=(c == KC - 1)),
                              after=G("xn3T_ready") + free["PJ"], counts=g["pj_pe"])
            last["xn3T_free"] = [m]
            R = lambda make, after: dve.do(make, after=after, counts=g["r_dve"])
            bt = slice(b * N_TILES, (b + 1) * N_TILES)
            weight, pos, chosen = routing["weight"], routing["pos"], routing["chosen"]
            pr = probs[:, :, 0:E]
            r = R(lambda e: e.tensor_tensor(lg[:], PJ[:, 0:N_TILES * E].rearrange("p (t e) -> p t e", t=N_TILES),
                                            be(rb[:]), op=ALU.add), [m, bias_ready])
            free["PJ"] = [r]
            r = R(lambda e: e.tensor_reduce(red[:], lg[:], AX.X, ALU.max), [r])
            r = R(lambda e: e.tensor_tensor(lg[:], lg[:], bc(red[:]), op=ALU.subtract), [r])
            x = act.do(lambda e: e.activation(pr, lg[:], ACT.Exp), after=[r, consts] + G("probs_free"),
                       counts=g["r_act"])
            r = R(lambda e: e.tensor_reduce(red[:], pr, AX.X, ALU.add), [x, r])
            r = R(lambda e: e.reciprocal(red[:], red[:]), [r])
            r = R(lambda e: e.tensor_tensor(pr, pr, bc(red[:]), op=ALU.mult), [r])
            for t in range(N_TILES):
                r2 = R(lambda e, t=t: e.max(top8[:, t, :], probs[:, t, 0:E]), [r])
            r = R(lambda e: e.tensor_copy(top8[:, :, TOPK:8], sentinel[:]), [r2])
            for t in range(N_TILES):
                r2 = R(lambda e, t=t: e.match_replace(repl[:, t, :], top8[:, t, :], probs[:, t, :], -8.0), [r])
            r = R(lambda e: e.tensor_scalar(mask[:], repl[:, :, 0:E], -8.0, None, ALU.is_equal), [r2])
            mb = R(lambda e: e.tensor_copy(maskb16[:], mask[:]), [r])
            r = R(lambda e: e.tensor_tensor(pr, pr, mask[:], op=ALU.mult), [mb])
            r = R(lambda e: e.tensor_reduce(red[:], pr, AX.X, ALU.add), [r])
            r = R(lambda e: e.reciprocal(red[:], red[:]), [r])
            r = R(lambda e: e.tensor_tensor(weight[:, bt, :], pr, bc(red[:]), op=ALU.mult), [r])
            r = R(lambda e: e.tensor_copy(chosen[:, bt, :], mask[:]), [r])
            last["probs_free"] = [r]
            last["mask_ready"] = [r]

        def place(b):
            bt = slice(b * N_TILES, (b + 1) * N_TILES)
            pos = routing["pos"]
            for t in range(N_TILES + 1):
                terms = [(tri, t)] if t < N_TILES else []
                terms += [(onesb, s_) for s_ in range(min(t, N_TILES))]
                for i, (w, s_) in enumerate(terms):
                    m = pe.do(lambda e, t=t, i=i, w=w, s_=s_, n=len(terms): e.matmul(
                        PJ[:, t * E:(t + 1) * E], w[:], maskb16[:, s_, :], start=(i == 0), stop=(i == n - 1)),
                        after=G("mask_ready") + [consts] + free["PJ"], counts=g["pj_pe"])
            R = lambda make, after: dve.do(make, after=after, counts=g["r_dve"])
            r = R(lambda e: e.tensor_tensor(pos[:, bt, :], PJ[:, 0:N_TILES * E].rearrange("p (t e) -> p t e", t=N_TILES),
                                            be(count[:]), op=ALU.add), [m, consts] + G("count_ready"))
            c = R(lambda e: e.tensor_tensor(count[:], PJ[:, N_TILES * E:(N_TILES + 1) * E], count[:], op=ALU.add), [r])
            last["count_ready"] = [c]
            free["PJ"] = [c]
            r = R(lambda e: e.tensor_tensor(key[:], pos[:, bt, :], be(ebase[:]), op=ALU.add), [r])
            r = R(lambda e: e.tensor_tensor(key[:], key[:], mask[:], op=ALU.mult), [r])
            for t in range(N_TILES):
                r2 = R(lambda e, t=t: e.max(key8[:, t, :], key[:, t, :]), [r])
            w = dve.do(lambda e: e.tensor_scalar(rows_i[b % 2][:], key8[:, :, 0:TOPK], -1.0, None, ALU.add),
                       after=[r2] + G(f"rows_free{b % 2}"), counts=g["r_rows"])
            for t in range(N_TILES):
                for k in range(TOPK):
                    s = pool.do(lambda e, t=t, k=k: e.indirect_dma_start(
                        rows_dram, bass.IndirectOffsetOnAxis(rows_i[b % 2][:, t, k:k + 1], 0), xn3[:, t, :], None),
                        after=[w] + G("xn3_ready"), counts=scattered)
            last["xn3_free"] = last[f"rows_free{b % 2}"] = [s]

        def tasks(b, h):
            nxt, out = b * PAIRS + h // 2 + 1, b - 1
            first, second, third = [], [], []
            if nxt < B * PAIRS:
                first.append(lambda: (project_k if h % 2 else project_q)(nxt))
            half = 2 * b + 1 + h // 8
            if h % 8 in V_TILE_AT and half < 2 * B:
                second.append(lambda: project_v(half, V_TILE_AT.index(h % 8)))
            if b + 1 < B:
                if h == 4:
                    second.append(lambda: load(b + 1))
                if h == 6:
                    second.append(lambda: split_ctx(b + 1))
                if h == 9:
                    second.append(lambda: norm2(b + 1))
                if h in (11, 13):
                    third.append(lambda: transpose_x(b + 1, (h - 11) // 2))
            if out >= 0:
                if h == 2:
                    third.append(lambda: output(out, 0))
                    third.append(lambda: output(out, 1))
                    third.append(lambda: norm3(out))
                if h in (5, 6):
                    third.append(lambda: transpose_x3(out, h - 5))
                if h == 7:
                    third.append(lambda: route(out))
                if h == 9:
                    third.append(lambda: place(out))
            return first, second, third

        load(0)
        split_ctx(0)
        norm2(0)
        transpose_x(0, 0)
        transpose_x(0, 1)
        project_q(0)
        project_k(0)
        for t in range(N_TILES):
            project_v(0, t)
        for hh in range(B * H + 2):
            first, second, third = tasks(*divmod(hh, H)) if hh < B * H else ([], [], [])
            for f in first:
                f()
            if hh < B * H:
                scores(hh)
            if 0 <= hh - 1 < B * H:
                normalise(hh - 1)
            if hh < B * H:
                row_max(hh)
                exponent(hh)
            for f in second:
                f()
            if 0 <= hh - 1 < B * H:
                transpose_probs(hh - 1)
            for f in third:
                f()
            if hh - 2 >= 0:
                weigh_values(hh - 2)
        output(B - 1, 0)
        output(B - 1, 1)
        norm3(B - 1)
        transpose_x3(B - 1, 0)
        transpose_x3(B - 1, 1)
        route(B - 1)
        place(B - 1)
        sp.do(lambda e: e.nop(), after=G("x2_free"))
        pool.do(lambda e: e.nop(), after=G("xn3_free"))
        p.run()


def experts(nc, d, rows_dram, y_dram, routing):
    with ExitStack() as stack:
        p = Part(nc, stack, "ex")
        pe, act, dve, pool, sp = p.pe, p.act, p.dve, p.pool, p.sp
        ident, const_ready, _ = constants(p)
        NX = 3
        W1 = p.sb("w1", [P, E * KC * FF])
        W2 = p.sb("w2", [P, E * FC * D])
        WE = KC * FF
        b1T = p.sb("b1T", [P, E * FC])
        x_in = [p.sb(f"x{i}", [P, RT, D]) for i in range(NX)]
        xT = [tuple(p.sb(f"xT{i}{j}", [P, KC, ROWS], F32R) for j in range(2)) for i in range(2)]
        w1 = [tuple(p.sb(f"w1_{i}{j}", [P, KC, FF], F32R) for j in range(2)) for i in range(2)]
        w2 = [tuple(p.sb(f"w2_{i}{j}", [P, FC, D], F32R) for j in range(2)) for i in range(2)]
        b1 = [p.sb(f"b1_{i}", [P, FC]) for i in range(2)]
        h32 = p.sb("h32", [P, FC, ROWS])
        hT = [tuple(p.sb(f"hT{i}{j}", [P, FC, ROWS], F32R) for j in range(2)) for i in range(2)]
        y = [p.sb(f"y{i}", [P, RT, D]) for i in range(2)]
        XB = [p.bank(f"X{i}") for i in range(2)]
        HB = [p.bank(f"H{i}") for i in range(4)]
        YB = [p.bank(f"Y{i}") for i in range(2)]

        w_in = [p.dma_counter(f"w_in{e_}") for e_ in range(E)]
        b1_in = p.dma_counter("b1_in")
        b1_ready = sp.do(lambda e: e.dma_start(b1T[:], d['b1T']), counts=b1_in)
        w_ready = []
        for e_ in range(E):
            sp.do(lambda e, e_=e_: e.dma_start(W1[:, e_ * WE:(e_ + 1) * WE].rearrange("p (k n) -> p k n", k=KC),
                                               d['w1'][e_].rearrange("(k p) n -> p k n", p=P)), counts=w_in[e_])
            w_ready.append(sp.do(lambda e, e_=e_: e.dma_start(
                W2[:, e_ * WE:(e_ + 1) * WE].rearrange("p (k n) -> p k n", k=FC),
                d['w2'][e_].rearrange("(k p) n -> p k n", p=P)), counts=w_in[e_]))

        tab = p.counter("tables")
        R = lambda make, after: dve.do(make, after=after, counts=tab)
        count = routing["count"]
        scr = p.sb("scr", [P, 4, E])
        scr_i = p.sb("scr_i", [P, E], I32)
        tiles, cum, base, one = (scr[:, i, :] for i in range(4))
        tile_no = p.sb("tile_no", [1, MOE_TILES])
        spare = y[1][:].rearrange("p a c -> p (a c)")
        top = spare[:, 0:ALL_TILES * 8].rearrange("p (t k) -> p t k", k=8)
        before, row, hit = (spare[0:1, ALL_TILES * 8 + i * MOE_TILES:ALL_TILES * 8 + (i + 1) * MOE_TILES]
                            for i in range(3))
        owner = p.sb("owner", [1, MOE_TILES])
        owner_i, row_i = p.sb("owner_i", [1, MOE_TILES], I32), p.sb("row_i", [1, MOE_TILES], I32)
        pad_i = p.sb("pad_i", [1, E], I32)
        region = p.sb("region", [1, E])
        pool_tab = p.counter("pool_tab")
        pool.do(lambda e: e.iota(tile_no[:], [[1, MOE_TILES]], base=0, channel_multiplier=0,
                                 allow_small_or_imprecise_dtypes=True), counts=pool_tab)
        it = pool.do(lambda e: e.iota(region[:], [[REGION, E]], base=0, channel_multiplier=0,
                                      allow_small_or_imprecise_dtypes=True), counts=pool_tab)
        r = R(lambda e: e.memset(one, 1.0), [])
        r = R(lambda e: e.tensor_scalar(scr_i[:], count[:], float(ROWS - 1), None, ALU.add), [r])
        r = R(lambda e: e.tensor_scalar(scr_i[:], scr_i[:], ROWS.bit_length() - 1, None, ALU.arith_shift_right), [r])
        r = R(lambda e: e.tensor_copy(tiles, scr_i[:]), [r])
        r = R(lambda e: e.tensor_tensor_scan(cum, one, tiles, 0.0, ALU.mult, ALU.add), [r])
        r = R(lambda e: e.tensor_tensor(base, cum, tiles, op=ALU.subtract), [r])
        r = R(lambda e: e.tensor_scalar(base, base, float(ROWS), 1.0, ALU.mult, ALU.add), [r])
        r = R(lambda e: e.tensor_tensor(pad_i[:], count[0:1, :], region[:], op=ALU.add), [r, it])
        pad_ready = r
        r = R(lambda e: e.memset(owner[:], 0.0), [r])
        r = R(lambda e: e.memset(before, 0.0), [r])
        for e_ in range(E):
            h = R(lambda e, e_=e_: e.tensor_scalar(hit, tile_no[:], cum[0:1, e_:e_ + 1], None, ALU.is_ge), [r, it])
            r = R(lambda e: e.tensor_tensor(owner[:], owner[:], hit, op=ALU.add), [h])
            r = R(lambda e, e_=e_: e.scalar_tensor_tensor(before, hit, tiles[0:1, e_:e_ + 1], before,
                                                          op0=ALU.mult, op1=ALU.add), [r])
        r = R(lambda e: e.tensor_scalar(hit, owner[:], float(E), None, ALU.is_lt), [r])
        r = R(lambda e: e.tensor_tensor(owner[:], owner[:], hit, op=ALU.mult), [r])
        r = R(lambda e: e.tensor_copy(owner_i[:], owner[:]), [r])
        r = R(lambda e: e.tensor_tensor(row, tile_no[:], before, op=ALU.subtract), [r])
        r = R(lambda e: e.tensor_scalar(row, row, float(ROWS), None, ALU.mult), [r])
        r = R(lambda e: e.scalar_tensor_tensor(row, owner[:], float(REGION), row, op0=ALU.mult, op1=ALU.add), [r])
        table_ready = R(lambda e: e.tensor_tensor(row_i[:], row, hit, op=ALU.mult), [r])

        z = dve.do(lambda e: e.memset(y[0][:], 0.0), counts=p.counter("zero"))
        padded = p.dma_counter("padded")
        for e_ in range(E):
            def pad(e, e_=e_):
                at = e.value_load(pad_i[0:1, e_:e_ + 1], min_val=0, max_val=E * REGION - ROWS)
                return e.dma_start(rows_dram[bass.ds(at, ROWS), :].rearrange("(p a) c -> p a c", p=P), y[0][:])
            pads = sp.do(pad, after=[z, pad_ready], counts=padded)

        pos, chosen, weight = routing["pos"], routing["chosen"], routing["weight"]
        slots, slot_weight = routing["slots"], routing["slot_weight"]
        key = h32[:].rearrange("p a b -> p (a b)")[:, 0:ALL_TILES * E].rearrange("p (t e) -> p t e", e=E)
        eq = h32[:].rearrange("p a b -> p (a b)")[:, ALL_TILES * E:2 * ALL_TILES * E].rearrange("p (t e) -> p t e", e=E)
        r = R(lambda e: e.tensor_tensor(key, pos[:], base.rearrange("p (a e) -> p a e", a=1)
                                        .broadcast_to([P, ALL_TILES, E]), op=ALU.add), [table_ready])
        r = R(lambda e: e.tensor_tensor(key, key, chosen[:], op=ALU.mult), [r])
        for t in range(ALL_TILES):
            r2 = R(lambda e, t=t: e.max(top[:, t, :], key[:, t, :]), [r])
        for k in range(TOPK):
            r = R(lambda e, k=k: e.tensor_tensor(eq, key, top[:, :, k:k + 1].broadcast_to([P, ALL_TILES, E]),
                                                 op=ALU.is_equal), [r2, r])
            r = R(lambda e: e.tensor_tensor(eq, eq, weight[:], op=ALU.mult), [r])
            r = R(lambda e, k=k: e.tensor_reduce(slot_weight[:, :, k], eq, AX.X, ALU.add), [r])
        slots_done = R(lambda e: e.tensor_scalar(slots[:], top[:, :, 0:TOPK], -1.0, None, ALU.add), [r])

        g = {n: p.counter(n) for n in ("t_pe", "x_hi", "x_lo", "w1_hi", "w1_lo", "w2_hi", "w2_lo", "b1c", "h_pe",
                                      "gelu", "h_hi", "h_lo", "y_pe", "y_ev")}
        x_loaded = [p.dma_counter(f"x_loaded{i}") for i in range(NX)]
        y_stored = [p.dma_counter(f"y_stored{i}") for i in range(2)]
        last = {}
        G = lambda k: last.get(k, [])

        def load_rows(j):
            def load(e):
                at = e.value_load(row_i[0:1, j:j + 1], min_val=0, max_val=E * REGION - ROWS)
                return e.dma_start(x_in[j % NX][:], rows_dram[bass.ds(at, ROWS), :].rearrange("(a p) c -> p a c", p=P))
            last[f"x{j}"] = [sp.do(load, after=[table_ready, pads] + G(f"x_free{j % NX}"), counts=x_loaded[j % NX])]

        def owner_of(e, j):
            return e.value_load(owner_i[0:1, j:j + 1], min_val=0, max_val=E - 1)

        flat = lambda t: t[:].rearrange("p a b -> p (a b)")

        def split_w1(j):
            h1, l1 = w1[j % 2]
            regs = {}

            def w1_hi(e):
                regs["dve"] = owner_of(e, j)
                return e.tensor_copy(flat(h1), W1[:, bass.ds(regs["dve"] * WE, WE)])

            def w1_lo(e):
                at = owner_of(e, j)
                return e.tensor_tensor(flat(l1), W1[:, bass.ds(at * WE, WE)], f32(flat(h1)), op=ALU.subtract)
            wait = ([w_ready[e_] for e_ in range(E)] + [b1_ready, table_ready])
            a = dve.do(w1_hi, after=wait + G(f"w1_free{j % 2}"), counts=g["w1_hi"])
            b = pool.do(w1_lo, after=wait + [a] + G(f"w1_free{j % 2}"), counts=g["w1_lo"])
            c = dve.do(lambda e: e.tensor_copy(b1[j % 2][:], b1T[:, bass.ds(regs["dve"] * FC, FC)]),
                       after=G(f"b1_free{j % 2}"), counts=g["b1c"])
            last[f"w1_{j}"] = [a, b]
            last[f"b1_{j}"] = [c]

        def split_w2(j):
            h2, l2 = w2[j % 2]
            regs = {}

            def w2_hi(e):
                regs["dve"] = owner_of(e, j)
                return e.tensor_copy(flat(h2), W2[:, bass.ds(regs["dve"] * WE, WE)])
            d_ = dve.do(w2_hi, after=G(f"w2_free{j % 2}"), counts=g["w2_hi"])
            e_ = dve.do(lambda e: e.tensor_tensor(flat(l2), W2[:, bass.ds(regs["dve"] * WE, WE)], f32(flat(h2)),
                                                  op=ALU.subtract), after=[d_] + G(f"w2_free{j % 2}"),
                        counts=g["w2_lo"])
            last[f"w2_{j}"] = [d_, e_]

        def transpose_rows(j):
            bank = XB[j % 2]
            for c in range(KC):
                for a in range(RT):
                    m = pe.do(lambda e, c=c, a=a: e.transpose(bank[:, c * ROWS + a * P:c * ROWS + (a + 1) * P],
                                                              x_in[j % NX][:, a, c * P:(c + 1) * P], ident[:]),
                              after=G(f"x{j}") + G(f"X_free{j % 2}") + [const_ready], counts=g["t_pe"])
            last[f"x_free{j % NX}"] = [m]
            hi, lo = xT[j % 2]
            view = bank[:].rearrange("p (c s) -> p c s", c=KC)
            a = act.do(lambda e: e.activation(hi[:], view, ACT.Copy), after=[m] + G(f"xT_free{j % 2}"),
                       counts=g["x_hi"])
            l = dve.do(lambda e: e.tensor_tensor(lo[:], view, f32(hi[:]), op=ALU.subtract),
                       after=[m, a] + G(f"xT_free{j % 2}"), counts=g["x_lo"])
            last[f"X_free{j % 2}"] = [l]
            last[f"xT{j}"] = [a, l]

        def hidden(j):
            hh, hl = hT[j % 2]
            for u in range(FC // 2):
                bank = HB[2 * (j % 2) + u]
                for f in (2 * u, 2 * u + 1):
                    terms = [(w, x, c) for c in range(KC) for w, x in split3(w1[j % 2], xT[j % 2])]
                    for i, (w, x, c) in enumerate(terms):
                        m = pe.do(lambda e, f=f, i=i, w=w, x=x, c=c, bank=bank, n=len(terms): e.matmul(
                            bank[:, (f % 2) * ROWS:(f % 2 + 1) * ROWS], w[:, c, f * P:(f + 1) * P], x[:, c, :],
                            start=(i == 0), stop=(i == n - 1)),
                            after=G(f"w1_{j}") + G(f"xT{j}") + G(f"H_free{2 * (j % 2) + u}"), counts=g["h_pe"])
                for f in (2 * u, 2 * u + 1):
                    a = act.do(lambda e, f=f, bank=bank: e.activation(
                        h32[:, f, :], bank[:, (f % 2) * ROWS:(f % 2 + 1) * ROWS], ACT.Gelu, bias=b1[j % 2][:, f:f + 1]),
                        after=[m, slots_done] + G(f"b1_{j}") + G(f"h32_free{u}"), counts=g["gelu"])
                last[f"H_free{2 * (j % 2) + u}"] = [a]
                fs = slice(2 * u, 2 * u + 2)
                hi = act.do(lambda e, fs=fs: e.activation(hh[:, fs, :], h32[:, fs, :], ACT.Copy),
                            after=[a] + G(f"hT_free{j % 2}"), counts=g["h_hi"])
                lo = dve.do(lambda e, fs=fs: e.tensor_tensor(hl[:, fs, :], h32[:, fs, :], f32(hh[:, fs, :]),
                                                             op=ALU.subtract),
                            after=[a, hi] + G(f"hT_free{j % 2}"), counts=g["h_lo"])
                last[f"h32_free{u}"] = [lo]
                last[f"h{j}_{u}"] = [hi, lo]
            last[f"w1_free{j % 2}"] = last[f"xT_free{j % 2}"] = [m]
            last[f"b1_free{j % 2}"] = [a]

        def results(j):
            bank = YB[j % 2]
            for a in range(RT):
                terms = [(h, w, f) for f in range(FC) for h, w in split3(hT[j % 2], w2[j % 2])]
                for i, (h, w, f) in enumerate(terms):
                    m = pe.do(lambda e, a=a, i=i, h=h, w=w, f=f, n=len(terms): e.matmul(
                        bank[:, a * D:(a + 1) * D], h[:, f, a * P:(a + 1) * P], w[:, f, :],
                        start=(i == 0), stop=(i == n - 1)),
                        after=G(f"w2_{j}") + G(f"h{j}_{f // 2}") + G(f"Y_free{j % 2}"), counts=g["y_pe"])
            last[f"w2_free{j % 2}"] = last[f"hT_free{j % 2}"] = [m]
            o = act.do(lambda e: e.activation(y[j % 2][:], bank[:].rearrange("p (a c) -> p a c", a=RT), ACT.Copy),
                       after=[m] + G(f"y_free{j % 2}") + [pads], counts=g["y_ev"])
            last[f"Y_free{j % 2}"] = [o]
            last[f"y_free{j % 2}"] = [sp.do(lambda e: e.dma_start(
                y_dram[j * ROWS:(j + 1) * ROWS, :].rearrange("(a p) c -> p a c", p=P), y[j % 2][:]),
                after=[o], counts=y_stored[j % 2])]

        for j in range(NX):
            load_rows(j)
        split_w1(0)
        split_w1(1)
        split_w2(0)
        transpose_rows(0)
        for j in range(MOE_TILES + 1):
            if j + NX < MOE_TILES:
                load_rows(j + NX)
            if j + 1 < MOE_TILES:
                transpose_rows(j + 1)
            if j < MOE_TILES:
                hidden(j)
            if j + 2 < MOE_TILES:
                split_w1(j + 2)
            if j >= 1:
                results(j - 1)
            if j + 1 < MOE_TILES:
                split_w2(j + 1)
        sp.do(lambda e: e.nop(), after=G("y_free0") + G("y_free1") + [pads])
        p.run()


def combine(nc, d, x2_dram, y_dram, out, routing):
    with ExitStack() as stack:
        p = Part(nc, stack, "co")
        pe, act, dve, pool, sp = p.pe, p.act, p.dve, p.pool, p.sp
        ident, const_ready, _ = constants(p)
        slots, slot_weight, weight = routing["slots"], routing["slot_weight"], routing["weight"]
        NB = 6
        b2 = p.sb("b2", [E, D])
        wT = p.sb("wT", [E, TOKENS])
        got = [p.sb(f"got{i}", [P, TOPK, D]) for i in range(NB)]
        x2 = [p.sb(f"x2_{i}", [P, N_TILES, D]) for i in range(2)]
        o = [p.sb(f"o{i}", [P, N_TILES, D]) for i in range(2)]
        TB = [p.bank(f"T{i}") for i in range(2)]
        BB = [p.bank(f"B{i}") for i in range(2)]
        b2_in = p.dma_counter("b2_in")
        b2_ready = sp.do(lambda e: e.dma_start(b2[:], d['b2']), counts=b2_in)
        gathered = [p.dma_counter(f"gathered{i}") for i in range(NB)]
        x2_in = [p.dma_counter(f"x2_in{i}") for i in range(2)]
        stored = [p.dma_counter(f"stored{i}") for i in range(2)]
        g = {n: p.counter(n) for n in ("wT_pe", "wT_ev", "b_pe", "sum")}
        last = {}
        G = lambda k: last.get(k, [])

        def gather(tt):
            for k in range(TOPK):
                last[f"g{tt}"] = [pool.do(lambda e, k=k: e.indirect_dma_start(
                    got[tt % NB][:, k, :], None, y_dram, bass.IndirectOffsetOnAxis(slots[:, tt, k:k + 1], 0)),
                    after=G(f"got_free{tt % NB}"), counts=gathered[tt % NB])]

        for b in range(B):
            x2_ready = sp.do(lambda e, b=b: e.dma_start(x2[b % 2][:], x2_dram[b]), after=G(f"x2_free{b % 2}"),
                             counts=x2_in[b % 2])
            for t in range(N_TILES):
                m = pe.do(lambda e, b=b, t=t: e.transpose(TB[b % 2][0:E, t * P:(t + 1) * P],
                                                          weight[:, b * N_TILES + t, :], ident[:]),
                          after=[const_ready] + G(f"T_free{b % 2}"), counts=g["wT_pe"])
            w = act.do(lambda e, b=b: e.activation(wT[:, b * S:(b + 1) * S], TB[b % 2][0:E, :], ACT.Copy), after=[m],
                       counts=g["wT_ev"])
            last[f"T_free{b % 2}"] = [w]
            for t in range(N_TILES):
                tt = b * N_TILES + t
                gather(tt)
                m = pe.do(lambda e, tt=tt: e.matmul(BB[tt % 2][:, 0:D], wT[:, tt * P:(tt + 1) * P], b2[:],
                                                    start=True, stop=True),
                          after=[w, b2_ready] + G(f"B_free{tt % 2}"), counts=g["b_pe"])
                acc = o[b % 2][:, t, :]
                s = dve.do(lambda e, b=b, t=t, tt=tt, acc=acc: e.tensor_tensor(acc, BB[tt % 2][:, 0:D],
                                                                              x2[b % 2][:, t, :], op=ALU.add),
                           after=[m, x2_ready] + G(f"o_free{b % 2}"), counts=g["sum"])
                last[f"B_free{tt % 2}"] = [s]
                for k in range(TOPK):
                    s = dve.do(lambda e, tt=tt, k=k, acc=acc: e.scalar_tensor_tensor(
                        acc, got[tt % NB][:, k, :], slot_weight[:, tt, k:k + 1], acc, op0=ALU.mult, op1=ALU.add),
                        after=[s] + G(f"g{tt}"), counts=g["sum"])
                last[f"got_free{tt % NB}"] = [s]
            last[f"x2_free{b % 2}"] = [s]
            last[f"o_free{b % 2}"] = [sp.do(lambda e, b=b: e.dma_start(
                out[b].rearrange("(t p) c -> p t c", p=P), o[b % 2][:]), after=[s], counts=stored[b % 2])]
        sp.do(lambda e: e.nop(), after=G("o_free0") + G("o_free1"))
        p.run()


def decoder_layer(nc, d, out):
    with ExitStack() as stack:
        scratch = lambda n, shape: nc.dram_tensor(n, shape, F32, kind="Internal").ap()
        x1_dram = scratch("x1_rows", [B, P, N_TILES, D])
        x2_dram = scratch("x2_rows", [B, P, N_TILES, D])
        rows_dram = scratch("expert_rows", [E * REGION, D])
        y_dram = scratch("expert_results", [MOE_TILES * ROWS, D])
        first_attention(nc, d, x1_dram)
        sb = lambda n, shape, dt=F32: stack.enter_context(nc.sbuf_tensor("routing_" + n, shape, dt))
        routing = {n: sb(n, [P, ALL_TILES, E]) for n in ("weight", "pos", "chosen")}
        routing["count"] = sb("count", [P, E])
        routing["slots"] = sb("slots", [P, ALL_TILES, TOPK], I32)
        routing["slot_weight"] = sb("slot_weight", [P, ALL_TILES, TOPK])
        cross_attention(nc, d, x1_dram, x2_dram, rows_dram, routing)
        experts(nc, d, rows_dram, y_dram, routing)
        combine(nc, d, x2_dram, y_dram, out, routing)


def kernel(**inputs):
    import concourse.bacc as bacc
    from concourse.bass_utils import run_bass_kernel_spmd

    take = lambda name: np.asarray(inputs[name])
    own = {n: take(f"L0_attn_{n}") for n in ("Wqkv", "bqkv", "Wln", "bln")}
    own |= {n: take(f"L0_xattn_{n}") for n in ("bq", "bk", "bv", "bo")}
    own |= {n + "T": take(f"L0_xattn_{n}").T for n in ("Wq", "Wk", "Wv", "Wo")}
    own |= {n: take(f"L0_ffn_{n}") for n in ("router_w", "router_b", "w1", "w2", "b2")}
    own["b1T"] = take("L0_ffn_b1").reshape(E, FC, P).transpose(2, 0, 1).reshape(P, E * FC)
    own["x"] = take("x")
    own["ctxT"] = take("ctx_1024").transpose(0, 2, 1)

    nc = bacc.Bacc("TRN2", target_bir_lowering=False, num_devices=1)
    arrays, d = {}, {}
    for name, a in own.items():
        arrays["in_" + name] = np.ascontiguousarray(a)
        d[name] = nc.dram_tensor("in_" + name, a.shape, F32, kind="ExternalInput").ap()
    out = nc.dram_tensor("out", (B, S, D), F32, kind="ExternalOutput").ap()
    decoder_layer(nc, d, out)
    result = run_bass_kernel_spmd(nc, [arrays], core_ids=[0])
    return result.results[0]["out"]
```

```python
from contextlib import ExitStack

import numpy as np

import concourse.bass as bass
from concourse import mybir

F32 = mybir.dt.float32
F32R = mybir.dt.float32r
BF16 = mybir.dt.bfloat16
I32 = mybir.dt.int32
ACT = mybir.ActivationFunctionType
ALU = mybir.AluOpType
AX = mybir.AxisListType

P = 128
B, S, D = 8, 512, 256
N_TILES = S // P
KC = D // P
H, HD = 16, 64
INNER = H * HD
PAIRS = H // 2
E, TOPK, FF = 16, 4, 512
FC = FF // P
TOKENS = B * S
ALL_TILES = TOKENS // P
ROWS = 256
RT = ROWS // P
REGION = TOKENS + ROWS
MOE_TILES = (TOKENS * TOPK + E * (ROWS - 1)) // ROWS
LN_EPS, EPS_SUM, EPS_NORM = 1e-5, 1e-7, 1e-12
NEG = -1e30


class Counter:

    def __init__(self, sem, step=1):
        self.sem, self.step, self.value = sem, step, 0

    def next(self):
        self.value += self.step
        return (self, self.value)


class Queue:

    def __init__(self):
        self.steps = []

    def do(self, make, after=(), counts=None):
        self.steps.append((make, [a for a in after if a is not None], counts))
        return counts.next() if counts is not None else None

    def play(self, engine):
        waited = {}
        for make, after, counts in self.steps:
            for sig, value in after:
                if waited.get(sig, 0) < value:
                    engine.wait_ge(sig.sem, value)
                    waited[sig] = value
            instruction = make(engine)
            if counts is not None:
                instruction.then_inc(counts.sem, counts.step)


class Part:

    def __init__(self, nc, stack, name):
        self.nc, self.stack, self.name = nc, stack, name
        self.pe, self.act, self.dve, self.pool, self.sp = (Queue() for _ in range(5))

    def sb(self, name, shape, dtype=F32):
        return self.stack.enter_context(self.nc.sbuf_tensor(f"{self.name}_{name}", shape, dtype))

    def bank(self, name):
        return self.stack.enter_context(self.nc.psum_tensor(f"{self.name}_{name}", [P, 512], F32))

    def counter(self, name, step=1):
        return Counter(self.stack.enter_context(self.nc.semaphore(f"{self.name}_{name}")), step)

    def dma_counter(self, name):
        return self.counter(name, 16)

    def run(self):
        with self.nc.Block() as block:
            for register, queue in ((block.tensor, self.pe), (block.scalar, self.act), (block.vector, self.dve),
                                    (block.gpsimd, self.pool), (block.sync, self.sp)):
                register(queue.play)


def split3(a, b):
    (ah, al), (bh, bl) = a, b
    return ((al, bh), (ah, bl), (ah, bh))


def f32(ap):
    return ap.bitcast(F32)


def constants(part):
    done = part.counter("const")
    ident = part.sb("ident", [P, P])
    e0 = part.pool.do(lambda e: e.memset(ident[:], 0.0), counts=done)
    e1 = part.pool.do(lambda e: e.affine_select(out=ident[:], in_=ident[:], compare_op=ALU.not_equal, fill=1.0,
                                                base=0, pattern=[[-1, P]], channel_multiplier=1),
                      after=[e0], counts=done)
    return ident, e1, done


def load_split(part, name, dram, shape, stage, scale=None):
    hi, lo = part.sb(name + "_hi", shape, F32R), part.sb(name + "_lo", shape, F32R)
    dims = "p a b -> p (a b)"
    size = shape[1] * shape[2]
    view = stage["tile"][:, 0:size]
    got = part.act.do(lambda e: e.dma_start(view.rearrange("p (a b) -> p a b", a=shape[1]), dram),
                     after=stage["free"], counts=stage["dma"])
    h2, l2 = hi[:].rearrange(dims), lo[:].rearrange(dims)
    if scale is not None:
        got = part.dve.do(lambda e: e.tensor_scalar(view, view, scale, None, ALU.mult), after=[got],
                          counts=stage["split"])
    a = part.act.do(lambda e: e.activation(h2, view, ACT.Copy), after=[got], counts=stage["hi"])
    d = part.dve.do(lambda e: e.tensor_tensor(l2, view, f32(h2), op=ALU.subtract), after=[got, a],
                    counts=stage["split"])
    stage["free"] = [d]
    return (hi, lo), d


class Norm:

    def __init__(self, part, name):
        self.part = part
        self.stats = part.sb(name + "_stats", [P, N_TILES, 6])
        self.mv = part.sb(name + "_mv", [P, N_TILES, 2])
        self.rstd = part.sb(name + "_rstd", [P, N_TILES])
        self.power = part.sb(name + "_power", [P, N_TILES])
        self.dve, self.pool = part.counter(name + "_dve"), part.counter(name + "_pool")
        self.power_set = part.pool.do(lambda e: e.memset(self.power[:], -0.5), counts=self.pool)
        self.last = []

    def find(self, x, ready):
        p, mv, stats, rstd = self.part, self.mv, self.stats, self.rstd
        for t in range(N_TILES):
            s = p.dve.do(lambda e, t=t: e.bn_stats(stats[:, t, :], x[:, t, :]), after=ready + self.last,
                         counts=self.dve)
        for t in range(N_TILES):
            a = p.dve.do(lambda e, t=t: e.bn_aggr(mv[:, t, :], stats[:, t, :]), after=[s], counts=self.dve)
        v = p.dve.do(lambda e: e.tensor_scalar(rstd[:], mv[:, :, 1], LN_EPS, None, ALU.add), after=[a],
                     counts=self.dve)
        self.found = p.pool.do(lambda e: e.tensor_tensor(rstd[:], rstd[:], self.power[:], op=ALU.pow),
                                  after=[v, self.power_set], counts=self.pool)

    def apply(self, x, out, out_free):
        p, mv, rstd = self.part, self.mv, self.rstd
        for t in range(N_TILES):
            d = p.dve.do(lambda e, t=t: e.tensor_scalar(out[:, t, :], x[:, t, :], mv[:, t, 0:1], rstd[:, t:t + 1],
                                                        ALU.subtract, ALU.mult),
                         after=[self.found] + out_free, counts=self.dve)
        self.last = [d]
        return d


def first_attention(nc, d, x1_dram, W):
    with ExitStack() as stack:
        p = Part(nc, stack, "a1")
        pe, act, dve, pool, sp = p.pe, p.act, p.dve, p.pool, p.sp
        ident, const_ready, _ = constants(p)
        stage = {"tile": p.sb("stage", [P, KC * 768]), "dma": p.dma_counter("w_in"), "hi": p.counter("w_hi"),
                 "split": p.counter("w_split"), "free": []}
        x_loaded = [p.dma_counter(f"x_loaded{i}") for i in range(2)]
        x_in = [p.sb(f"x{i}", [P, N_TILES, D]) for i in range(2)]

        def load_x(b, free):
            return sp.do(lambda e: e.dma_start(x_in[b % 2][:], d['x'][b].rearrange("(t p) c -> p t c", p=P)),
                         after=free, counts=x_loaded[b % 2])

        Wqkv, wqkv_ready = load_split(p, "wqkv", d['Wqkv'].rearrange("(k p) n -> p k n", p=P), [P, KC, 768], stage)
        bias_in = p.dma_counter("bias_in")
        bqkv = p.sb("bqkv", [P, 768])
        bvT = p.sb("bvT", [P, KC])
        bln = p.sb("bln", [P, D])
        act.do(lambda e: e.dma_start(bqkv[:], d['bqkv'].rearrange("(a n) -> a n", a=1).broadcast_to([P, 768])),
              counts=bias_in)
        act.do(lambda e: e.dma_start(bvT[:], d['bqkv'][512:768].rearrange("(k p) -> p k", p=P),
                                    allow_slow_non_contiguous=True), counts=bias_in)
        bias_ready = act.do(lambda e: e.dma_start(bln[:], d['bln'].rearrange("(a n) -> a n", a=1)
                                                 .broadcast_to([P, D])), counts=bias_in)
        norm = Norm(p, "ln")
        xn = p.sb("xn", [P, N_TILES, D])
        xT = [tuple(p.sb(f"xT{i}{j}", [P, KC, S], F32R) for j in range(2)) for i in range(2)]
        qk = p.sb("qk", [P, N_TILES, 512])
        v32 = p.sb("v32", [P, N_TILES, D])
        v = [tuple(p.sb(f"v{i}{j}", [P, N_TILES, D], F32R) for j in range(2)) for i in range(2)]
        qk_stats = p.sb("qk_stats", [P, N_TILES * 2, 6])
        qk_mv = p.sb("qk_mv", [P, N_TILES * 2, 2])
        neg_mean = p.sb("neg_mean", [P, N_TILES * 2])
        sq = p.sb("sq", [P, N_TILES, 512])
        sq4 = p.sb("sq4", [P, D])
        s2 = p.sb("s2", [P, N_TILES * 2])
        s4 = p.sb("s4", [P, N_TILES])
        qf = p.sb("qf", [P, N_TILES])
        half = p.sb("half", [P, N_TILES])
        q2n = p.sb("q2n", [P, N_TILES, D])
        q2T = tuple(p.sb(f"q2T{i}", [P, KC, S], F32R) for i in range(2))
        k2 = p.sb("k2", [P, N_TILES, D])
        k2s = tuple(p.sb(f"k2s{i}", [P, N_TILES, D], F32R) for i in range(2))
        k4 = p.sb("k4", [P, N_TILES, D])
        ones = p.sb("ones", [P, 2])
        knorm = p.sb("knorm", [P, KC])
        kv32 = p.sb("kv32", [P, KC, D])
        kv = tuple(p.sb(f"kv{i}", [P, KC, D], F32R) for i in range(2))
        yT = tuple(p.sb(f"yT{i}", [P, KC, S], F32R) for i in range(2))
        xb = [p.sb(f"xb{i}", [P, N_TILES, D]) for i in range(3)]
        x1 = [p.sb(f"x1_{i}", [P, N_TILES, D]) for i in range(2)]
        T = [p.bank(f"T{i}") for i in range(2)]
        QK = [p.bank(f"QK{i}") for i in range(2)]
        V, KV, NB, Y = p.bank("V"), p.bank("KV"), p.bank("NB"), p.bank("Y")
        free = {k: [] for k in ("T0", "T1", "QK0", "QK1", "V", "KV", "NB", "Y")}

        g = {n: p.counter(n) for n in ("xT_pe", "xT_hi", "xT_lo", "qkv_pe", "qk_ev", "v_ev", "v_hi", "v_lo", "st",
                                      "sqr", "small", "small_pool", "q2n", "q2T_pe", "q2T_hi", "q2T_lo", "k2",
                                      "k2_hi", "k2_lo", "k4", "kv_pe", "kn_pool", "kn", "kv_ev", "kv_hi", "kv_lo",
                                      "yT_pe", "yT_hi", "yT_lo", "y_pe", "xb", "x1")}
        stored = [p.dma_counter(f"x1_stored{i}") for i in range(2)]
        c0 = pool.do(lambda e: e.memset(ones[:], 1.0), counts=g["small_pool"])
        c1 = pool.do(lambda e: e.memset(half[:], 0.5), counts=g["small_pool"])
        prev = {}
        done = {}
        G = lambda k: prev.get(k, [])

        def transposed(src, dst, names, src_ready, dst_free):
            for c in range(KC):
                for t in range(N_TILES):
                    tp = pe.do(lambda e, c=c, t=t: e.transpose(T[c][:, t * P:(t + 1) * P],
                                                               src[:, t, c * P:(c + 1) * P], ident[:]),
                               after=[src_ready, const_ready] + free[f"T{c}"], counts=g[names + "_pe"])
                hi = act.do(lambda e, c=c: e.activation(dst[0][:, c, :], T[c][:], ACT.Copy),
                            after=[tp] + dst_free, counts=g[names + "_hi"])
                lo = dve.do(lambda e, c=c: e.tensor_tensor(dst[1][:, c, :], T[c][:], f32(dst[0][:, c, :]),
                                                           op=ALU.subtract),
                            after=[tp, hi] + dst_free, counts=g[names + "_lo"])
                free[f"T{c}"] = [lo]
            return tp, [hi, lo]

        def find_mean(b):
            loaded = load_x(b, G(f"x_in{b % 2}"))
            norm.find(x_in[b % 2], [loaded])
            done[b] = {"x": loaded}

        def normalise(b):
            done[b]["xn"] = norm.apply(x_in[b % 2], xn, G("xn"))

        def residual(b):
            xi = x_in[b % 2]
            e_xb = pool.do(lambda e: e.tensor_tensor(
                xb[b % 3][:], xi[:], bln[:].rearrange("p (a c) -> p a c", a=1).broadcast_to([P, N_TILES, D]),
                op=ALU.add), after=[done[b]["x"], bias_ready] + G(f"xb{b % 3}"), counts=g["xb"])
            prev[f"x_in{b % 2}"] = [done[b]["xn"], e_xb]
            done[b]["xb"] = e_xb

        def transpose_x(b):
            tp, done[b]["xT"] = transposed(xn, xT[b % 2], "xT", done[b]["xn"], G(f"xT{b % 2}"))
            prev["xn"] = [tp]

        def project(b, u):
            par, dn = b % 2, done[b]
            xT_ready = dn["xT"]
            for t in (2 * u, 2 * u + 1):
                bank = QK[t % 2]
                for c in range(KC):
                    for i, (a, w) in enumerate(split3(xT[par], Wqkv)):
                        m = pe.do(lambda e, t=t, c=c, i=i, a=a, w=w, bank=bank: e.matmul(
                            bank[:], a[:, c, t * P:(t + 1) * P], w[:, c, 0:512],
                            start=(c == 0 and i == 0), stop=(c == KC - 1 and i == 2)),
                            after=xT_ready + [wqkv_ready] + free[f"QK{t % 2}"], counts=g["qkv_pe"])
                ev = dve.do(lambda e, t=t, bank=bank: e.tensor_tensor(qk[:, t, :], bank[:], bqkv[:, 0:512], op=ALU.add),
                            after=[m, bias_ready] + G("qk"), counts=g["qk_ev"])
                free[f"QK{t % 2}"] = [ev]
                for c in range(KC):
                    for i, (a, w) in enumerate(split3(xT[par], Wqkv)):
                        mv_ = pe.do(lambda e, t=t, c=c, i=i, a=a, w=w: e.matmul(
                            V[:, (t % 2) * D:(t % 2 + 1) * D], a[:, c, t * P:(t + 1) * P], w[:, c, 512:768],
                            start=(c == 0 and i == 0), stop=(c == KC - 1 and i == 2)),
                            after=(free["V"] if t % 2 == 0 else []), counts=g["qkv_pe"])
                if t % 2 == 1:
                    ve = dve.do(lambda e, t=t: e.tensor_tensor(
                        v32[:, t - 1:t + 1, :], V[:].rearrange("p (a c) -> p a c", a=2),
                        bqkv[:, 512:768].rearrange("p (a c) -> p a c", a=1).broadcast_to([P, 2, D]), op=ALU.add),
                        after=[mv_] + G("v32"), counts=g["v_ev"])
                    free["V"] = [ve]
                for j in range(2):
                    st = dve.do(lambda e, t=t, j=j: e.bn_stats(qk_stats[:, 2 * t + j, :], qk[:, t, j * D:(j + 1) * D]),
                                after=[ev] + G("stats"), counts=g["st"])
            ts = slice(2 * u, 2 * u + 2)
            vh = act.do(lambda e: e.activation(v[par][0][:, ts, :], v32[:, ts, :], ACT.Copy), after=[ve] + G(f"v{par}"),
                        counts=g["v_hi"])
            vl = pool.do(lambda e: e.tensor_tensor(v[par][1][:, ts, :], v32[:, ts, :], f32(v[par][0][:, ts, :]),
                                                   op=ALU.subtract),
                         after=[vh, ve] + G(f"v{par}"), counts=g["v_lo"])
            if u == 1:
                prev["v32"] = [vl]
            dn.update(qk=ev, st=st, v=[vh, vl])

        def spread(b, u):
            dn, js = done[b], slice(4 * u, 4 * u + 4)
            for j in range(4 * u, 4 * u + 4):
                ag = dve.do(lambda e, j=j: e.bn_aggr(qk_mv[:, j, :], qk_stats[:, j, :]),
                            after=[dn["st"]] + G("mv"), counts=g["st"])
            nm = dve.do(lambda e: e.tensor_scalar(neg_mean[:, js], qk_mv[:, js, 0], -1.0, None, ALU.mult),
                        after=[ag] + G("neg_mean"), counts=g["st"])
            if u == 1:
                prev["stats"] = [ag]
            s2a = dve.do(lambda e: e.tensor_scalar(s2[:, js], qk_mv[:, js, 1], float(D), EPS_SUM, ALU.mult, ALU.add),
                         after=[ag] + G("s2"), counts=g["small"])
            s2b = dve.do(lambda e: e.reciprocal(s2[:, js], s2[:, js]), after=[s2a], counts=g["small"])
            if u == 1:
                prev["mv"] = [s2a, nm]
            dn[f"spread{u}"] = (nm, s2b)

        def square(b, u):
            dn, tiles, ts = done[b], (2 * u, 2 * u + 1), slice(2 * u, 2 * u + 2)
            nm, _ = dn[f"spread{u}"]
            for t in tiles:
                for j in range(2):
                    a1 = act.do(lambda e, t=t, j=j: e.activation(
                        sq[:, t, j * D:(j + 1) * D], qk[:, t, j * D:(j + 1) * D], ACT.Square,
                        bias=neg_mean[:, 2 * t + j:2 * t + j + 1]), after=[nm, dn["qk"]] + G("sq"), counts=g["sqr"])
                    if j == 0:
                        a2 = act.do(lambda e, t=t: e.activation(sq4[:], sq[:, t, 0:D], ACT.Square,
                                                                accum_out=s4[:, t:t + 1]),
                                    after=[a1] + G("s4") + G("sq4"), counts=g["sqr"])
                        prev["sq4"] = [a2]
            if u == 1:
                prev["qk"] = prev["neg_mean"] = [a1]
            r = pool.do(lambda e: e.tensor_tensor(s4[:, ts], s4[:, ts], half[:, ts], op=ALU.pow), after=[a1, a2, c1],
                        counts=g["small_pool"])
            dn[f"square{u}"] = (a1, r)

        def scale(b, u):
            dn = done[b]
            tiles, ts, js = (2 * u, 2 * u + 1), slice(2 * u, 2 * u + 2), slice(4 * u, 4 * u + 4)
            (_, s2b), (a1, r) = dn[f"spread{u}"], dn[f"square{u}"]
            aq = s2[:, js].rearrange("p (t j) -> p t j", j=2)[:, :, 0]
            for t in tiles:
                kn_ = dve.do(lambda e, t=t: e.tensor_scalar(k2[:, t, :], sq[:, t, D:512], s2[:, 2 * t + 1:2 * t + 2],
                                                            None, ALU.mult),
                             after=[s2b, a1] + G("k2"), counts=g["k2"])
            f1 = dve.do(lambda e: e.tensor_tensor(s4[:, ts], s4[:, ts], aq, op=ALU.mult), after=[r, s2b], counts=g["small"])
            f2 = dve.do(lambda e: e.tensor_scalar(s4[:, ts], s4[:, ts], EPS_NORM, float(S) ** 0.5, ALU.max, ALU.mult),
                        after=[f1], counts=g["small"])
            f3 = dve.do(lambda e: e.reciprocal(s4[:, ts], s4[:, ts]), after=[f2], counts=g["small"])
            f4 = dve.do(lambda e: e.tensor_tensor(qf[:, ts], s4[:, ts], aq, op=ALU.mult), after=[f3] + G("qf"),
                        counts=g["small"])
            for t in tiles:
                qn = dve.do(lambda e, t=t: e.tensor_scalar(q2n[:, t, :], sq[:, t, 0:D], qf[:, t:t + 1], None, ALU.mult),
                            after=[f4, a1] + G("q2n"), counts=g["q2n"])
            if u == 1:
                prev["s4"], prev["qf"] = [f4], [qn]
                prev["sq"], prev["s2"] = [qn, kn_], [kn_, f4]
            k4e = pool.do(lambda e: e.tensor_tensor(k4[:, ts, :], k2[:, ts, :], k2[:, ts, :], op=ALU.mult),
                          after=[kn_] + G("k4"), counts=g["k4"])
            kh = act.do(lambda e: e.activation(k2s[0][:, ts, :], k2[:, ts, :], ACT.Copy), after=[kn_] + G("k2s"),
                        counts=g["k2_hi"])
            kl = dve.do(lambda e: e.tensor_tensor(k2s[1][:, ts, :], k2[:, ts, :], f32(k2s[0][:, ts, :]), op=ALU.subtract),
                        after=[kh, kn_] + G("k2s"), counts=g["k2_lo"])
            if u == 1:
                prev["k2"] = [kl, k4e]
            dn.update(q2n=qn, k2s=[kh, kl], k4=k4e)

        def state(b):
            par, dn = b % 2, done[b]
            tp, dn["q2T"] = transposed(q2n, q2T, "q2T", dn["q2n"], G("q2T"))
            prev["q2n"] = [tp]
            for c in range(KC):
                for t in range(N_TILES):
                    mn = pe.do(lambda e, t=t, c=c: e.matmul(NB[:, 2 * c:2 * c + 2], k4[:, t, c * P:(c + 1) * P],
                                                            ones[:], start=(t == 0), stop=(t == N_TILES - 1)),
                               after=[dn["k4"], c0] + free["NB"], counts=g["kv_pe"])
            prev["k4"] = [mn]
            for c in range(KC):
                for t in range(N_TILES):
                    for i, (a, w) in enumerate(split3(k2s, v[par])):
                        m = pe.do(lambda e, t=t, c=c, i=i, a=a, w=w: e.matmul(
                            KV[:, c * D:(c + 1) * D], a[:, t, c * P:(c + 1) * P], w[:, t, :],
                            start=(t == 0 and i == 0), stop=(t == N_TILES - 1 and i == 2)),
                            after=dn["k2s"] + dn["v"] + free["KV"], counts=g["kv_pe"])
            prev["k2s"] = prev[f"v{par}"] = [m]
            nb = NB[:, 0:4].rearrange("p (c j) -> p c j", j=2)[:, :, 0]
            n1 = dve.do(lambda e: e.tensor_copy(knorm[:], nb), after=[mn] + G("knorm"), counts=g["kn"])
            free["NB"] = [n1]
            n2 = pool.do(lambda e: e.tensor_tensor(knorm[:], knorm[:], half[:, 0:KC], op=ALU.pow), after=[n1],
                         counts=g["kn_pool"])
            n3 = dve.do(lambda e: e.tensor_scalar(knorm[:], knorm[:], EPS_NORM, None, ALU.max), after=[n2],
                        counts=g["kn"])
            n4 = dve.do(lambda e: e.reciprocal(knorm[:], knorm[:]), after=[n3], counts=g["kn"])
            for c in range(KC):
                k5 = dve.do(lambda e, c=c: e.tensor_scalar(kv32[:, c, :], KV[:, c * D:(c + 1) * D], knorm[:, c:c + 1],
                                                           None, ALU.mult),
                            after=[n4, m] + G("kv32"), counts=g["kv_ev"])
            prev["knorm"] = [k5]
            free["KV"] = [k5]
            k6 = act.do(lambda e: e.activation(kv[0][:], kv32[:], ACT.Copy), after=[k5] + G("kv"),
                        counts=g["kv_hi"])
            k7 = dve.do(lambda e: e.tensor_tensor(kv[1][:], kv32[:], f32(kv[0][:]), op=ALU.subtract),
                        after=[k6, k5] + G("kv"), counts=g["kv_lo"])
            prev["kv32"] = [k7]
            dn["kv"] = [k6, k7]

        def attend(b):
            par, dn = b % 2, done[b]
            for m_ in range(KC):
                terms = [(w, a, c, 512) for c in range(KC) for w, a in split3(Wqkv, xT[par])]
                terms += [(w, a, c, 0) for c in range(KC) for w, a in split3(kv, q2T)]
                for i, (w, a, c, off) in enumerate(terms):
                    yp = pe.do(lambda e, m_=m_, i=i, w=w, a=a, c=c, off=off, n=len(terms): e.matmul(
                        QK[m_][:], w[:, c, off + m_ * P:off + (m_ + 1) * P], a[:, c, :],
                        start=(i == 0), stop=(i == n - 1)),
                        after=(free[f"QK{m_}"] if off else dn["q2T"] + dn["kv"]), counts=g["yT_pe"])
                hi = act.do(lambda e, m_=m_: e.activation(yT[0][:, m_, :], QK[m_][:], ACT.Identity,
                                                          bias=bvT[:, m_:m_ + 1]),
                            after=[yp, bias_ready] + G("yT"), counts=g["yT_hi"])
                lo = dve.do(lambda e, m_=m_: e.scalar_tensor_tensor(
                    yT[1][:, m_, :], QK[m_][:], bvT[:, m_:m_ + 1], f32(yT[0][:, m_, :]), op0=ALU.add,
                    op1=ALU.subtract), after=[yp, hi] + G("yT"), counts=g["yT_lo"])
                free[f"QK{m_}"] = [lo]
            prev[f"xT{par}"] = prev["q2T"] = prev["kv"] = [yp]
            dn["yT"] = [hi, lo]

        def output(b):
            par, dn, o = b % 2, done[b], x1[b % 2]
            for u, (name, bank) in enumerate((("Y", Y), ("V", V))):
                for t in (2 * u, 2 * u + 1):
                    for c in range(KC):
                        for i, (a, w) in enumerate(split3(yT, Wln)):
                            m = pe.do(lambda e, t=t, c=c, i=i, a=a, w=w, bank=bank: e.matmul(
                                bank[:, (t % 2) * D:(t % 2 + 1) * D], a[:, c, t * P:(t + 1) * P], w[:, c, :],
                                start=(c == 0 and i == 0), stop=(c == KC - 1 and i == 2)),
                                after=dn["yT"] + [wln_ready] + (free[name] if t % 2 == 0 else []), counts=g["y_pe"])
                ye = dve.do(lambda e, u=u, bank=bank: e.tensor_tensor(
                    o[:, 2 * u:2 * u + 2, :], bank[:].rearrange("p (a c) -> p a c", a=2), xb[b % 3][:, 2 * u:2 * u + 2, :],
                    op=ALU.add), after=[m, dn["xb"]] + G(f"x1{par}"), counts=g["x1"])
                free[name] = [ye]
            prev["yT"] = [m]
            prev[f"xb{b % 3}"] = [ye]
            prev[f"x1{par}"] = [sp.do(lambda e: e.dma_start(x1_dram[b], o[:]), after=[ye], counts=stored[par])]

        find_mean(0)
        normalise(0)
        residual(0)
        transpose_x(0)
        Wln, wln_ready = load_split(p, "wln", d['Wln'].rearrange("(k p) n -> p k n", p=P), [P, KC, D], stage)

        chunk_in = stage["tile"][:, 0:INNER]
        chunk_loaded = p.dma_counter("chunk_loaded")
        prev["chunk"] = stage["free"]
        chunk_scaled, chunk_hi, chunk_lo = (p.counter("chunk_" + n) for n in ("scaled", "hi", "lo"))

        def prepare_weight(i):
            name, c = list(W)[i // KC], i % KC
            hi, lo = (w[:, c, :] for w in W[name])
            got = sp.do(lambda e: e.dma_start(chunk_in, d[name][c * P:(c + 1) * P, :]), after=G("chunk"),
                        counts=chunk_loaded)
            if name == "WqT":
                got = dve.do(lambda e: e.tensor_scalar(chunk_in, chunk_in, HD ** -0.5, None, ALU.mult), after=[got],
                             counts=chunk_scaled)
            a = act.do(lambda e: e.activation(hi, chunk_in, ACT.Copy), after=[got], counts=chunk_hi)
            prev["chunk"] = [pool.do(lambda e: e.tensor_tensor(lo, chunk_in, f32(hi), op=ALU.subtract),
                                     after=[got, a], counts=chunk_lo)]

        for b in range(B + 1):
            projecting, attending, coming = b < B, b >= 1, b + 1 < B
            if projecting:
                project(b, 0)
            if coming:
                find_mean(b + 1)
            if projecting:
                spread(b, 0)
            if attending:
                state(b - 1)
                if b - 1 < len(W) * KC:
                    prepare_weight(b - 1)
            if projecting:
                project(b, 1)
                spread(b, 1)
            if coming:
                normalise(b + 1)
            if projecting:
                square(b, 0)
                scale(b, 0)
            if attending:
                attend(b - 1)
            if coming:
                residual(b + 1)
                transpose_x(b + 1)
            if projecting:
                square(b, 1)
                scale(b, 1)
            if attending:
                output(b - 1)
        sp.do(lambda e: e.nop(), after=G("x10") + G("x11"))
        p.run()


SCORE_AT = {3: 0, 2: 512, 0: 896, 1: 1024}
SCORE_BANK = ((3, 0, 0), (2, 1, 0), (1, 2, 0), (0, 2, 256))
MIN_COLS = 256
PROB_T_AT = {0: 0, 1: 512, 3: 896, 2: 1024}
TRIANGLE = 1280
V_TILE_AT = {(3, 0): (0, 0), (3, 1): (0, 1), (5, 0): (0, 2), (5, 1): (0, 3),
             (9, 1): (1, 0), (13, 1): (1, 1), (15, 0): (1, 2), (15, 1): (1, 3)}
BANK_COLS = ((0, 512), (512, 1024), (1024, TRIANGLE))


def cross_attention(nc, d, x1_dram, x2_dram, rows_dram, routing, W, projecting, resident):
    with ExitStack() as stack:
        p = Part(nc, stack, "xa")
        upper = lambda name, shape: projecting.enter_context(nc.sbuf_tensor(f"xa_{name}", shape, F32R, side="right"))
        pe, act, dve, pool, sp = p.pe, p.act, p.dve, p.pool, p.sp
        ident, const_ready, _ = constants(p)
        cols = lambda n: p.sb(n, [P, N_TILES, D])
        xn = cols("xn")
        ctx32 = p.sb("ctx32", [P, KC, S])
        oT = p.sb("oT", [P, PAIRS, S])
        WoT = p.sb("WoT", [P, PAIRS, D])
        bqT, bkT = p.sb("bqT", [P, PAIRS]), p.sb("bkT", [P, PAIRS])
        bv, bo = p.sb("bv", [P, INNER]), p.sb("bo", [P, D])
        rw, rb = p.sb("rw", [P, KC, E]), p.sb("rb", [P, E])
        bias_in = p.dma_counter("bias_in")
        row = lambda v, n: v.rearrange("(a n) -> a n", a=1).broadcast_to([P, n])
        act.do(lambda e: e.dma_start(WoT[:], d['WoT'].rearrange("(k p) n -> p k n", p=P)), counts=bias_in)
        act.do(lambda e: e.dma_start(bqT[:], d['bq'].rearrange("(k p) -> p k", p=P), allow_slow_non_contiguous=True),
               counts=bias_in)
        act.do(lambda e: e.dma_start(bkT[:], d['bk'].rearrange("(k p) -> p k", p=P), allow_slow_non_contiguous=True),
               counts=bias_in)
        act.do(lambda e: e.dma_start(bv[:], row(d['bv'], INNER)), counts=bias_in)
        act.do(lambda e: e.dma_start(bo[:], row(d['bo'], D)), counts=bias_in)
        act.do(lambda e: e.dma_start(rw[:], d['router_w'].rearrange("(k p) n -> p k n", p=P)), counts=bias_in)
        bias_in_all = act.do(lambda e: e.dma_start(rb[:], row(d['router_b'], E)), counts=bias_in)
        const_p = p.counter("const_pool")

        identb, maskb = p.sb("identb", [P, P], BF16), p.sb("maskb", [P, P], BF16)
        tri, onesb = p.sb("tri", [P, P], BF16), p.sb("onesb", [P, P], BF16)
        for tile, fill in ((identb, 0.0), (maskb, 0.0), (tri, 1.0), (onesb, 1.0)):
            m0 = pool.do(lambda e, tile=tile, fill=fill: e.memset(tile[:], fill), counts=const_p)
        pool.do(lambda e: e.affine_select(out=identb[:], in_=identb[:], compare_op=ALU.not_equal, fill=1.0, base=0,
                                          pattern=[[-1, P]], channel_multiplier=1), after=[m0], counts=const_p)
        pool.do(lambda e: e.affine_select(out=maskb[:], in_=maskb[:], compare_op=ALU.is_ge, fill=NEG, base=0,
                                          pattern=[[-1, P]], channel_multiplier=1), after=[m0], counts=const_p)
        tri_ready = pool.do(lambda e: e.affine_select(out=tri[:], in_=tri[:], compare_op=ALU.is_ge, fill=0.0, base=-1,
                                                      pattern=[[1, P]], channel_multiplier=-1), after=[m0],
                            counts=const_p)
        ebase = p.sb("ebase", [P, E])
        for e_ in range(E):
            m1 = pool.do(lambda e, e_=e_: e.memset(ebase[:, e_:e_ + 1], float(e_ * REGION + 1)), counts=const_p)
        probs = p.sb("probs", [P, N_TILES, E + 4])
        sentinel = p.sb("sentinel", [P, N_TILES, 4])
        number, region = p.sb("number", [P, 1]), p.sb("region", [1, E])
        pool.do(lambda e: e.iota(number[:], [[0, 1]], base=0, channel_multiplier=1,
                                 allow_small_or_imprecise_dtypes=True), counts=const_p)
        pool.do(lambda e: e.iota(region[:], [[REGION, E]], base=0, channel_multiplier=0,
                                 allow_small_or_imprecise_dtypes=True), counts=const_p)
        for i in range(4):
            pool.do(lambda e, i=i: e.memset(probs[:, :, E + i:E + i + 1], float(-1 - i)), counts=const_p)
            m2 = pool.do(lambda e, i=i: e.memset(sentinel[:, :, i:i + 1], float(-1 - i)), counts=const_p)
        count = routing["count"]
        consts = pool.do(lambda e: e.memset(count[:], 0.0), counts=const_p)

        ln2, ln3 = Norm(p, "ln2"), Norm(p, "ln3")
        x1 = [cols(f"x1_{i}") for i in range(2)]
        xT = [tuple(upper(f"xT{i}{j}", [P, KC, S]) for j in range(2)) for i in range(2)]
        cT = [tuple(upper(f"cT{i}{j}", [P, KC, S]) for j in range(2)) for i in range(2)]
        nmax = [p.sb(f"nmax{i}", [P, N_TILES]) for i in range(2)]
        sums = [p.sb(f"sums{i}", [P, N_TILES]) for i in range(2)]
        x2 = cols("x2")
        xn3 = cols("xn3")
        xn3T = xn[:].rearrange("p t c -> p (t c)").rearrange("p (k s) -> p k s", k=KC)
        small = lambda n, k=E: p.sb(n, [P, N_TILES, k])
        lg, repl, mask, key = small("lg"), small("repl", E + 4), small("mask"), small("key")
        maskb16 = p.sb("maskb16", [P, N_TILES, E], BF16)
        top8, key8 = small("top8", 8), small("key8", 8)
        red = p.sb("red", [P, N_TILES])
        rows_i = [p.sb(f"rows{i}", [P, N_TILES, TOPK], I32) for i in range(2)]

        heads = ExitStack()
        own = lambda name, shape, dtype=F32: heads.enter_context(nc.sbuf_tensor(f"xa_{name}", shape, dtype))
        v = [own(f"v{i}", [P, N_TILES, INNER // 2]) for i in range(2)]
        qs = [[own(f"qs{i}{j}", [P, S], F32R) for j in range(2)] for i in range(2)]
        ks = [[own(f"ks{i}{j}", [P, 2, S], F32R) for j in range(2)] for i in range(2)]
        prob = [own(f"prob{i}", [P, TRIANGLE]) for i in range(2)]
        probT = [own(f"probT{i}", [P, TRIANGLE]) for i in range(2)]

        SB = [p.bank(f"S{i}") for i in range(3)]
        TB = [p.bank(f"T{i}") for i in range(2)]
        work = [p.bank(f"work{i}") for i in range(3)]
        free = {"S0": [], "S1": [], "S2": [], "T0": [], "T1": []}
        work_free, turn = [[], [], []], [0]

        def next_bank():
            i = turn[0] % 3
            turn[0] += 1
            return work[i], i, work_free[i]

        names = ("x_hi", "x_lo", "c_hi", "c_lo", "c_lo_first", "pj_pe", "part_hi", "part_lo", "v_ev", "s_pe", "max",
                 "exp", "rcp", "norm", "t_pe", "t_act", "t_dve", "pv_pe", "o_ev", "xb", "x2", "xn3T",
                 "r_dve", "r_act", "r_rows")
        g = {n: p.counter(n) for n in names}
        x1_in = [p.dma_counter(f"x1_in{i}") for i in range(2)]
        ctx_in, x2_out = p.dma_counter("ctx_in"), p.dma_counter("x2_out")
        scattered, padded = p.dma_counter("scattered"), p.dma_counter("padded")

        stacked = [p.dma_counter(f"k_stacked{i}") for i in range(2)]
        last = {}
        G = lambda k: last.get(k, [])

        def load(b):
            last[f"x1_loaded{b}"] = [sp.do(lambda e: e.dma_start(x1[b % 2][:], x1_dram[b]),
                                           after=G(f"x1_free{b % 2}"), counts=x1_in[b % 2])]
            last["ctx_loaded"] = [sp.do(lambda e: e.dma_start(ctx32[:], d['ctxT'][b].rearrange("(k p) s -> p k s", p=P)),
                                        after=G("ctx32_free"), counts=ctx_in)]

        def split_ctx(b):
            hi, lo = cT[b % 2]
            a = act.do(lambda e: e.activation(hi[:], ctx32[:], ACT.Copy),
                       after=G("ctx_loaded") + G(f"cT_free{b % 2}"), counts=g["c_hi"])
            engine, count_ = (dve, g["c_lo_first"]) if b == 0 else (pool, g["c_lo"])
            l = engine.do(lambda e: e.tensor_tensor(lo[:], ctx32[:], f32(hi[:]), op=ALU.subtract),
                        after=[a] + G("ctx_loaded") + G(f"cT_free{b % 2}"), counts=count_)
            last["ctx32_free"] = [l]
            last[f"cT_ready{b}"] = [a, l]

        def find2(b):
            ln2.find(x1[b % 2], G(f"x1_loaded{b}"))

        def norm2(b):
            last["xn_ready"] = [ln2.apply(x1[b % 2], xn, G("xn_free") + G("xn3T_free"))]
            last[f"xb{b}"] = [pool.do(lambda e: e.tensor_tensor(
                x1[b % 2][:], x1[b % 2][:], bo[:].rearrange("p (a c) -> p a c", a=1).broadcast_to([P, N_TILES, D]),
                op=ALU.add), after=G("xn_ready") + [bias_ready], counts=g["xb"])]

        def transpose_x(b, c):
            PJ, bank, freed = next_bank()
            for t in range(N_TILES):
                m = pe.do(lambda e, t=t: e.transpose(PJ[:, t * P:(t + 1) * P], xn[:, t, c * P:(c + 1) * P], ident[:]),
                          after=G("xn_ready") + freed + [const_ready], counts=g["pj_pe"])
            hi, lo = xT[b % 2]
            a = act.do(lambda e: e.activation(hi[:, c, :], PJ[:], ACT.Copy), after=[m] + G(f"xT_free{b % 2}"),
                       counts=g["x_hi"])
            l = dve.do(lambda e: e.tensor_tensor(lo[:, c, :], PJ[:], f32(hi[:, c, :]), op=ALU.subtract),
                       after=[m, a] + G(f"xT_free{b % 2}"), counts=g["x_lo"])
            work_free[bank] = [l]
            last["xn_free"] = [m]
            last[f"xT_ready{b}"] = G(f"xT_ready{b}") + [a, l]

        def project(src, w, col, ready):
            PJ, bank, freed = next_bank()
            for c in range(KC):
                for i, (ww, xx) in enumerate(split3(W[w], src)):
                    m = pe.do(lambda e, c=c, i=i, ww=ww, xx=xx: e.matmul(
                        PJ[:], ww[:, c, col:col + P], xx[:, c, :], start=(c == 0 and i == 0),
                        stop=(c == KC - 1 and i == 2)), after=ready + freed, counts=g["pj_pe"])
            return m, PJ, bank

        def project_split(n, which, src, w, bias):
            b, pr = divmod(n, PAIRS)
            at = {"q": "xT", "k": "cT"}[which]
            m, PJ, bank = project(src[b % 2], w, pr * P, G(f"{at}_ready{b}"))
            evacuated = []
            for j in range(2):
                own, other = slice(HD * j, HD * j + HD), slice(HD * (1 - j), HD * (1 - j) + HD)
                if which == "q":
                    hi, lo = qs[n % 2][j][own, :], qs[n % 2][j][other, :]
                else:
                    hi, lo = ks[n % 2][j][own, 0, :], ks[n % 2][j][own, 1, :]
                a = act.do(lambda e, own=own, hi=hi: e.activation(hi, PJ[own, :], ACT.Identity,
                                                                  bias=bias[own, pr:pr + 1]),
                           after=[m, bias_ready] + G(f"stack_free{n % 2}"), counts=g["part_hi"])
                evacuated.append(dve.do(lambda e, own=own, hi=hi, lo=lo: e.scalar_tensor_tensor(
                    lo, PJ[own, :], bias[own, pr:pr + 1], f32(hi), op0=ALU.add, op1=ALU.subtract),
                    after=[m, a] + G(f"stack_free{n % 2}"), counts=g["part_lo"]))
                if which == "k":
                    copied = sp.do(lambda e, own=own, other=other, j=j: e.dma_start(
                        f32(ks[n % 2][j][other, :, :]), f32(ks[n % 2][j][own, :, :])),
                        after=[evacuated[-1], a] + G(f"stack_free{n % 2}"), counts=stacked[n % 2])
            work_free[bank] = [evacuated[-1]]
            last[f"{at}_free{b % 2}"] = [m]
            last[f"{which}_ready{n}"] = [a, evacuated[-1]] + ([copied] if which == "k" else [])

        def project_q(n):
            project_split(n, "q", xT, "WqT", bqT)

        def project_k(n):
            project_split(n, "k", cT, "WkT", bkT)

        def project_v(n, t):
            b, half = divmod(n, 2)
            PJ, bank, freed = next_bank()
            for c in range(KC):
                for i, (xx, ww) in enumerate(split3(cT[b % 2], W["WvT"])):
                    m = pe.do(lambda e, c=c, i=i, ww=ww, xx=xx: e.matmul(
                        PJ[:], xx[:, c, t * P:(t + 1) * P], ww[:, c, half * 512:half * 512 + 512],
                        start=(c == 0 and i == 0), stop=(c == KC - 1 and i == 2)),
                        after=G(f"cT_ready{b}") + freed, counts=g["pj_pe"])
            v_ = dve.do(lambda e: e.tensor_tensor(v[n % 2][:, t, :], PJ[:], bv[:, half * 512:half * 512 + 512],
                                                  op=ALU.add),
                        after=[m, bias_ready] + G(f"v_free{n % 2}"), counts=g["v_ev"])
            work_free[bank] = [v_]
            last[f"cT_free{b % 2}"] = [m]
            last[f"v_ready{n}"] = [v_]

        def scores(hh):
            n, odd = divmod(hh, 2)
            for i, bank, at in SCORE_BANK:
                width = (i + 1) * P
                cols = max(width, MIN_COLS)
                for part in (1, 0):
                    pe.do(lambda e, bank=bank, i=i, at=at, cols=cols, part=part: e.matmul(
                        SB[bank][:, at:at + cols], qs[n % 2][odd][:, i * P:(i + 1) * P],
                        ks[n % 2][odd][:, part, 0:cols], start=(part == 1), stop=False),
                        after=G(f"q_ready{n}") + G(f"k_ready{n}") + free[f"S{bank}"])
                m = pe.do(lambda e, bank=bank, at=at, width=width: e.matmul(
                    SB[bank][:, at + width - P:at + width], identb[:], maskb[:], start=False, stop=True),
                    after=[tri_ready], counts=g["s_pe"])
                last[f"S{bank}"] = [m]
            last[f"stack_free{n % 2}"] = [m]

        def row_max(hh):
            for i, bank, at in SCORE_BANK:
                r = dve.do(lambda e, bank=bank, i=i, at=at: e.tensor_reduce(
                    nmax[hh % 2][:, i:i + 1], SB[bank][:, at:at + (i + 1) * P], AX.X, ALU.max, negate=True),
                    after=G(f"S{bank}") + G(f"nmax_free{hh % 2}"), counts=g["max"])
                last[f"max{bank}"] = [r]

        def exponent(hh):
            for i, bank, at in SCORE_BANK:
                width = (i + 1) * P
                a = act.do(lambda e, bank=bank, i=i, at=at, width=width: e.activation(
                    prob[hh % 2][:, SCORE_AT[i]:SCORE_AT[i] + width], SB[bank][:, at:at + width], ACT.Exp,
                    bias=nmax[hh % 2][:, i:i + 1], accum_out=sums[hh % 2][:, i:i + 1]),
                    after=G(f"S{bank}") + G(f"max{bank}") + G(f"prob_free{hh % 2}") + G(f"sums_free{hh % 2}"),
                    counts=g["exp"])
                free[f"S{bank}"] = [a]
            last[f"exp{hh}"] = [a]
            last[f"nmax_free{hh % 2}"] = [a]

        def normalise(hh):
            r = dve.do(lambda e: e.reciprocal(sums[hh % 2][:], sums[hh % 2][:]), after=G(f"exp{hh}"), counts=g["rcp"])
            for i in range(N_TILES):
                at, width = SCORE_AT[i], (i + 1) * P
                s = dve.do(lambda e, i=i, at=at, width=width: e.tensor_scalar(
                    prob[hh % 2][:, at:at + width], prob[hh % 2][:, at:at + width], sums[hh % 2][:, i:i + 1], None,
                    ALU.mult), after=[r], counts=g["norm"])
            last[f"norm{hh}"] = [s]
            last[f"sums_free{hh % 2}"] = [s]

        def transpose_probs(hh):
            W, bank, freed = next_bank()
            for k, (target, tiles) in enumerate(((TB[0], (0,)), (TB[1], (1, 3)), (W, (2,)))):
                for j in tiles:
                    for i in range(j, N_TILES):
                        at = PROB_T_AT[j] - BANK_COLS[k][0] + (i - j) * P
                        m = pe.do(lambda e, target=target, i=i, j=j, at=at: e.transpose(
                            target[:, at:at + P], prob[hh % 2][:, SCORE_AT[i] + j * P:SCORE_AT[i] + (j + 1) * P],
                            ident[:]), after=G(f"norm{hh}") + (freed if k == 2 else free[f"T{k}"]), counts=g["t_pe"])
                lo_, hi_ = BANK_COLS[k]
                if k == 2:
                    ev = dve.do(lambda e, target=target, lo_=lo_, hi_=hi_: e.tensor_copy(
                        probT[hh % 2][:, lo_:hi_], target[:, 0:hi_ - lo_]),
                        after=[m] + G(f"probT_free{hh % 2}"), counts=g["t_dve"])
                else:
                    ev = act.do(lambda e, target=target, lo_=lo_, hi_=hi_: e.activation(
                        probT[hh % 2][:, lo_:hi_], target[:, 0:hi_ - lo_], ACT.Copy),
                        after=[m] + G(f"probT_free{hh % 2}"), counts=g["t_act"])
                if k == 2:
                    work_free[bank] = [ev]
                else:
                    free[f"T{k}"] = [ev]
                last[f"probT{hh}"] = G(f"probT{hh}") + [ev]
            last[f"prob_free{hh % 2}"] = [m]

        def weigh_values(hh):
            b, h = divmod(hh, H)
            n, col = hh // 8, (h % 8) // 2 * P
            OB, bank, freed = next_bank()
            for j in range(N_TILES):
                m = pe.do(lambda e, j=j: e.matmul(
                    OB[:, j * P:512], v[n % 2][:, j, col:col + P],
                    probT[hh % 2][:, PROB_T_AT[j]:PROB_T_AT[j] + (N_TILES - j) * P],
                    start=(j == 0), stop=(j == N_TILES - 1)),
                    after=G(f"probT{hh}") + G(f"v_ready{n}") + freed, counts=g["pv_pe"])
            last[f"probT_free{hh % 2}"] = last[f"v_free{n % 2}"] = [m]
            return hh, m, OB, bank

        def keep_values(hh, m, OB, bank):
            b, h = divmod(hh, H)
            rows = slice(HD * (h % 2), HD * (h % 2) + HD)
            a = act.do(lambda e: e.activation(oT[rows, h // 2, :], OB[rows, :], ACT.Copy),
                       after=[m] + G("oT_free"), counts=g["o_ev"])
            work_free[bank] = [a]
            last[f"oT_ready{b}"] = [a]

        def output(b, u):
            PJ, bank, freed = next_bank()
            for t in (2 * u, 2 * u + 1):
                for pr in range(PAIRS):
                    m = pe.do(lambda e, t=t, pr=pr: e.matmul(
                        PJ[:, (t % 2) * D:(t % 2 + 1) * D], oT[:, pr, t * P:(t + 1) * P], WoT[:, pr, :],
                        start=(pr == 0), stop=(pr == PAIRS - 1)),
                        after=G(f"oT_ready{b}") + [bias_ready] + freed, counts=g["pj_pe"])
            o = dve.do(lambda e: e.tensor_tensor(x2[:, 2 * u:2 * u + 2, :], PJ[:].rearrange("p (a c) -> p a c", a=2),
                                                 x1[b % 2][:, 2 * u:2 * u + 2, :], op=ALU.add),
                       after=[m] + G(f"xb{b}") + G("x2_free"), counts=g["x2"])
            work_free[bank] = [o]
            last["oT_free"] = [m]
            last[f"x1_free{b % 2}"] = [o]
            last["x2_ready"] = [o]

        def find3(b):
            last["x2_stored"] = [sp.do(lambda e: e.dma_start(x2_dram[b], x2[:]), after=G("x2_ready"), counts=x2_out)]
            ln3.find(x2, G("x2_ready"))

        def norm3(b):
            last["xn3_ready"] = [ln3.apply(x2, xn3, G("xn3_free"))]
            last["x2_free"] = G("x2_stored") + G("xn3_ready")

        def transpose_x3(b, c):
            PJ, bank, freed = next_bank()
            for t in range(N_TILES):
                m = pe.do(lambda e, t=t: e.transpose(PJ[:, t * P:(t + 1) * P], xn3[:, t, c * P:(c + 1) * P], ident[:]),
                          after=G("xn3_ready") + freed, counts=g["pj_pe"])
            a = act.do(lambda e: e.activation(xn3T[:, c, :], PJ[:], ACT.Copy), after=[m] + G("xn3T_free") + G("xn_free"),
                       counts=g["xn3T"])
            work_free[bank] = [a]
            last["xn3T_ready"] = [a]

        bc = lambda ap: ap.rearrange("p (t a) -> p t a", a=1).broadcast_to([P, N_TILES, E])
        be = lambda ap: ap.rearrange("p (a e) -> p a e", a=1).broadcast_to([P, N_TILES, E])

        def route(b):
            PJ, bank, freed = next_bank()
            for t in range(N_TILES):
                for c in range(KC):
                    m = pe.do(lambda e, t=t, c=c: e.matmul(PJ[:, t * E:(t + 1) * E], xn3T[:, c, t * P:(t + 1) * P],
                                                           rw[:, c, :], start=(c == 0), stop=(c == KC - 1)),
                              after=G("xn3T_ready") + freed, counts=g["pj_pe"])
            last["xn3T_free"] = [m]
            R = lambda make, after: dve.do(make, after=after, counts=g["r_dve"])
            r = R(lambda e: e.tensor_tensor(lg[:], PJ[:, 0:N_TILES * E].rearrange("p (t e) -> p t e", t=N_TILES),
                                            be(rb[:]), op=ALU.add), [m, bias_ready])
            work_free[bank] = [r]
            r = R(lambda e: e.tensor_reduce(red[:], lg[:], AX.X, ALU.max), [r])
            r = R(lambda e: e.tensor_tensor(lg[:], lg[:], bc(red[:]), op=ALU.subtract), [r])
            last["logits_ready"] = [r]

        def choose(b):
            R = lambda make, after: dve.do(make, after=after, counts=g["r_dve"])
            bt = slice(b * N_TILES, (b + 1) * N_TILES)
            weight, chosen = routing["weight"], routing["chosen"]
            pr, r = probs[:, :, 0:E], G("logits_ready")[0]
            x = act.do(lambda e: e.activation(pr, lg[:], ACT.Exp), after=[r, consts] + G("probs_free"),
                       counts=g["r_act"])
            r = R(lambda e: e.tensor_reduce(red[:], pr, AX.X, ALU.add), [x, r])
            r = R(lambda e: e.reciprocal(red[:], red[:]), [r])
            r = R(lambda e: e.tensor_tensor(pr, pr, bc(red[:]), op=ALU.mult), [r])
            for t in range(N_TILES):
                r2 = R(lambda e, t=t: e.max(top8[:, t, :], probs[:, t, 0:E]), [r])
            r = R(lambda e: e.tensor_copy(top8[:, :, TOPK:8], sentinel[:]), [r2])
            for t in range(N_TILES):
                r2 = R(lambda e, t=t: e.match_replace(repl[:, t, :], top8[:, t, :], probs[:, t, :], -8.0), [r])
            r = R(lambda e: e.tensor_scalar(mask[:], repl[:, :, 0:E], -8.0, None, ALU.is_equal), [r2])
            mb = R(lambda e: e.tensor_copy(maskb16[:], mask[:]), [r])
            r = R(lambda e: e.tensor_tensor(pr, pr, mask[:], op=ALU.mult), [mb])
            r = R(lambda e: e.tensor_reduce(red[:], pr, AX.X, ALU.add), [r])
            r = R(lambda e: e.reciprocal(red[:], red[:]), [r])
            r = R(lambda e: e.tensor_tensor(weight[:, bt, :], pr, bc(red[:]), op=ALU.mult), [r])
            r = R(lambda e: e.tensor_copy(chosen[:, bt, :], mask[:]), [r])
            last["probs_free"] = [r]
            last["mask_ready"] = [r]

        def place(b):
            bt = slice(b * N_TILES, (b + 1) * N_TILES)
            pos = routing["pos"]
            PJ, bank, freed = next_bank()
            for t in range(N_TILES + 1):
                terms = [(tri, t)] if t < N_TILES else []
                terms += [(onesb, s_) for s_ in range(min(t, N_TILES))]
                for i, (w, s_) in enumerate(terms):
                    m = pe.do(lambda e, t=t, i=i, w=w, s_=s_, n=len(terms): e.matmul(
                        PJ[:, t * E:(t + 1) * E], w[:], maskb16[:, s_, :], start=(i == 0), stop=(i == n - 1)),
                        after=G("mask_ready") + [consts] + freed, counts=g["pj_pe"])
            R = lambda make, after: dve.do(make, after=after, counts=g["r_dve"])
            r = R(lambda e: e.tensor_tensor(pos[:, bt, :], PJ[:, 0:N_TILES * E].rearrange("p (t e) -> p t e", t=N_TILES),
                                            be(count[:]), op=ALU.add), [m, consts] + G("count_ready"))
            c = R(lambda e: e.tensor_tensor(count[:], PJ[:, N_TILES * E:(N_TILES + 1) * E], count[:], op=ALU.add), [r])
            last["count_ready"] = [c]
            work_free[bank] = [c]
            r = R(lambda e: e.tensor_tensor(key[:], pos[:, bt, :], be(ebase[:]), op=ALU.add), [r])
            r = R(lambda e: e.tensor_tensor(key[:], key[:], mask[:], op=ALU.mult), [r])
            for t in range(N_TILES):
                r2 = R(lambda e, t=t: e.max(key8[:, t, :], key[:, t, :]), [r])
            w = dve.do(lambda e: e.tensor_scalar(rows_i[b % 2][:], key8[:, :, 0:TOPK], -1.0, None, ALU.add),
                       after=[r2] + G(f"rows_free{b % 2}"), counts=g["r_rows"])
            for t in range(N_TILES):
                for k in range(TOPK):
                    s = pool.do(lambda e, t=t, k=k: e.indirect_dma_start(
                        rows_dram, bass.IndirectOffsetOnAxis(rows_i[b % 2][:, t, k:k + 1], 0), xn3[:, t, :], None),
                        after=[w] + G("xn3_ready"), counts=scattered)
            last["xn3_free"] = last[f"rows_free{b % 2}"] = [s]

        def load_w1():
            projecting.close()
            resident("w1", sp, G(f"xT_free{(B - 1) % 2}"))

        def load_w2():
            heads.close()
            resident("w2", sp, G(f"probT_free{(B * H - 1) % 2}"))

        def make_tables():
            R = lambda make, after: dve.do(make, after=after, counts=g["r_dve"])
            scr = p.sb("scr", [P, 5, E])
            scr_i, pad_i = p.sb("scr_i", [P, E], I32), p.sb("pad_i", [1, E], I32)
            tiles, cum, base, one, hit = (scr[:, i, :] for i in range(5))
            of_tile = p.sb("of_tile", [P, 4])
            owner, before, row, some = (of_tile[:, i:i + 1] for i in range(4))
            zeros = ctx32[:].rearrange("p a b -> p (a b)")[:, 0:RT * D]
            z = R(lambda e: e.memset(zeros, 0.0), G("ctx32_free"))
            pad_ready = R(lambda e: e.tensor_tensor(pad_i[:], count[0:1, :], region[:], op=ALU.add),
                          G("count_ready") + [consts])
            for e_ in range(E):
                def pad(e, e_=e_):
                    at = e.value_load(pad_i[0:1, e_:e_ + 1], min_val=0, max_val=E * REGION - ROWS)
                    return e.dma_start(rows_dram[bass.ds(at, ROWS), :].rearrange("(p a) c -> p (a c)", p=P), zeros)
                last["pads"] = [sp.do(pad, after=[z, pad_ready], counts=padded)]
            r = R(lambda e: e.memset(one, 1.0), [])
            r = R(lambda e: e.tensor_scalar(scr_i[:], count[:], float(ROWS - 1), None, ALU.add), [r])
            r = R(lambda e: e.tensor_scalar(scr_i[:], scr_i[:], ROWS.bit_length() - 1, None, ALU.arith_shift_right),
                  [r])
            r = R(lambda e: e.tensor_copy(tiles, scr_i[:]), [r])
            r = R(lambda e: e.tensor_tensor_scan(cum, one, tiles, 0.0, ALU.mult, ALU.add), [r])
            r = R(lambda e: e.tensor_tensor(base, cum, tiles, op=ALU.subtract), [r])
            r = R(lambda e: e.tensor_scalar(base, base, float(ROWS), 1.0, ALU.mult, ALU.add), [r])
            r = R(lambda e: e.tensor_scalar(hit, cum, number[:, 0:1], None, ALU.is_le), [r])
            r = R(lambda e: e.tensor_reduce(owner, hit, AX.X, ALU.add), [r])
            r = R(lambda e: e.tensor_tensor(hit, hit, tiles, op=ALU.mult), [r])
            r = R(lambda e: e.tensor_reduce(before, hit, AX.X, ALU.add), [r])
            r = R(lambda e: e.tensor_scalar(some, owner, float(E), None, ALU.is_lt), [r])
            r = R(lambda e: e.tensor_tensor(owner, owner, some, op=ALU.mult), [r])
            r = R(lambda e: e.tensor_tensor(row, number[:], before, op=ALU.subtract), [r])
            r = R(lambda e: e.tensor_scalar(row, row, float(ROWS), None, ALU.mult), [r])
            r = R(lambda e: e.scalar_tensor_tensor(row, owner, float(REGION), row, op0=ALU.mult, op1=ALU.add), [r])
            r = R(lambda e: e.tensor_tensor(row, row, some, op=ALU.mult), [r])
            W_, bank, freed = next_bank()
            for i, column in enumerate((owner, row)):
                m = pe.do(lambda e, i=i, column=column: e.transpose(W_[0:1, i * P:(i + 1) * P], column, ident[:]),
                          after=[r] + freed, counts=g["pj_pe"])
            r = R(lambda e: e.tensor_copy(routing["owner"][:], W_[0:1, 0:MOE_TILES]), [m])
            r = R(lambda e: e.tensor_copy(routing["first_row"][:], W_[0:1, P:P + MOE_TILES]), [r])
            work_free[bank] = [r]
            pos, chosen, weight = routing["pos"], routing["chosen"], routing["weight"]
            slots, slot_weight = routing["slots"], routing["slot_weight"]
            spare = [x[:].rearrange("p t c -> p (t c)") for x in x1]
            key_, eq = (spare[0][:, i * ALL_TILES * E:(i + 1) * ALL_TILES * E].rearrange("p (t e) -> p t e", e=E)
                        for i in range(2))
            top = spare[1][:, 0:ALL_TILES * 8].rearrange("p (t k) -> p t k", k=8)
            r = R(lambda e: e.tensor_tensor(key_, pos[:], base.rearrange("p (a e) -> p a e", a=1)
                                            .broadcast_to([P, ALL_TILES, E]), op=ALU.add),
                  [r] + G("x1_free0") + G("x1_free1"))
            r = R(lambda e: e.tensor_tensor(key_, key_, chosen[:], op=ALU.mult), [r])
            for t in range(ALL_TILES):
                r2 = R(lambda e, t=t: e.max(top[:, t, :], key_[:, t, :]), [r])
            for k in range(TOPK):
                r = R(lambda e, k=k: e.tensor_tensor(eq, key_, top[:, :, k:k + 1].broadcast_to([P, ALL_TILES, E]),
                                                     op=ALU.is_equal), [r2, r])
                r = R(lambda e: e.tensor_tensor(eq, eq, weight[:], op=ALU.mult), [r])
                r = R(lambda e, k=k: e.tensor_reduce(slot_weight[:, :, k], eq, AX.X, ALU.add), [r])
            R(lambda e: e.tensor_scalar(slots[:], top[:, :, 0:TOPK], -1.0, None, ALU.add), [r])

        def tasks(b, h):
            pair, done, coming = b * PAIRS + h // 2 + 1, b - 1, b + 1
            halves = (2 * b + 1, 2 * b + 2)
            plan = {}
            add = lambda at, place_, task, *args: plan.setdefault((at, place_), []).append(lambda: task(*args))
            if pair < B * PAIRS and h % 2 == 0:
                add(h, 0, project_k, pair)
                add(h, 1, project_q, pair)
            for (at, place_), (half, t) in V_TILE_AT.items():
                if halves[half] < 2 * B:
                    add(at, place_, project_v, halves[half], t)
            if done >= 0:
                add(1, 1, output, done, 0)
                add(2, 1, output, done, 1)
                add(3, 0, find3, done)
                add(4, 0, norm3, done)
                add(6, 1, transpose_x3, done, 0)
                add(7, 0, transpose_x3, done, 1)
                add(9, 0, route, done)
                add(10, 0, choose, done)
                add(11, 0, place, done)
            if coming == B:
                add(13, 1, load_w1)
            if coming < B:
                add(4, 1, load, coming)
                add(6, 1, split_ctx, coming)
                add(7, 1, find2, coming)
                add(10, 1, norm2, coming)
                add(11, 1, transpose_x, coming, 0)
                add(13, 0, transpose_x, coming, 1)
            return plan.get((h, 0), []), plan.get((h, 1), [])

        load(0)
        split_ctx(0)
        find2(0)
        bias_ready = dve.do(lambda e: e.tensor_scalar(bqT[:], bqT[:], HD ** -0.5, None, ALU.mult),
                            after=[bias_in_all], counts=p.counter("bias"))
        norm2(0)
        project_k(0)
        for t in range(N_TILES):
            project_v(0, t)
        transpose_x(0, 0)
        transpose_x(0, 1)
        project_q(0)
        for hh in range(B * H + 2):
            first, second = tasks(*divmod(hh, H)) if hh < B * H else ([], [])
            if hh < B * H:
                scores(hh)
                row_max(hh)
                exponent(hh)
            if 0 <= hh - 1 < B * H:
                transpose_probs(hh - 1)
            if hh < B * H:
                normalise(hh)
            for f in first:
                f()
            if hh - 2 >= 0:
                weighed = weigh_values(hh - 2)
                second.insert(len(second) if hh % H == 2 else 0, lambda weighed=weighed: keep_values(*weighed))
            for f in second:
                f()
        load_w2()
        output(B - 1, 0)
        output(B - 1, 1)
        find3(B - 1)
        norm3(B - 1)
        transpose_x3(B - 1, 0)
        transpose_x3(B - 1, 1)
        route(B - 1)
        choose(B - 1)
        place(B - 1)
        make_tables()
        sp.do(lambda e: e.nop(), after=G("x2_free") + G("pads"))
        pool.do(lambda e: e.nop(), after=G("xn3_free"))
        p.run()


WE = KC * FF


def resident_weights(nc, stack, d):
    held = {}

    def load(name, queue, after):
        tile = stack.enter_context(nc.sbuf_tensor("experts_" + name, [P, E * WE], F32, side="right"))
        loaded = Counter(stack.enter_context(nc.semaphore(name + "_loaded")), 16)
        for e_ in range(E):
            weights = d[name][e_].rearrange("(k p) n -> p k n", p=P)
            ready = queue.do(lambda e, e_=e_, weights=weights: e.dma_start(
                tile[:, e_ * WE:(e_ + 1) * WE].rearrange("p (k n) -> p k n", n=weights.shape[2]), weights),
                after=after, counts=loaded)
        held[name] = (tile, ready)
    return held, load


def experts(nc, d, rows_dram, y_dram, routing, held):
    with ExitStack() as stack:
        p = Part(nc, stack, "ex")
        pe, act, dve, pool, sp = p.pe, p.act, p.dve, p.pool, p.sp
        ident, const_ready, _ = constants(p)
        NX = 3
        (W1, w1_loaded), (W2, w2_loaded) = held["w1"], held["w2"]
        b1T = p.sb("b1T", [P, E * FC])
        x_in = [p.sb(f"x{i}", [P, RT, D]) for i in range(NX)]
        xT = [tuple(p.sb(f"xT{i}{j}", [P, KC, ROWS], F32R) for j in range(2)) for i in range(2)]
        w1 = [tuple(p.sb(f"w1_{i}{j}", [P, KC, FF], F32R) for j in range(2)) for i in range(2)]
        w2 = [tuple(p.sb(f"w2_{i}{j}", [P, FC, D], F32R) for j in range(2)) for i in range(2)]
        b1 = [p.sb(f"b1_{i}", [P, FC]) for i in range(2)]
        h32 = p.sb("h32", [P, FC, ROWS])
        hT = [tuple(p.sb(f"hT{i}{j}", [P, FC, ROWS], F32R) for j in range(2)) for i in range(2)]
        y = [p.sb(f"y{i}", [P, RT, D]) for i in range(2)]
        XB = [p.bank(f"X{i}") for i in range(2)]
        HB = [p.bank(f"H{i}") for i in range(4)]
        YB = [p.bank(f"Y{i}") for i in range(2)]

        b1_in = p.dma_counter("b1_in")
        b1_ready = sp.do(lambda e: e.dma_start(b1T[:], d['b1T']), counts=b1_in)

        owner_i, row_i = routing["owner"], routing["first_row"]

        g = {n: p.counter(n) for n in ("t_pe", "x_hi", "x_lo", "w1_hi", "w1_lo", "w2_hi", "w2_lo", "b1c", "h_pe",
                                      "gelu", "h_hi", "h_lo", "y_pe", "y_ev")}
        x_loaded = [p.dma_counter(f"x_loaded{i}") for i in range(NX)]
        y_stored = [p.dma_counter(f"y_stored{i}") for i in range(2)]
        last = {}
        G = lambda k: last.get(k, [])

        def load_rows(j):
            def load(e):
                at = e.value_load(row_i[0:1, j:j + 1], min_val=0, max_val=E * REGION - ROWS)
                return e.dma_start(x_in[j % NX][:], rows_dram[bass.ds(at, ROWS), :].rearrange("(a p) c -> p a c", p=P))
            last[f"x{j}"] = [sp.do(load, after=G(f"x_free{j % NX}"), counts=x_loaded[j % NX])]

        def owner_of(e, j):
            return e.value_load(owner_i[0:1, j:j + 1], min_val=0, max_val=E - 1)

        flat = lambda t: t[:].rearrange("p a b -> p (a b)")

        def split_w1(j):
            h1, l1 = w1[j % 2]
            regs = {}

            def w1_hi(e):
                regs["dve"] = owner_of(e, j)
                return e.tensor_copy(flat(h1), W1[:, bass.ds(regs["dve"] * WE, WE)])

            def w1_lo(e):
                at = owner_of(e, j)
                return e.tensor_tensor(flat(l1), W1[:, bass.ds(at * WE, WE)], f32(flat(h1)), op=ALU.subtract)
            wait = [w1_loaded, b1_ready]
            a = dve.do(w1_hi, after=wait + G(f"w1_free{j % 2}"), counts=g["w1_hi"])
            b = pool.do(w1_lo, after=wait + [a] + G(f"w1_free{j % 2}"), counts=g["w1_lo"])
            c = dve.do(lambda e: e.tensor_copy(b1[j % 2][:], b1T[:, bass.ds(regs["dve"] * FC, FC)]),
                       after=G(f"b1_free{j % 2}"), counts=g["b1c"])
            last[f"w1_{j}"] = [a, b]
            last[f"b1_{j}"] = [c]

        def split_w2(j):
            h2, l2 = w2[j % 2]
            regs = {}

            def w2_hi(e):
                regs["dve"] = owner_of(e, j)
                return e.tensor_copy(flat(h2), W2[:, bass.ds(regs["dve"] * WE, WE)])
            d_ = dve.do(w2_hi, after=[w2_loaded] + G(f"w2_free{j % 2}"), counts=g["w2_hi"])
            e_ = dve.do(lambda e: e.tensor_tensor(flat(l2), W2[:, bass.ds(regs["dve"] * WE, WE)], f32(flat(h2)),
                                                  op=ALU.subtract), after=[d_] + G(f"w2_free{j % 2}"),
                        counts=g["w2_lo"])
            last[f"w2_{j}"] = [d_, e_]

        def transpose_rows(j):
            bank = XB[j % 2]
            for c in range(KC):
                for a in range(RT):
                    m = pe.do(lambda e, c=c, a=a: e.transpose(bank[:, c * ROWS + a * P:c * ROWS + (a + 1) * P],
                                                              x_in[j % NX][:, a, c * P:(c + 1) * P], ident[:]),
                              after=G(f"x{j}") + G(f"X_free{j % 2}") + [const_ready], counts=g["t_pe"])
            last[f"x_free{j % NX}"] = [m]
            hi, lo = xT[j % 2]
            view = bank[:].rearrange("p (c s) -> p c s", c=KC)
            a = act.do(lambda e: e.activation(hi[:], view, ACT.Copy), after=[m] + G(f"xT_free{j % 2}"),
                       counts=g["x_hi"])
            l = dve.do(lambda e: e.tensor_tensor(lo[:], view, f32(hi[:]), op=ALU.subtract),
                       after=[m, a] + G(f"xT_free{j % 2}"), counts=g["x_lo"])
            last[f"X_free{j % 2}"] = [l]
            last[f"xT{j}"] = [a, l]

        def hidden(j):
            hh, hl = hT[j % 2]
            for u in range(FC // 2):
                bank = HB[2 * (j % 2) + u]
                for f in (2 * u, 2 * u + 1):
                    terms = [(w, x, c) for c in range(KC) for w, x in split3(w1[j % 2], xT[j % 2])]
                    for i, (w, x, c) in enumerate(terms):
                        m = pe.do(lambda e, f=f, i=i, w=w, x=x, c=c, bank=bank, n=len(terms): e.matmul(
                            bank[:, (f % 2) * ROWS:(f % 2 + 1) * ROWS], w[:, c, f * P:(f + 1) * P], x[:, c, :],
                            start=(i == 0), stop=(i == n - 1)),
                            after=G(f"w1_{j}") + G(f"xT{j}") + G(f"H_free{2 * (j % 2) + u}"), counts=g["h_pe"])
                for f in (2 * u, 2 * u + 1):
                    a = act.do(lambda e, f=f, bank=bank: e.activation(
                        h32[:, f, :], bank[:, (f % 2) * ROWS:(f % 2 + 1) * ROWS], ACT.Gelu, bias=b1[j % 2][:, f:f + 1]),
                        after=[m] + G(f"b1_{j}") + G(f"h32_free{u}"), counts=g["gelu"])
                last[f"H_free{2 * (j % 2) + u}"] = [a]
                fs = slice(2 * u, 2 * u + 2)
                hi = act.do(lambda e, fs=fs: e.activation(hh[:, fs, :], h32[:, fs, :], ACT.Copy),
                            after=[a] + G(f"hT_free{j % 2}"), counts=g["h_hi"])
                lo = dve.do(lambda e, fs=fs: e.tensor_tensor(hl[:, fs, :], h32[:, fs, :], f32(hh[:, fs, :]),
                                                             op=ALU.subtract),
                            after=[a, hi] + G(f"hT_free{j % 2}"), counts=g["h_lo"])
                last[f"h32_free{u}"] = [lo]
                last[f"h{j}_{u}"] = [hi, lo]
            last[f"w1_free{j % 2}"] = last[f"xT_free{j % 2}"] = [m]
            last[f"b1_free{j % 2}"] = [a]

        def results(j):
            bank = YB[j % 2]
            for a in range(RT):
                terms = [(h, w, f) for f in range(FC) for h, w in split3(hT[j % 2], w2[j % 2])]
                for i, (h, w, f) in enumerate(terms):
                    m = pe.do(lambda e, a=a, i=i, h=h, w=w, f=f, n=len(terms): e.matmul(
                        bank[:, a * D:(a + 1) * D], h[:, f, a * P:(a + 1) * P], w[:, f, :],
                        start=(i == 0), stop=(i == n - 1)),
                        after=G(f"w2_{j}") + G(f"h{j}_{f // 2}") + G(f"Y_free{j % 2}"), counts=g["y_pe"])
            last[f"w2_free{j % 2}"] = last[f"hT_free{j % 2}"] = [m]
            o = act.do(lambda e: e.activation(y[j % 2][:], bank[:].rearrange("p (a c) -> p a c", a=RT), ACT.Copy),
                       after=[m] + G(f"y_free{j % 2}"), counts=g["y_ev"])
            last[f"Y_free{j % 2}"] = [o]
            last[f"y_free{j % 2}"] = [sp.do(lambda e: e.dma_start(
                y_dram[j * ROWS:(j + 1) * ROWS, :].rearrange("(a p) c -> p a c", p=P), y[j % 2][:]),
                after=[o], counts=y_stored[j % 2])]

        for j in range(NX):
            load_rows(j)
        split_w1(0)
        split_w1(1)
        split_w2(0)
        transpose_rows(0)
        for j in range(MOE_TILES + 1):
            if j + NX < MOE_TILES:
                load_rows(j + NX)
            if j + 1 < MOE_TILES:
                transpose_rows(j + 1)
            if j < MOE_TILES:
                hidden(j)
            if j + 2 < MOE_TILES:
                split_w1(j + 2)
            if j >= 1:
                results(j - 1)
            if j + 1 < MOE_TILES:
                split_w2(j + 1)
        sp.do(lambda e: e.nop(), after=G("y_free0") + G("y_free1"))
        p.run()


def combine(nc, d, x2_dram, y_dram, out, routing):
    with ExitStack() as stack:
        p = Part(nc, stack, "co")
        pe, act, dve, pool, sp = p.pe, p.act, p.dve, p.pool, p.sp
        ident, const_ready, _ = constants(p)
        slots, slot_weight, weight = routing["slots"], routing["slot_weight"], routing["weight"]
        NB = 6
        b2 = p.sb("b2", [E, D])
        wT = p.sb("wT", [E, TOKENS])
        got = [p.sb(f"got{i}", [P, TOPK, D]) for i in range(NB)]
        x2 = [p.sb(f"x2_{i}", [P, N_TILES, D]) for i in range(2)]
        o = [p.sb(f"o{i}", [P, N_TILES, D]) for i in range(2)]
        TB = [p.bank(f"T{i}") for i in range(2)]
        BB = [p.bank(f"B{i}") for i in range(2)]
        b2_in = p.dma_counter("b2_in")
        b2_ready = sp.do(lambda e: e.dma_start(b2[:], d['b2']), counts=b2_in)
        gathered = [p.dma_counter(f"gathered{i}") for i in range(NB)]
        x2_in = [p.dma_counter(f"x2_in{i}") for i in range(2)]
        stored = [p.dma_counter(f"stored{i}") for i in range(2)]
        g = {n: p.counter(n) for n in ("wT_pe", "wT_ev", "b_pe", "sum")}
        last = {}
        G = lambda k: last.get(k, [])

        def gather(tt):
            for k in range(TOPK):
                last[f"g{tt}"] = [pool.do(lambda e, k=k: e.indirect_dma_start(
                    got[tt % NB][:, k, :], None, y_dram, bass.IndirectOffsetOnAxis(slots[:, tt, k:k + 1], 0)),
                    after=G(f"got_free{tt % NB}"), counts=gathered[tt % NB])]

        for b in range(B):
            x2_ready = sp.do(lambda e, b=b: e.dma_start(x2[b % 2][:], x2_dram[b]), after=G(f"x2_free{b % 2}"),
                             counts=x2_in[b % 2])
            for t in range(N_TILES):
                m = pe.do(lambda e, b=b, t=t: e.transpose(TB[b % 2][0:E, t * P:(t + 1) * P],
                                                          weight[:, b * N_TILES + t, :], ident[:]),
                          after=[const_ready] + G(f"T_free{b % 2}"), counts=g["wT_pe"])
            w = act.do(lambda e, b=b: e.activation(wT[:, b * S:(b + 1) * S], TB[b % 2][0:E, :], ACT.Copy), after=[m],
                       counts=g["wT_ev"])
            last[f"T_free{b % 2}"] = [w]
            for t in range(N_TILES):
                tt = b * N_TILES + t
                gather(tt)
                m = pe.do(lambda e, tt=tt: e.matmul(BB[tt % 2][:, 0:D], wT[:, tt * P:(tt + 1) * P], b2[:],
                                                    start=True, stop=True),
                          after=[w, b2_ready] + G(f"B_free{tt % 2}"), counts=g["b_pe"])
                acc = o[b % 2][:, t, :]
                s = dve.do(lambda e, b=b, t=t, tt=tt, acc=acc: e.tensor_tensor(acc, BB[tt % 2][:, 0:D],
                                                                              x2[b % 2][:, t, :], op=ALU.add),
                           after=[m, x2_ready] + G(f"o_free{b % 2}"), counts=g["sum"])
                last[f"B_free{tt % 2}"] = [s]
                for k in range(TOPK):
                    s = dve.do(lambda e, tt=tt, k=k, acc=acc: e.scalar_tensor_tensor(
                        acc, got[tt % NB][:, k, :], slot_weight[:, tt, k:k + 1], acc, op0=ALU.mult, op1=ALU.add),
                        after=[s] + G(f"g{tt}"), counts=g["sum"])
                last[f"got_free{tt % NB}"] = [s]
            last[f"x2_free{b % 2}"] = [s]
            last[f"o_free{b % 2}"] = [sp.do(lambda e, b=b: e.dma_start(
                out[b].rearrange("(t p) c -> p t c", p=P), o[b % 2][:]), after=[s], counts=stored[b % 2])]
        sp.do(lambda e: e.nop(), after=G("o_free0") + G("o_free1"))
        p.run()


def decoder_layer(nc, d, out):
    with ExitStack() as stack:
        scratch = lambda n, shape: nc.dram_tensor(n, shape, F32, kind="Internal").ap()
        x1_dram = scratch("x1_rows", [B, P, N_TILES, D])
        x2_dram = scratch("x2_rows", [B, P, N_TILES, D])
        rows_dram = scratch("expert_rows", [E * REGION, D])
        y_dram = scratch("expert_results", [MOE_TILES * ROWS, D])
        projecting = ExitStack()
        W = {name: tuple(projecting.enter_context(nc.sbuf_tensor(f"{name}_{part}", [P, KC, INNER], F32R, side="right"))
                         for part in ("hi", "lo")) for name in ("WkT", "WqT", "WvT")}
        first_attention(nc, d, x1_dram, W)
        sb = lambda n, shape, dt=F32: stack.enter_context(nc.sbuf_tensor("routing_" + n, shape, dt))
        routing = {n: sb(n, [P, ALL_TILES, E]) for n in ("weight", "pos", "chosen")}
        routing["count"] = sb("count", [P, E])
        routing["owner"] = stack.enter_context(nc.sbuf_tensor("routing_owner", [1, MOE_TILES], I32))
        routing["first_row"] = stack.enter_context(nc.sbuf_tensor("routing_first_row", [1, MOE_TILES], I32))
        routing["slots"] = sb("slots", [P, ALL_TILES, TOPK], I32)
        routing["slot_weight"] = sb("slot_weight", [P, ALL_TILES, TOPK])
        held, load = resident_weights(nc, stack, d)
        cross_attention(nc, d, x1_dram, x2_dram, rows_dram, routing, W, projecting, load)
        experts(nc, d, rows_dram, y_dram, routing, held)
        combine(nc, d, x2_dram, y_dram, out, routing)


def kernel(**inputs):
    import concourse.bacc as bacc
    from concourse.bass_utils import run_bass_kernel_spmd

    take = lambda name: np.asarray(inputs[name])
    own = {n: take(f"L0_attn_{n}") for n in ("Wqkv", "bqkv", "Wln", "bln")}
    own |= {n: take(f"L0_xattn_{n}") for n in ("bq", "bk", "bv", "bo")}
    own |= {n + "T": take(f"L0_xattn_{n}").T for n in ("Wq", "Wk", "Wv", "Wo")}
    own |= {n: take(f"L0_ffn_{n}") for n in ("router_w", "router_b", "w1", "w2", "b2")}
    own["b1T"] = take("L0_ffn_b1").reshape(E, FC, P).transpose(2, 0, 1).reshape(P, E * FC)
    own["x"] = take("x")
    own["ctxT"] = take("ctx_1024").transpose(0, 2, 1)

    nc = bacc.Bacc("TRN2", target_bir_lowering=False, num_devices=1)
    arrays, d = {}, {}
    for name, a in own.items():
        arrays["in_" + name] = np.ascontiguousarray(a)
        d[name] = nc.dram_tensor("in_" + name, a.shape, F32, kind="ExternalInput").ap()
    out = nc.dram_tensor("out", (B, S, D), F32, kind="ExternalOutput").ap()
    decoder_layer(nc, d, out)
    result = run_bass_kernel_spmd(nc, [arrays], core_ids=[0])
    return result.results[0]["out"]
```
